# Optimizing a Trainium2 kernel written in Bass

```python
import numpy as np
import jax
import jax.numpy as jnp

def _softmax(x, axis=-1):
    return jax.nn.softmax(x, axis=axis)

def _gelu(x):
    return jax.nn.gelu(x, approximate=True)

def _silu(x):
    return jax.nn.silu(x)

def _sigmoid(x):
    return jax.nn.sigmoid(x)

def _layernorm(x, axis=-1, eps=1e-05):
    m = jnp.mean(x, axis=axis, keepdims=True)
    v = jnp.var(x, axis=axis, keepdims=True)
    return (x - m) / jnp.sqrt(v + eps)

def _scatter_add(tgt, idx, src, axis=0):
    return tgt.at[idx].add(src)

def _segment_sum(src, seg, n):
    return jax.ops.segment_sum(src, seg, n)
kernel_name = 'mk_adaln_attn_ffn_d1_seqx_r4_fe894f'

def setup_inputs(seed: int=0):
    np.random.seed(seed)
    _w = jnp.asarray

    def _rec_inputs():
        import jax
        import jax.numpy as jnp
        _rk = jax.random.key(seed)
        x = 7.22e-05 + 1 * jax.random.normal(jax.random.fold_in(_rk, 1), (2, 1024, 256), jnp.float32)
        _lenS = 1024 - jax.random.randint(jax.random.fold_in(_rk, 7), (2,), 0, max(1, 1024 // 4) + 1, jnp.int32)
        _lenS2 = 1024 - jax.random.randint(jax.random.fold_in(_rk, 8), (2,), 0, max(1, 1024 // 4) + 1, jnp.int32)
        condB_tauraws = -5.74692 + 0.777674 * jax.random.normal(jax.random.fold_in(_rk, 11), (2,), jnp.float32)
        cond_256 = -0.000235209 + 0.019331 * jax.random.normal(jax.random.fold_in(_rk, 12), (2, 64), jnp.float32)
        condB_bn2 = jnp.zeros((2,), jnp.float32)
        cond_1024 = -4.10585e-05 + 0.0199478 * jax.random.normal(jax.random.fold_in(_rk, 14), (2, 256), jnp.float32)
        itok_B_0_6 = jax.random.randint(jax.random.fold_in(_rk, 15), (2,), 0, 7, jnp.int32)
        return (x, condB_tauraws, cond_256, condB_bn2, cond_1024, itok_B_0_6)
    x, condB_tauraws, cond_256, condB_bn2, cond_1024, itok_B_0_6 = _rec_inputs()

    def _L0_cond_setup():
        import jax, jax.numpy as jnp
        import numpy as np
        import math
        B, T, E, D = (4, 512, 256, 4)

        def _tau_init(t):
            a = 0.1 ** (1.0 / max(t - 1, 1))
            tt = -math.log(max(a, 1e-10))
            return math.log(math.exp(tt) - 1 + 1e-10)

        def causal_ema(b, tau_raw):
            alpha = jnp.exp(-jax.nn.softplus(tau_raw)).astype(b.dtype)

            def step(h, bt):
                h = alpha * h + bt
                return (h, h)
            h0 = jnp.zeros((b.shape[0], b.shape[2]), b.dtype)
            _, hs = jax.lax.scan(step, h0, jnp.swapaxes(b, 0, 1))
            return jnp.swapaxes(hs, 0, 1)
        key = jax.random.key(seed)
        ks = jax.random.split(key, 10)
        s = 0.02
        return {'x': jax.random.normal(ks[0], (B, T, E), jnp.float32), 'tau_ctx': jnp.float32(_tau_init(max(T // 2, 4))), 'tau_raws': jnp.array([_tau_init(max(T // 2 ** i, 2)) for i in range(D)], jnp.float32), 'Wg': jax.random.normal(ks[1], (E, 2 * E), jnp.float32) * s, 'bg': jnp.full((E,), -0.5, jnp.float32), 'Wn1': jax.random.normal(ks[2], (E // 4, E), jnp.float32) * s, 'bn1': jnp.zeros((E // 4,), jnp.float32), 'Wn2': jax.random.normal(ks[3], (D, E // 4), jnp.float32) * s, 'bn2': jnp.zeros((D,), jnp.float32), 'blend': jax.random.normal(ks[4], (D, E), jnp.float32) * s, 'Wsoma': jax.random.normal(ks[5], (E, E), jnp.float32) * s, 'bsoma': jnp.zeros((E,), jnp.float32), 'Wtemp': jax.random.normal(ks[6], (E, E), jnp.float32) * s, 'btemp': jnp.zeros((E,), jnp.float32), 'Wout': jax.random.normal(ks[7], (E, E), jnp.float32) * s, 'gamma': jnp.ones((E,), jnp.float32), 'beta': jnp.zeros((E,), jnp.float32)}
    _L0_cond_all = _L0_cond_setup()
    _L0_cond_in = {k: v for k, v in _L0_cond_all.items() if k in ('tau_ctx', 'Wg', 'bg', 'Wn1', 'bn1', 'Wsoma', 'bsoma', 'Wtemp', 'btemp', 'Wout', 'gamma', 'beta')}
    del _L0_cond_all

    def _L0_attn_setup():
        import jax, jax.numpy as jnp
        import numpy as np
        B, T, C = (2, 512, 256)
        DIM, H = (256, 16)
        HD = DIM // H
        key = jax.random.key(seed)
        ks = jax.random.split(key, 6)
        s_in = 1.0 / np.sqrt(C)
        s_proj = 1.0 / np.sqrt(DIM)
        return {'x': jax.random.normal(ks[0], (B, T, C), dtype=jnp.float32), 'Wqkv': jax.random.normal(ks[1], (C, 3 * DIM), dtype=jnp.float32) * s_in, 'bqkv': jnp.zeros((3 * DIM,), dtype=jnp.float32), 'r_sigma': jnp.float32(0.1), 'Wproj': jax.random.normal(ks[2], (DIM, C), dtype=jnp.float32) * s_proj, 'bproj': jnp.zeros((C,), dtype=jnp.float32)}
    _L0_attn_all = _L0_attn_setup()
    _L0_attn_in = {k: v for k, v in _L0_attn_all.items() if k in ('Wqkv', 'bqkv', 'r_sigma', 'Wproj', 'bproj')}
    del _L0_attn_all

    def _L0_cond2_setup():
        import jax, jax.numpy as jnp
        import numpy as np
        N_PROFILES = 8
        HIDDEN = 256
        BOTTLENECK = 128
        EPS = 1e-05
        key = jax.random.key(seed)
        ks = jax.random.split(key, 8)
        B, S, H, K, P = (16, 512, HIDDEN, BOTTLENECK, N_PROFILES)
        down_w = jax.random.normal(ks[0], (P, H, K), dtype=jnp.float32) * (1.0 / np.sqrt(H))
        down_b = jax.random.normal(ks[1], (P, K), dtype=jnp.float32) * 0.01
        up_w = jax.random.normal(ks[2], (P, K, H), dtype=jnp.float32) * (1.0 / np.sqrt(K))
        up_b = jax.random.normal(ks[3], (P, H), dtype=jnp.float32) * 0.01
        ln_g = jnp.ones((P, H), dtype=jnp.float32)
        ln_b = jnp.zeros((P, H), dtype=jnp.float32)
        hidden = jax.random.normal(ks[4], (B, S, H), dtype=jnp.float32)
        profile_ids = jax.random.randint(ks[5], (B,), 0, P)
        return {'hidden': hidden, 'profile_ids': profile_ids, 'down_w': down_w, 'down_b': down_b, 'up_w': up_w, 'up_b': up_b, 'ln_g': ln_g, 'ln_b': ln_b}
    _L0_cond2_all = _L0_cond2_setup()
    _L0_cond2_in = {k: v for k, v in _L0_cond2_all.items() if k in ('down_w', 'down_b', 'up_w', 'up_b', 'ln_g', 'ln_b')}
    del _L0_cond2_all

    def _L0_ffn_setup():
        import jax, jax.numpy as jnp
        import numpy as np
        TOP_K = 2
        CAPACITY_FACTOR = 1.0
        key = jax.random.key(seed)
        ks = jax.random.split(key, 4)
        sl, bs, hs, ffn, E = (512, 8, 256, 1024, 8)
        x = jax.random.normal(ks[0], (sl, bs, hs), dtype=jnp.float32)
        w_router = jax.random.normal(ks[1], (hs, E), dtype=jnp.float32) * 0.02
        w1 = jax.random.normal(ks[2], (E, hs, ffn), dtype=jnp.float32) * 0.02
        w2 = jax.random.normal(ks[3], (E, ffn, hs), dtype=jnp.float32) * 0.02
        bias = jnp.zeros((1, 1, hs), dtype=jnp.float32)
        return {'x': x, 'w_router': w_router, 'w1': w1, 'w2': w2, 'bias': bias}
    _L0_ffn_all = _L0_ffn_setup()
    _L0_ffn_in = {k: v for k, v in _L0_ffn_all.items() if k in ('w_router', 'w1', 'w2', 'bias')}
    del _L0_ffn_all
    return {'x': x, 'condB_tauraws': condB_tauraws, 'cond_256': cond_256, 'condB_bn2': condB_bn2, 'cond_1024': cond_1024, 'itok_B_0_6': itok_B_0_6, 'L0_cond_tau_ctx': _L0_cond_in['tau_ctx'], 'L0_cond_Wg': _L0_cond_in['Wg'], 'L0_cond_bg': _L0_cond_in['bg'], 'L0_cond_Wn1': _L0_cond_in['Wn1'], 'L0_cond_bn1': _L0_cond_in['bn1'], 'L0_cond_Wsoma': _L0_cond_in['Wsoma'], 'L0_cond_bsoma': _L0_cond_in['bsoma'], 'L0_cond_Wtemp': _L0_cond_in['Wtemp'], 'L0_cond_btemp': _L0_cond_in['btemp'], 'L0_cond_Wout': _L0_cond_in['Wout'], 'L0_cond_gamma': _L0_cond_in['gamma'], 'L0_cond_beta': _L0_cond_in['beta'], 'L0_attn_Wqkv': _L0_attn_in['Wqkv'], 'L0_attn_bqkv': _L0_attn_in['bqkv'], 'L0_attn_r_sigma': _L0_attn_in['r_sigma'], 'L0_attn_Wproj': _L0_attn_in['Wproj'], 'L0_attn_bproj': _L0_attn_in['bproj'], 'L0_cond2_down_w': _L0_cond2_in['down_w'], 'L0_cond2_down_b': _L0_cond2_in['down_b'], 'L0_cond2_up_w': _L0_cond2_in['up_w'], 'L0_cond2_up_b': _L0_cond2_in['up_b'], 'L0_cond2_ln_g': _L0_cond2_in['ln_g'], 'L0_cond2_ln_b': _L0_cond2_in['ln_b'], 'L0_ffn_w_router': _L0_ffn_in['w_router'], 'L0_ffn_w1': _L0_ffn_in['w1'], 'L0_ffn_w2': _L0_ffn_in['w2'], 'L0_ffn_bias': _L0_ffn_in['bias']}

def reference(x, condB_tauraws, cond_256, condB_bn2, cond_1024, itok_B_0_6, L0_cond_tau_ctx, L0_cond_Wg, L0_cond_bg, L0_cond_Wn1, L0_cond_bn1, L0_cond_Wsoma, L0_cond_bsoma, L0_cond_Wtemp, L0_cond_btemp, L0_cond_Wout, L0_cond_gamma, L0_cond_beta, L0_attn_Wqkv, L0_attn_bqkv, L0_attn_r_sigma, L0_attn_Wproj, L0_attn_bproj, L0_cond2_down_w, L0_cond2_down_b, L0_cond2_up_w, L0_cond2_up_b, L0_cond2_ln_g, L0_cond2_ln_b, L0_ffn_w_router, L0_ffn_w1, L0_ffn_w2, L0_ffn_bias):
    import jax
    import jax.numpy as jnp

    def _L0_cond_ref(x, tau_ctx, tau_raws, Wg, bg, Wn1, bn1, Wn2, bn2, blend, Wsoma, bsoma, Wtemp, btemp, Wout, gamma, beta):
        import jax, jax.numpy as jnp
        import numpy as np
        import math
        B, T, E, D = (4, 512, 256, 4)

        def _tau_init(t):
            a = 0.1 ** (1.0 / max(t - 1, 1))
            tt = -math.log(max(a, 1e-10))
            return math.log(math.exp(tt) - 1 + 1e-10)

        def causal_ema(b, tau_raw):
            alpha = jnp.exp(-jax.nn.softplus(tau_raw)).astype(b.dtype)

            def step(h, bt):
                h = alpha * h + bt
                return (h, h)
            h0 = jnp.zeros((b.shape[0], b.shape[2]), b.dtype)
            _, hs = jax.lax.scan(step, h0, jnp.swapaxes(b, 0, 1))
            return jnp.swapaxes(hs, 0, 1)
        ctx = causal_ema(x, tau_ctx)
        gate_in = jnp.concatenate([x, ctx], axis=-1)
        wg = jax.nn.sigmoid(jnp.einsum('btc,ec->bte', gate_in, Wg) + bg)
        gated = x * wg
        h1 = jax.nn.gelu(jnp.einsum('btc,hc->bth', x, Wn1) + bn1, approximate=False)
        mod = 0.5 + jax.nn.sigmoid(jnp.einsum('bth,dh->btd', h1, Wn2) + bn2)
        traces = jax.vmap(lambda tau, m: causal_ema(gated * m[..., None], tau))(tau_raws, jnp.moveaxis(mod, -1, 0))
        blend_w = jax.nn.softmax(blend, axis=0)
        temporal = jnp.einsum('dbtc,dc->btc', traces, blend_w)
        gate = jax.nn.sigmoid(jnp.einsum('btc,ec->bte', temporal, Wtemp) + btemp)
        soma = jax.nn.gelu(jnp.einsum('btc,ec->bte', x, Wsoma) + bsoma, approximate=False)
        out = jnp.einsum('btc,ec->bte', soma * gate, Wout)
        mu = out.mean(-1, keepdims=True)
        var = out.var(-1, keepdims=True)
        return (out - mu) / jnp.sqrt(var + 1e-05) * gamma + beta

    def _L0_attn_ref(x, Wqkv, bqkv, r_sigma, Wproj, bproj):
        import jax, jax.numpy as jnp
        import numpy as np
        B, T, C = (2, 512, 256)
        DIM, H = (256, 16)
        HD = DIM // H
        b, t, c = x.shape
        qkv = x @ Wqkv + bqkv
        qkv = qkv.reshape(b, t, 3, H, HD).transpose(2, 0, 3, 1, 4)
        q, k, v = (qkv[0], qkv[1], qkv[2])
        qn = jnp.sum(q * q, axis=-1)
        kn = jnp.sum(k * k, axis=-1)
        dot = jnp.einsum('bhid,bhjd->bhij', k, q)
        dist2 = kn[..., :, None] + qn[..., None, :] - 2.0 * dot
        Kmat = jnp.exp(-dist2 * r_sigma)
        out = jnp.einsum('bhij,bhjd->bhid', Kmat, v)
        out = out.transpose(0, 2, 1, 3).reshape(b, t, DIM)
        return out @ Wproj + bproj

    def _L0_cond2_ref(hidden, profile_ids, down_w, down_b, up_w, up_b, ln_g, ln_b):
        import jax, jax.numpy as jnp
        import numpy as np
        N_PROFILES = 8
        HIDDEN = 256
        BOTTLENECK = 128
        EPS = 1e-05
        Wd = down_w[profile_ids]
        bd = down_b[profile_ids][:, None]
        Wu = up_w[profile_ids]
        bu = up_b[profile_ids][:, None]
        g = ln_g[profile_ids][:, None]
        b = ln_b[profile_ids][:, None]
        z = jax.nn.relu(jnp.einsum('bsh,bhk->bsk', hidden, Wd) + bd)
        y = hidden + jnp.einsum('bsk,bkh->bsh', z, Wu) + bu
        mu = jnp.mean(y, axis=-1, keepdims=True)
        var = jnp.mean(jnp.square(y - mu), axis=-1, keepdims=True)
        return (y - mu) * jax.lax.rsqrt(var + EPS) * g + b

    def _L0_ffn_ref(x, w_router, w1, w2, bias):
        import jax, jax.numpy as jnp
        import numpy as np
        TOP_K = 2
        CAPACITY_FACTOR = 1.0
        sl, bs, hs = x.shape
        E = w_router.shape[1]
        xf = x.reshape(-1, hs)
        T = xf.shape[0]
        capacity = int(CAPACITY_FACTOR * TOP_K * T / E)
        scores = jax.nn.softmax(xf @ w_router, axis=-1)
        expert_weights, top_experts = jax.lax.top_k(scores, TOP_K)
        flat_e = top_experts.reshape(-1)
        flat_w = expert_weights.reshape(-1)
        N = flat_e.shape[0]
        order = jnp.argsort(flat_e, stable=True)
        bin_ids = flat_e[order]
        tpe = jnp.zeros((E,), jnp.int32).at[flat_e].add(1)
        starts = jnp.cumsum(tpe) - tpe
        offsets = jnp.arange(N) - starts[bin_ids]
        valid = offsets < capacity
        slot = jnp.where(valid, bin_ids * capacity + offsets, E * capacity)
        src = order // TOP_K
        xb = jnp.zeros((E * capacity + 1, hs), x.dtype).at[slot].set(xf[src])
        xb = xb[:-1].reshape(E, capacity, hs)
        h = jax.nn.gelu(jnp.einsum('ech,ehf->ecf', xb, w1))
        y = jnp.einsum('ecf,efh->ech', h, w2).reshape(E * capacity, hs)
        yv = jnp.where(valid[:, None], y[jnp.minimum(slot, E * capacity - 1)], 0.0)
        out = jnp.zeros((T, hs), x.dtype).at[src].add(flat_w[order][:, None] * yv)
        return out.reshape(sl, bs, hs) + bias
    x = x + _L0_attn_ref(_L0_cond_ref(x, L0_cond_tau_ctx, condB_tauraws, L0_cond_Wg, L0_cond_bg, L0_cond_Wn1, L0_cond_bn1, cond_256, condB_bn2, cond_1024, L0_cond_Wsoma, L0_cond_bsoma, L0_cond_Wtemp, L0_cond_btemp, L0_cond_Wout, L0_cond_gamma, L0_cond_beta), L0_attn_Wqkv, L0_attn_bqkv, L0_attn_r_sigma, L0_attn_Wproj, L0_attn_bproj)
    x = x + _L0_ffn_ref(_L0_cond2_ref(x, itok_B_0_6, L0_cond2_down_w, L0_cond2_down_b, L0_cond2_up_w, L0_cond2_up_b, L0_cond2_ln_g, L0_cond2_ln_b), L0_ffn_w_router, L0_ffn_w1, L0_ffn_w2, L0_ffn_bias)
    return x

_drawn_inputs = setup_inputs


def setup_inputs(seed=0):
    import zlib

    import numpy as np

    out = dict(_drawn_inputs(seed))
    spreads = {'condB_bn2': (0.0, 0.8),
     'L0_cond_bg': (-0.5, 0.6),
     'L0_cond_bn1': (0.0, 0.8),
     'L0_cond_bsoma': (0.0, 0.1),
     'L0_cond_btemp': (0.0, 0.269),
     'L0_cond_gamma': (1.0, 0.2),
     'L0_cond_beta': (0.0, 0.1),
     'L0_attn_bqkv': (0.0, 0.1),
     'L0_attn_bproj': (0.0, 0.8),
     'L0_cond2_ln_g': (1.0, 0.6),
     'L0_cond2_ln_b': (0.0, 0.8),
     'L0_ffn_bias': (0.0, 0.8)}
    factors = {'condB_tauraws': 8.0,
     'cond_256': 8.0,
     'cond_1024': 8.0,
     'L0_cond_Wn1': 8.0,
     'L0_cond2_down_w': 8.0,
     'L0_cond2_down_b': 64.0,
     'L0_cond2_up_w': 8.0,
     'L0_cond2_up_b': 64.0,
     'L0_ffn_w_router': 8.0,
     'L0_ffn_w1': 8.0,
     'L0_ffn_w2': 8.0}
    for name, (base, spread) in spreads.items():
        noise = np.random.default_rng([zlib.crc32(name.encode()), seed]).standard_normal(out[name].shape)
        drawn = base * np.exp(spread * noise) if base else spread * noise
        out[name] = jnp.asarray(drawn.astype(out[name].dtype))
    for name, factor in factors.items():
        out[name] = (out[name] * factor).astype(out[name].dtype)
    return out
```

```python
from contextlib import ExitStack

import concourse.bass as bass
from concourse import mybir

F32 = mybir.dt.float32
BF16 = mybir.dt.bfloat16
I32 = mybir.dt.int32
U32 = mybir.dt.uint32
ALU = mybir.AluOpType
ACT = mybir.ActivationFunctionType
AX_X = mybir.AxisListType.X

P = 128
B, T, E = 2, 1024, 256
N = B * T
CT = E // P
NT = N // P
BT = T // P
H, HD = 16, 16
HG = 4
NG = B * H // HG
HID = E // 4
D = 2
VW = HG * HD + HD
KQ = 6 * HD + 6
BOT = 128
NPROF = 8
NE, FF = 8, 1024
FT = FF // P
CAP = 2 * N // NE
ST = CAP // P
CH = 4
TC = NT // CH
ROW = E + 4
EPS = 1e-5
OOB = 8192
NROWS = N + P

C_BG, C_BSOMA, C_BTEMP, C_GAMMA, C_BETA, C_BQ, C_BK, C_BLEND, C_BN1, C_TAU, C_BN2, C_R = (
    0, 2, 4, 6, 8, 10, 12, 14, 18, 19, 22, 24)
NCOLS = 25


class Shared:

    def __init__(self, arrays):
        self.x = arrays["x"]
        self.xT = arrays["xT"]
        self.cols = arrays["cols"]
        self.rows = arrays["rows"]
        self.pid = arrays["pid"]
        self.WgT = arrays["WgT"]
        self.Wn1T = arrays["Wn1T"]
        self.Wn2T = arrays["Wn2T"]
        self.WsomaT = arrays["WsomaT"]
        self.WtempT = arrays["WtempT"]
        self.WoutT = arrays["WoutT"]
        self.Wqkv = arrays["Wqkv"]
        self.Wproj = arrays["Wproj"]
        self.down_w = arrays["down_w"]
        self.down_b = arrays["down_b"]
        self.up_w = arrays["up_w"]
        self.up_b = arrays["up_b"]
        self.ln_g = arrays["ln_g"]
        self.ln_b = arrays["ln_b"]
        self.Wr = arrays["Wr"]
        self.w1 = arrays["w1"]
        self.w2 = arrays["w2"]
        self.out = arrays["out"]


def build(nc, arrays):
    q_dram = nc.dram_tensor("q_parts", (3, B * E, T), BF16, kind="Internal").ap()
    k_dram = nc.dram_tensor("k_parts", (3, B * E, T), BF16, kind="Internal").ap()
    n_dram = nc.dram_tensor("norm_parts", (3, 2, B * H, T), BF16, kind="Internal").ap()
    o_dram = nc.dram_tensor("attn_out", (B * E, T), F32, kind="Internal").ap()
    slots_dram = nc.dram_tensor("slot_rows", (NE * CAP, ROW), F32, kind="Internal").ap()

    top = ExitStack()

    def sem(name):
        return top.enter_context(nc.semaphore(name))

    def sbuf(stack, name, shape, dt=F32):
        return stack.enter_context(nc.sbuf_tensor(name, shape, dt))

    with top:
        ident = sbuf(top, "ident", [P, P])
        cols_sb = sbuf(top, "cols_sb", [P, NCOLS])
        rows_sb = sbuf(top, "rows_sb", [P, 3, E])
        eps_sb = sbuf(top, "eps_sb", [P, 1])
        wproj_sb = sbuf(top, "wproj_sb", [P, CT, E])
        vals = sbuf(top, "vals", [P, NG, BT, VW])
        g = Shared(arrays)
        g.q_dram, g.k_dram, g.n_dram, g.o_dram, g.slots_dram = q_dram, k_dram, n_dram, o_dram, slots_dram
        g.ident, g.cols_sb, g.rows_sb, g.eps_sb, g.wproj_sb, g.vals = ident, cols_sb, rows_sb, eps_sb, wproj_sb, vals

        with ExitStack() as s:
            block_a(nc, s, sem, sbuf, g)
        with ExitStack() as s:
            block_b(nc, s, sem, sbuf, g)
        with ExitStack() as s:
            block_c(nc, s, sem, sbuf, g)
        with ExitStack() as s:
            block_d(nc, s, sem, sbuf, g)


def block_a(nc, s, sem, sbuf, g):
    ident, eps_sb, vals = g.ident, g.eps_sb, g.vals
    col = lambda c, n=1: g.cols_sb[:, c:c + n]
    wg_sb = sbuf(s, "wg_sb", [P, 2 * CT, E])
    wn1_sb = sbuf(s, "wn1_sb", [P, CT, HID])
    wn2_sb = sbuf(s, "wn2_sb", [HID, D])
    wn2_rep = sbuf(s, "wn2_rep", [HID, D, P])
    wsoma_sb = sbuf(s, "wsoma_sb", [P, CT, E])
    wtemp_sb = sbuf(s, "wtemp_sb", [P, CT, E])
    wout_sb = sbuf(s, "wout_sb", [P, CT, E])
    wqkv_sb = sbuf(s, "wqkv_sb", [P, CT, 3 * E])
    small = sbuf(s, "small", [P, 40])
    head_sel = sbuf(s, "head_sel", [P, 32])
    xT_sb = sbuf(s, "xT_sb", [P, CT, N])
    somaT = sbuf(s, "somaT", [P, CT, N])
    wgT = sbuf(s, "wgT", [P, CT, N])
    modT = sbuf(s, "modT", [P, D, N])
    ctxT = sbuf(s, "ctxT", [P, CT, N])
    traces = sbuf(s, "traces", [P, D, CT, N])
    h1T = sbuf(s, "h1T", [HID, N])
    parts = sbuf(s, "parts", [P, 2, 3, T], BF16)
    nparts = sbuf(s, "nparts", [P, 3, T], BF16)
    stats = sbuf(s, "stats", [P, NT, 6])
    mv = sbuf(s, "mv", [P, NT, 2])
    rstd = sbuf(s, "rstd", [P, 2, NT])
    cond = ctxT[:, :, :].rearrange("p c n -> p (c n)").rearrange("p (t e) -> p t e", e=E)
    hT = modT
    work = traces[:, :, :, :].rearrange("p d c n -> p (d c n)").rearrange("p (k t) -> p k t", t=T)
    squares, scaled, rest, norms = work[:, 0:4], work[:, 4:6], work[:, 6], work[:, 7]
    ps = s.enter_context(nc.psum_tensor("ps_a", [P, 4, T], F32))

    ALPHA, BW, R2, BQ2, T0 = small[:, 0:3], small[:, 4:8], small[:, 8:9], small[:, 10:12], small[:, 16:32]
    NEGR = small[:, 9:10]

    w_x, w_a, w_c, w_q = sem("x_loaded"), sem("early_weights_loaded"), sem("cols_loaded"), sem("late_weights_loaded")
    idt, dch = sem("ident_built"), sem("dve_a_chain")
    full = sem("ps_a_full")
    free = [sem(f"ps_a_free{i}") for i in range(4)]
    h1_ok, soma_ok, wg_ok, mod_ok, gate_ok = sem("h1_ok"), sem("soma_ok"), sem("wg_ok"), sem("mod_ok"), sem("gate_ok")
    ctx_ok, temp_ok, sg_ok, cond_ok, std_ok, ln_ok, hT_ok = (
        sem("ctx_ok"), sem("temp_ok"), sem("sg_ok"), sem("cond_ok"), sem("std_ok"), sem("ln_ok"), sem("hT_ok"))
    tau_ok, bl_ok, etau_ok, var_ok, rep_ok, sel_ok, coef_ok = (
        sem("tau_ok"), sem("blend_exp_ok"), sem("tau_exp_ok"), sem("var_ok"), sem("wn2_rep_ok"), sem("head_sel_ok"),
        sem("coef_ok"))
    sq_ok, scaled_ok, part1_ok, split_ok, stored, nrm_ok, nsplit_ok, nstored, val_ok = (
        sem("squares_ok"), sem("scaled_ok"), sem("part1_ok"), sem("split_ok"), [sem(f"parts_stored{i}") for i in range(2)], sem("norms_ok"),
        sem("norms_split"), sem("norms_stored"), sem("values_ok"))
    small_ok = sem("blend_shift_ok")

    order = ([("h1", b, 0) for b in range(B)] + [("soma", b, i) for b in range(B) for i in range(CT)]
             + [("wg", b, i) for b in range(B) for i in range(CT)] + [("mod", b, d) for b in range(B) for d in range(D)]
             + [("gate", b, i) for b in range(B) for i in range(CT)] + [("out", b, i) for b in range(B) for i in range(2)]
             + [("tr", b, i) for b in range(B) for i in range(CT)])
    for b in range(B):
        order += [("q", b, 0), ("q", b, 1), ("k", b, 0), ("k", b, 1), ("v", b, 0), ("v", b, 1), ("n", b, 0)]
    step = {o: i for i, o in enumerate(order)}
    buf = lambda o: ps[:, step[o] % 4]
    bs = lambda b: slice(b * T, (b + 1) * T)

    with nc.Block() as block:
        @block.sync
        def _(sp):
            sp.dma_start(xT_sb[:, 0, :], g.xT[0:P, :]).then_inc(w_x, 16)
            sp.dma_start(xT_sb[:, 1, :], g.xT[P:E, :]).then_inc(w_x, 16)
            for dst, src, k in ((wn1_sb, g.Wn1T, CT), (wsoma_sb, g.WsomaT, CT), (wg_sb, g.WgT, 2 * CT)):
                sp.dma_start(dst[:, :, :], src.rearrange("(k p) n -> p k n", p=P)).then_inc(w_a, 16)
            for dst, src in ((wtemp_sb, g.WtempT), (wout_sb, g.WoutT), (wqkv_sb, g.Wqkv), (g.wproj_sb, g.Wproj)):
                sp.dma_start(dst[:, :, :], src.rearrange("(k p) n -> p k n", p=P)).then_inc(w_q, 16)
            for u, (b, kind, i) in enumerate((b, kind, i) for b in range(B) for kind in "qk" for i in range(CT)):
                dst = g.q_dram if kind == "q" else g.k_dram
                sp.wait_ge(split_ok, u + 1)
                for j in range(3):
                    sp.dma_start(dst[j, b * E + i * P:b * E + (i + 1) * P, :], parts[:, u % 2, j, :]).then_inc(stored[u % 2], 16)
                if u % 4 == 3:
                    sp.wait_ge(nsplit_ok, b + 1)
                    for w in range(4):
                        kk, ii = w // 2, w % 2
                        for j in range(3):
                            sp.dma_start(g.n_dram[j, kk, b * H + 8 * ii:b * H + 8 * ii + 8, :],
                                         nparts[32 * w:32 * w + 8, j, :]).then_inc(nstored, 16)
            for i in range(2):
                sp.wait_ge(stored[i], 16 * 3 * 4)
            sp.wait_ge(nstored, 16 * 12 * B)

        @block.gpsimd
        def _(pool):
            pool.dma_start(g.cols_sb[:, :], g.cols).then_inc(w_c, 16)
            pool.dma_start(wn2_sb[:, :], g.Wn2T).then_inc(w_c, 16)
            pool.dma_start(g.rows_sb[:, :, :], g.rows.rearrange("(o r) e -> o r e", o=1).broadcast_to([P, 3, E])).then_inc(w_c, 16)
            nc.gpsimd.memset(ident[:, :], 0.0).then_inc(idt, 1)
            nc.gpsimd.memset(vals[:, :, :, :], 0.0).then_inc(idt, 1)
            pool.wait_ge(idt, 1)
            nc.gpsimd.affine_select(out=ident[:, :], in_=ident[:, :], compare_op=ALU.not_equal, fill=1.0, base=0,
                                    pattern=[[-1, P]], channel_multiplier=1).then_inc(idt, 1)
            nc.gpsimd.memset(eps_sb[:, :], EPS).then_inc(idt, 1)

        @block.vector
        def _(dve):
            chain = [0]

            def link(ins):
                chain[0] += 1
                ins.then_inc(dch, 1)
                dve.wait_ge(dch, chain[0])

            v = nc.vector
            dve.wait_ge(w_c, 48)
            link(v.tensor_tensor(T0[:, 0:2], col(C_BLEND, 2), col(C_BLEND + 2, 2), ALU.max))
            for d in range(D):
                last = v.tensor_tensor(T0[:, 2 + 2 * d:4 + 2 * d], col(C_BLEND + 2 * d, 2), T0[:, 0:2], ALU.subtract)
            last.then_inc(small_ok, 1)
            link(v.tensor_scalar(NEGR, col(C_R), -1.0, None, ALU.mult))
            dve.wait_ge(idt, 4)
            link(v.memset(head_sel[:, :], 0.0))
            link(v.tensor_reduce(head_sel[:, 0:8], ident[:, :].rearrange("p (h d) -> p h d", d=HD), AX_X, ALU.add))
            v.tensor_scalar(head_sel[:, 0:8], head_sel[:, 0:8], NEGR, None, ALU.mult).then_inc(sel_ok, 1)
            for d in range(D):
                last = v.tensor_copy(wn2_rep[:, d, :], wn2_sb[:, d:d + 1].to_broadcast([HID, P]))
            last.then_inc(rep_ok, 1)
            link(v.tensor_scalar(R2, col(C_R), 2.0, None, ALU.mult))
            v.tensor_scalar(BQ2, col(C_BQ, 2), R2, None, ALU.mult).then_inc(coef_ok, 1)
            dve.wait_ge(etau_ok, 2)
            link(v.tensor_scalar(T0[:, 6:9], small[:, 12:15], 1.0, None, ALU.add))
            link(v.reciprocal(ALPHA, T0[:, 6:9]))
            link(v.tensor_tensor(T0[:, 10:12], T0[:, 12:14], T0[:, 14:16], ALU.add))
            link(v.reciprocal(T0[:, 10:12], T0[:, 10:12]))
            for d in range(D):
                last = v.tensor_tensor(BW[:, 2 * d:2 * d + 2], T0[:, 12 + 2 * d:14 + 2 * d], T0[:, 10:12], ALU.mult)
            link(last)
            dve.wait_ge(w_x, 32)
            for b in range(B):
                for i in range(CT):
                    last = v.tensor_tensor_scan(ctxT[:, i, bs(b)], small[:, 0:1].to_broadcast([P, T]),
                                                xT_sb[:, i, bs(b)], 0.0, ALU.mult, ALU.add)
                last.then_inc(ctx_ok, 1)
            for b in range(B):
                dve.wait_ge(wg_ok, CT * (b + 1))
                link(v.tensor_tensor(wgT[:, :, bs(b)], wgT[:, :, bs(b)], xT_sb[:, :, bs(b)], ALU.mult))
                dve.wait_ge(mod_ok, D * (b + 1))
                for d in range(D):
                    for i in range(CT):
                        last = v.scalar_tensor_tensor(traces[:, d, i, bs(b)], modT[:, d, bs(b)], 0.5, wgT[:, i, bs(b)],
                                                      ALU.add, ALU.mult)
                link(last)
                for d in range(D):
                    for i in range(CT):
                        last = v.tensor_tensor_scan(traces[:, d, i, bs(b)], small[:, 1 + d:2 + d].to_broadcast([P, T]),
                                                    traces[:, d, i, bs(b)], 0.0, ALU.mult, ALU.add)
                link(last)
                for i in range(CT):
                    last = v.tensor_scalar(traces[:, 0, i, bs(b)], traces[:, 0, i, bs(b)], BW[:, i:i + 1], None, ALU.mult)
                link(last)
                for i in range(CT):
                    last = v.scalar_tensor_tensor(traces[:, 0, i, bs(b)], traces[:, 1, i, bs(b)], BW[:, 2 + i:3 + i],
                                                  traces[:, 0, i, bs(b)], ALU.mult, ALU.add)
                last.then_inc(temp_ok, 1)
            for b in range(B):
                dve.wait_ge(gate_ok, CT * (b + 1))
                dve.wait_ge(soma_ok, CT * (b + 1))
                v.tensor_tensor(somaT[:, :, bs(b)], somaT[:, :, bs(b)], wgT[:, :, bs(b)], ALU.mult).then_inc(sg_ok, 1)
            for b in range(B):
                tiles = range(b * BT, (b + 1) * BT)
                dve.wait_ge(cond_ok, 2 * (b + 1))
                for t in tiles:
                    last = v.bn_stats(stats[:, t, :], cond[:, t, :])
                link(last)
                for t in tiles:
                    last = v.bn_aggr(mv[:, t, :], stats[:, t, :])
                last.then_inc(var_ok, 1)
                dve.wait_ge(std_ok, b + 1)
                dve.wait_ge(var_ok, b + 1)
                link(v.reciprocal(rstd[:, 1, b * BT:(b + 1) * BT], rstd[:, 0, b * BT:(b + 1) * BT]))
                for t in tiles:
                    last = v.tensor_scalar(cond[:, t, :], cond[:, t, :], mv[:, t, 0:1], rstd[:, 1, t:t + 1],
                                           ALU.subtract, ALU.mult)
                last.then_inc(ln_ok, 1)
            for b in range(B):
                for i in range(CT):
                    o = ("tr", b, i)
                    dve.wait_ge(full, step[o] + 1)
                    v.tensor_scalar(hT[:, i, bs(b)], buf(o), col(C_GAMMA + i), col(C_BETA + i), ALU.mult,
                                    ALU.add).then_inc(free[step[o] % 4], 1)
            u = 0
            for b in range(B):
                for kind in "qk":
                    for i in range(CT):
                        dve.wait_ge(part1_ok, u + 1)
                        link(v.tensor_tensor(rest, scaled[:, u % 2], parts[:, u % 2, 0, :], ALU.subtract))
                        if u >= 2:
                            dve.wait_ge(stored[u % 2], 48 * (u // 2))
                        link(v.tensor_copy(parts[:, u % 2, 1, :], rest))
                        v.tensor_tensor(parts[:, u % 2, 2, :], rest, parts[:, u % 2, 1, :], ALU.subtract).then_inc(split_ok, 1)
                        u += 1
                        dve.wait_ge(split_ok, u)
                for j in range(2):
                    o = ("v", b, j)
                    dve.wait_ge(full, step[o] + 1)
                    for hg in range(4):
                        last = v.tensor_tensor(
                            vals[:, 4 * b + hg, 4 * j:4 * j + 4, 0:HG * HD],
                            buf(o).rearrange("p (t e) -> p t e", e=E)[:, :, 64 * hg:64 * hg + 64],
                            g.rows_sb[:, 0:1, 64 * hg:64 * hg + 64].to_broadcast([P, 4, 64]), ALU.add)
                    last.then_inc(free[step[o] % 4], 1)
                dve.wait_ge(nrm_ok, b + 1)
                if b:
                    dve.wait_ge(nstored, 16 * 12 * b)
                link(v.tensor_copy(nparts[:, 0, :], norms))
                link(v.tensor_tensor(rest, norms, nparts[:, 0, :], ALU.subtract))
                link(v.tensor_copy(nparts[:, 1, :], rest))
                v.tensor_tensor(nparts[:, 2, :], rest, nparts[:, 1, :], ALU.subtract).then_inc(nsplit_ok, 1)
                dve.wait_ge(nsplit_ok, b + 1)

        @block.scalar
        def _(act):
            a = nc.scalar.activation
            act.wait_ge(w_c, 48)
            a(small[:, 12:15], col(C_TAU, 3), ACT.Exp).then_inc(etau_ok, 1)
            act.wait_ge(small_ok, 1)
            a(T0[:, 12:16], T0[:, 2:6], ACT.Exp).then_inc(etau_ok, 1)

            def evacuate(o, ok, dst, src, func, **kw):
                act.wait_ge(full, step[o] + 1)
                a(dst, src, func, **kw).then_inc(ok, 1)

            def release(o):
                pass

            for b in range(B):
                evacuate(("h1", b, 0), h1_ok, h1T[:, bs(b)], buf(("h1", b, 0))[0:HID, :], ACT.Gelu,
                         bias=g.cols_sb[0:HID, C_BN1:C_BN1 + 1])
            for b in range(B):
                for i in range(CT):
                    evacuate(("soma", b, i), soma_ok, somaT[:, i, bs(b)], buf(("soma", b, i)), ACT.Gelu, bias=col(C_BSOMA + i))
            for b in range(B):
                for i in range(CT):
                    evacuate(("wg", b, i), wg_ok, wgT[:, i, bs(b)], buf(("wg", b, i)), ACT.Sigmoid, bias=col(C_BG + i))
            for b in range(B):
                for d in range(D):
                    evacuate(("mod", b, d), mod_ok, modT[:, d, bs(b)], buf(("mod", b, d)), ACT.Sigmoid, bias=col(C_BN2 + d))
            for b in range(B):
                for i in range(CT):
                    act.wait_ge(temp_ok, b + 1)
                    evacuate(("gate", b, i), gate_ok, wgT[:, i, bs(b)], buf(("gate", b, i)), ACT.Sigmoid, bias=col(C_BTEMP + i))
            act.wait_ge(idt, 4)
            for b in range(B):
                for j in range(2):
                    o = ("out", b, j)
                    evacuate(o, cond_ok, cond[:, b * BT + 4 * j:b * BT + 4 * j + 4, :].rearrange("p t e -> p (t e)"),
                             buf(o), ACT.Identity)
                act.wait_ge(var_ok, b + 1)
                a(rstd[:, 0, b * BT:(b + 1) * BT], mv[:, b * BT:(b + 1) * BT, 1], ACT.Sqrt, bias=eps_sb[:, :]).then_inc(std_ok, 1)
            act.wait_ge(coef_ok, 1)
            u = 0
            for b in range(B):
                for kind in "qk":
                    for i in range(CT):
                        o = (kind, b, i)
                        act.wait_ge(full, step[o] + 1)
                        if b:
                            act.wait_ge(full, step[("n", b - 1, 0)] + 1)
                        bias = col((C_BQ if kind == "q" else C_BK) + i)
                        a(squares[:, 2 * (kind == "k") + i], buf(o), ACT.Square, bias=bias).then_inc(sq_ok, 1)
                        if u >= 2:
                            act.wait_ge(split_ok, u - 1)
                            act.wait_ge(stored[u % 2], 48 * (u // 2))
                        if kind == "q":
                            a(scaled[:, u % 2], buf(o), ACT.Identity, bias=BQ2[:, i:i + 1], scale=R2).then_inc(scaled_ok, 1)
                        else:
                            a(scaled[:, u % 2], buf(o), ACT.Identity, bias=bias).then_inc(scaled_ok, 1)
                        u += 1
                        act.wait_ge(scaled_ok, u)
                        a(parts[:, (u - 1) % 2, 0, :], scaled[:, (u - 1) % 2], ACT.Copy).then_inc(part1_ok, 1)
                o = ("n", b, 0)
                if b:
                    act.wait_ge(nsplit_ok, b)
                evacuate(o, nrm_ok, norms, buf(o), ACT.Identity)

        def read_of(o):
            kind, b, i = o
            return {"h1": (h1_ok, b + 1), "soma": (soma_ok, CT * b + i + 1), "wg": (wg_ok, CT * b + i + 1),
                    "mod": (mod_ok, D * b + i + 1), "gate": (gate_ok, CT * b + i + 1), "out": (cond_ok, 2 * b + i + 1),
                    "q": (scaled_ok, 4 * b + i + 1), "k": (scaled_ok, 4 * b + 2 + i + 1), "n": (nrm_ok, b + 1),
                    }.get(kind)

        @block.tensor
        def _(pe):
            frees = [0] * 4

            def start(o):
                if step[o] >= 4:
                    last = order[step[o] - 4]
                    r = read_of(last)
                    if r is None:
                        frees[step[last] % 4] += 1
                        pe.wait_ge(free[step[last] % 4], frees[step[last] % 4])
                    else:
                        pe.wait_ge(r[0], r[1])

            def product(o, m, lhsT, rhs, ks):
                start(o)
                for half in range(2):
                    hs = slice(512 * half, 512 * half + 512)
                    for k in range(ks):
                        last = nc.tensor.matmul(buf(o)[0:m, hs], lhsT(k), rhs(k, half), start=(k == 0), stop=(k == ks - 1))
                last.then_inc(full, 1)

            def tok(b, half):
                return slice(b * T + 512 * half, b * T + 512 * half + 512)

            pe.wait_ge(w_x, 32)
            pe.wait_ge(w_a, 48)
            for b in range(B):
                product(("h1", b, 0), HID, lambda k: wn1_sb[:, k, :], lambda k, h: xT_sb[:, k, tok(b, h)], CT)
            for b in range(B):
                for i in range(CT):
                    product(("soma", b, i), P, lambda k: wsoma_sb[:, k, i * P:(i + 1) * P],
                            lambda k, h: xT_sb[:, k, tok(b, h)], CT)
            for b in range(B):
                pe.wait_ge(ctx_ok, b + 1)
                for i in range(CT):
                    product(("wg", b, i), P, lambda k: wg_sb[:, k, i * P:(i + 1) * P],
                            lambda k, h: (xT_sb if k < CT else ctxT)[:, k % CT, tok(b, h)], 2 * CT)
            pe.wait_ge(rep_ok, 1)
            for b in range(B):
                pe.wait_ge(h1_ok, b + 1)
                for d in range(D):
                    product(("mod", b, d), P, lambda k: wn2_rep[:, d, :], lambda k, h: h1T[:, tok(b, h)], 1)
            pe.wait_ge(w_q, 64)
            for b in range(B):
                pe.wait_ge(temp_ok, b + 1)
                for i in range(CT):
                    product(("gate", b, i), P, lambda k: wtemp_sb[:, k, i * P:(i + 1) * P],
                            lambda k, h: traces[:, 0, k, tok(b, h)], CT)

            def rows_product(o, t0, lhsT, rhs):
                start(o)
                for j in range(4):
                    for k in range(CT):
                        last = nc.tensor.matmul(buf(o)[:, j * E:(j + 1) * E], lhsT(k, t0 + j), rhs(k), start=(k == 0),
                                                stop=(k == CT - 1))
                last.then_inc(full, 1)

            for b in range(B):
                pe.wait_ge(sg_ok, b + 1)
                for j in range(2):
                    rows_product(("out", b, j), b * BT + 4 * j, lambda k, t: somaT[:, k, t * P:(t + 1) * P],
                                 lambda k: wout_sb[:, k, :])
            pe.wait_ge(idt, 3)
            for b in range(B):
                pe.wait_ge(ln_ok, b + 1)
                for i in range(CT):
                    o = ("tr", b, i)
                    start(o)
                    for t in range(BT):
                        last = nc.tensor.transpose(buf(o)[:, t * P:(t + 1) * P], cond[:, b * BT + t, i * P:(i + 1) * P],
                                                   ident[:, :])
                    last.then_inc(full, 1)
            for n in range(4):
                o = order[step[("tr", 0, 0)] + n]
                pe.wait_ge(free[step[o] % 4], 1)
            pe.wait_ge(sel_ok, 1)
            for b in range(B):
                for c, kind in enumerate("qk"):
                    for i in range(CT):
                        product((kind, b, i), P, lambda k: wqkv_sb[:, k, c * E + i * P:c * E + (i + 1) * P],
                                lambda k, h: hT[:, k, tok(b, h)], CT)
                for j in range(2):
                    rows_product(("v", b, j), b * BT + 4 * j, lambda k, t: hT[:, k, t * P:(t + 1) * P],
                                 lambda k: wqkv_sb[:, k, 2 * E:3 * E])
                o = ("n", b, 0)
                start(o)
                pe.wait_ge(sq_ok, 4 * (b + 1))
                for half in range(2):
                    for w in range(4):
                        last = nc.tensor.matmul(buf(o)[32 * w:32 * w + 32, 512 * half:512 * half + 512], head_sel[:, :],
                                                squares[:, w, 512 * half:512 * half + 512], start=True, stop=True)
                last.then_inc(full, 1)


def block_b(nc, s, sem, sbuf, g):
    qa = [sbuf(s, f"qa{i}", [KQ, HG, T], BF16) for i in range(2)]
    ka = [sbuf(s, f"ka{i}", [KQ, HG, T], BF16) for i in range(2)]
    vg = [sbuf(s, f"vg{i}", [P, BT, VW]) for i in range(2)]
    probs = sbuf(s, "probs", [P, 2, HG, T])
    ost = [sbuf(s, f"ost{i}", [P, T]) for i in range(2)]
    fill = sbuf(s, "fill", [P, ROW])
    sc = [s.enter_context(nc.psum_tensor(f"scores{i}", [P, T], F32)) for i in range(2)]
    acc = [s.enter_context(nc.psum_tensor(f"acc{i}", [P, T], F32)) for i in range(2)]
    STEPS = BT * HG
    LOADS = 16 * 15
    loaded = [sem(f"group_loaded{i}") for i in range(2)]
    ones_ok = sem("ones_in_place")
    scored, exped, pv, evac = sem("scored"), sem("exped"), sem("pv_done"), sem("acc_evacuated")
    ost_out = [sem(f"ost_out{i}") for i in range(2)]
    filled = sem("fill_ready")
    fill_out = sem("fill_out")
    PV0 = 8
    EV0 = 2

    with nc.Block() as block:
        @block.gpsimd
        def _(pool):
            nc.gpsimd.memset(fill[:, :], 0.0).then_inc(filled, 1)
            pool.wait_ge(filled, 1)
            nc.gpsimd.iota(fill[:, E:E + 1].bitcast(I32), [[0, 1]], base=N, channel_multiplier=1).then_inc(filled, 1)
            pool.wait_ge(filled, 2)
            for c in range(NE * CAP // P):
                pool.dma_start(g.slots_dram[c * P:(c + 1) * P, :], fill[:, :]).then_inc(fill_out, 16)
            pool.dma_start(g.out[N:NROWS, :], fill[:, 0:E]).then_inc(fill_out, 16)
            pool.wait_ge(fill_out, 16 * (NE * CAP // P + 1))

        @block.sync
        def _(sp):
            def load(grp, gg, i):
                if gg is None:
                    sp.wait_ge(ones_ok, 2 * (i + 1))
                else:
                    sp.wait_ge(pv, grp * STEPS + (PV0 - STEPS))
                rows = lambda d, j: d[j, bass.ds(grp * (HG * HD), HG * HD), :].rearrange("(h d) t -> d h t", d=HD)
                for r, j in enumerate((0, 1, 2, 0, 1, 0)):
                    sp.dma_start(qa[i][r * HD:(r + 1) * HD, :, :], rows(g.q_dram, j)).then_inc(loaded[i], 16)
                for r, j in enumerate((0, 0, 0, 1, 1, 2)):
                    sp.dma_start(ka[i][r * HD:(r + 1) * HD, :, :], rows(g.k_dram, j)).then_inc(loaded[i], 16)
                for kk, dst in ((0, qa[i][99:102]), (1, ka[i][96:99])):
                    sp.dma_start(dst, g.n_dram[:, kk, bass.ds(grp * HG, HG), :]).then_inc(loaded[i], 16)
                sp.dma_start(vg[i][:, :, :], g.vals[:, bass.ds(grp, 1), :, :].rearrange("p o t w -> p (o t) w")).then_inc(loaded[i], 16)

            def store(grp, i):
                sp.wait_ge(evac, EV0 + 1 + grp)
                for h in range(HG):
                    sp.dma_start(g.o_dram[bass.ds(grp * (HG * HD) + h * HD, HD), :], ost[i][32 * h:32 * h + HD, :]).then_inc(ost_out[i], 16)

            load(0, None, 0)
            load(1, None, 1)
            with sp.Fori(0, NG // 2 - 1) as gg:
                load(gg * 2 + 2, gg + 1, 0)
                store(gg * 2, 0)
                load(gg * 2 + 3, gg + 1, 1)
                store(gg * 2 + 1, 1)
            store(NG - 2, 0)
            store(NG - 1, 1)
            for i in range(2):
                sp.wait_ge(ost_out[i], 64 + 64 * NG // 2)

        @block.vector
        def _(dve):
            v = nc.vector
            for i in range(2):
                v.memset(qa[i][96:102, :, :], 1.0).then_inc(ones_ok, 1)
                v.memset(ka[i][96:102, :, :], 1.0).then_inc(ones_ok, 1)
            v.memset(ost[0][:, 0:1], 0.0).then_inc(ost_out[0], 64)
            v.memset(ost[1][:, 0:1], 0.0).then_inc(ost_out[1], 64)
            v.memset(ost[0][:, 1:2], 0.0).then_inc(pv, PV0)
            v.memset(ost[1][:, 1:2], 0.0).then_inc(evac, EV0)
            dve.wait_ge(evac, EV0)

            def evacuate(grp, gg, i):
                dve.wait_ge(pv, grp * STEPS + (PV0 + STEPS))
                dve.wait_ge(ost_out[i], gg * 64 + 64)
                v.tensor_copy(ost[i][:, :], acc[i][:, :]).then_inc(evac, 1)

            with dve.Fori(0, NG // 2) as gg:
                evacuate(gg * 2, gg, 0)
                evacuate(gg * 2 + 1, gg, 1)

        @block.scalar
        def _(act):
            with act.Fori(0, NG // 2) as gg:
                for i in range(2):
                    base = gg * (2 * STEPS) + i * STEPS
                    for n in range(STEPS):
                        t, h = n // HG, n % HG
                        act.wait_ge(scored, base + (n + 1))
                        if h == 0:
                            act.wait_ge(pv, base + (PV0 + HG * t - HG))
                        nc.scalar.activation(probs[:, t % 2, h, :], sc[n % 2][:, :], ACT.Exp).then_inc(exped, 1)

        @block.tensor
        def _(pe):
            def scores(i, n):
                t, h = n // HG, n % HG
                for half in range(2):
                    last = nc.tensor.matmul(sc[n % 2][:, 512 * half:512 * half + 512], qa[i][:, h, t * P:(t + 1) * P],
                                            ka[i][:, h, 512 * half:512 * half + 512], start=True, stop=True)
                last.then_inc(scored, 1)

            def values(i, m):
                t, q = m // 4, m % 4
                for h in range(HG):
                    last = nc.tensor.matmul(acc[i][32 * h:32 * h + 32, 256 * q:256 * q + 256],
                                            vg[i][:, t, HD * h:HD * h + 32], probs[:, t % 2, h, 256 * q:256 * q + 256],
                                            start=(t == 0 and q % 2 == 0), stop=(t == BT - 1), skip_group_check=True)
                last.then_inc(pv, 1)

            def group(grp, gg, i, more, next_gg):
                pe.wait_ge(evac, grp + 1)
                for n in range(STEPS):
                    pe.wait_ge(exped, grp * STEPS + (n + 1))
                    if n + 2 < STEPS:
                        scores(i, n + 2)
                    elif more:
                        if n + 2 == STEPS:
                            pe.wait_ge(loaded[1 - i], next_gg * LOADS + LOADS)
                        scores(1 - i, n + 2 - STEPS)
                    if n >= HG - 1:
                        values(i, n - (HG - 1))
                for m in range(STEPS - HG + 1, STEPS):
                    values(i, m)

            pe.wait_ge(loaded[0], LOADS)
            scores(0, 0)
            scores(0, 1)
            with pe.Fori(0, NG // 2 - 1) as gg:
                group(gg * 2, gg, 0, True, gg)
                group(gg * 2 + 1, gg, 1, True, gg + 1)
            group(NG - 2, None, 0, True, NG // 2 - 1)
            group(NG - 1, None, 1, False, None)


def block_c(nc, s, sem, sbuf, g):
    ident = g.ident
    oT = sbuf(s, "oT", [P, CT, N])
    xr = sbuf(s, "xr", [P, NT, E])
    xbu = sbuf(s, "xbu", [P, 2, TC, E])
    outr = sbuf(s, "outr", [P, 2, TC, E])
    x1T = sbuf(s, "x1T", [P, 2, CT, TC * P])
    zT = sbuf(s, "zT", [P, 2, TC * P])
    y = sbuf(s, "y", [P, 2, TC, E])
    xfT = sbuf(s, "xfT", [P, 2, CT, TC * P])
    drow = sbuf(s, "drow", [P, NT, ROW])
    wd = sbuf(s, "wd", [P, B, CT, BOT])
    bd = sbuf(s, "bd", [P, B])
    wu = sbuf(s, "wu", [P, B, E])
    rowp = sbuf(s, "rowp", [P, B, 3, E])
    wr = sbuf(s, "wr", [P, CT, NE])
    pid_sb = sbuf(s, "pid_sb", [1, B], I32)
    stats = sbuf(s, "stats_c", [P, NT, 6])
    mv = sbuf(s, "mv_c", [P, NT, 2])
    sd = sbuf(s, "sd_c", [P, 2, NT])
    lg = sbuf(s, "lg", [P, NT, NE])
    mx = sbuf(s, "mx", [P, NT, 8])
    ix = sbuf(s, "ix", [P, NT, 8], U32)
    dl = sbuf(s, "dl", [P, NT, NE + 1])
    ex = sbuf(s, "ex", [P, NT, NE + 1])
    zz = sbuf(s, "zz", [P, NT, 2])
    ixf = sbuf(s, "ixf", [P, 2, NT])
    oh = sbuf(s, "oh", [P, 2, NT, NE])
    chosen = sbuf(s, "chosen", [P, NT, NE])
    off = sbuf(s, "off", [P, NT, NE])
    base = sbuf(s, "base", [P, NT + 1, NE])
    tmp = sbuf(s, "tmp", [P, 2, NT, NE])
    offk = sbuf(s, "offk", [P, 2, NT])
    over = sbuf(s, "over", [P, 2, NT])
    slotf = sbuf(s, "slotf", [P, 2, NT])
    sloti = sbuf(s, "sloti", [P, 2, NT], U32)
    iota_e = sbuf(s, "iota_e", [P, NE])
    iota_i = sbuf(s, "iota_i", [P, NE], I32)
    before = sbuf(s, "before", [P, P])
    ones = sbuf(s, "ones", [P, P])
    ps = s.enter_context(nc.psum_tensor("ps_c", [P, 4, T], F32))

    w_pid, w_d, w_o, w_x, w_r = sem("pid_loaded"), sem("adapter_loaded"), sem("attn_loaded"), sem("x_rows_loaded"), sem("router_loaded")
    cst, dch = sem("c_constants"), sem("dve_c_chain")
    full = sem("ps_c_full")
    x1_ok, t1_ok, z_ok, y_ok, var_ok, sd_ok, xf_ok, t2_ok, lg_ok, dl_ok, ex_ok, ch_ok, slot_ok, xbu_ok, out_ok, disp, outd, off_ok = (
        sem("x1_ok"), sem("x1T_ok"), sem("z_ok"), sem("y_ok"), sem("var_c_ok"), sem("sd_c_ok"), sem("xf_ok"), sem("xfT_ok"),
        sem("logits_ok"), sem("shifted_ok"), sem("expd_ok"), sem("chosen_ok"), sem("slots_ok"), sem("xbu_ok"), sem("outr_ok"),
        sem("dispatched"), [sem(f"out_started{i}") for i in range(2)], sem("offsets_ok"))
    xb_ok = sem("x_plus_bias_ok")

    STAGES = ("proj", "t1", "z", "y", "t2", "lg", "pre")
    order = [(st, w - k) for w in range(CH + len(STAGES) - 1) for k, st in reversed(list(enumerate(STAGES))) if 0 <= w - k < CH]
    step = {o: i for i, o in enumerate(order)}
    buf = lambda o: ps[:, step[o] % 4]
    tl = lambda c: slice(c * TC, (c + 1) * TC)

    with nc.Block() as block:
        @block.sync
        def _(sp):
            for b in range(B):
                for i in range(CT):
                    sp.dma_start(oT[:, i, b * T:(b + 1) * T], g.o_dram[b * E + i * P:b * E + (i + 1) * P, :]).then_inc(w_o, 16)
            sp.dma_start(pid_sb[:, :], g.pid).then_inc(w_pid, 16)
            sp.wait_ge(w_pid, 16)
            for b in range(B):
                prof = sp.value_load(pid_sb[0:1, b:b + 1], min_val=0, max_val=NPROF - 1)
                one = bass.ds(prof, 1)
                sp.dma_start(wd[:, b, :, :], g.down_w[one, :, :].rearrange("o (k p) n -> p (o k) n", p=P)).then_inc(w_d, 16)
                sp.dma_start(bd[:, b:b + 1], g.down_b[one, :].rearrange("o n -> n o")).then_inc(w_d, 16)
                sp.dma_start(wu[:, b, :], g.up_w[one, :, :].rearrange("o k n -> (o k) n")).then_inc(w_d, 16)
                for j, src in enumerate((g.up_b, g.ln_g, g.ln_b)):
                    sp.dma_start(rowp[:, b, j, :], src[one, :].broadcast_to([P, E])).then_inc(w_d, 16)
            for c in range(CH):
                sp.wait_ge(out_ok, c + 1)
                sp.dma_start(g.out[c * TC * P:(c + 1) * TC * P, :].rearrange("(t p) e -> p t e", p=P),
                             outr[:, c % 2, :, :]).then_inc(outd[c % 2], 16)
            for i in range(2):
                sp.wait_ge(outd[i], 16 * CH // 2)

        @block.gpsimd
        def _(pool):
            p = nc.gpsimd
            pool.dma_start(wr[:, :, :], g.Wr.rearrange("(k p) n -> p k n", p=P)).then_inc(w_r, 16)
            pool.dma_start(xr[:, :, :], g.x.rearrange("(t p) e -> p t e", p=P)).then_inc(w_x, 16)
            p.memset(before[:, :], 1.0).then_inc(cst, 1)
            p.memset(ones[:, :], 1.0)
            p.memset(base[:, 0, :], 0.0).then_inc(cst, 1)
            p.iota(iota_i[:, :], [[1, NE]], base=0, channel_multiplier=0).then_inc(cst, 1)
            for t in range(NT):
                last = p.iota(drow[:, t, E:E + 1].bitcast(I32), [[0, 1]], base=t * P, channel_multiplier=1)
            last.then_inc(cst, 1)
            pool.wait_ge(cst, 4)
            p.tensor_copy(iota_e[:, :], iota_i[:, :]).then_inc(cst, 1)
            p.affine_select(out=before[:, :], in_=before[:, :], compare_op=ALU.is_gt, fill=0.0, base=0,
                            pattern=[[1, P]], channel_multiplier=-1).then_inc(cst, 1)
            pool.wait_ge(w_x, 16)
            bias = lambda j, n: g.rows_sb[:, j:j + 1, :].to_broadcast([P, n, E])
            for c in range(CH):
                p.tensor_tensor(xr[:, tl(c), :], xr[:, tl(c), :], bias(1, TC), ALU.add).then_inc(xb_ok, 1)
            pool.wait_ge(w_d, 16 * 6 * B)
            for w in range(CH + 3):
                if w < CH:
                    c = w
                    pool.wait_ge(x1_ok, c + 1)
                    if c >= 2:
                        pool.wait_ge(outd[c % 2], 16 * (c // 2))
                        pool.wait_ge(y_ok, c - 1)
                    b = c * TC // BT
                    p.tensor_tensor(xbu[:, c % 2, :, :], xr[:, tl(c), :], rowp[:, b, 0:1, :].to_broadcast([P, TC, E]),
                                    ALU.add).then_inc(xbu_ok, 1)
                    p.tensor_tensor(outr[:, c % 2, :, :], xr[:, tl(c), :], bias(2, TC), ALU.add).then_inc(out_ok, 1)
                if w >= 3:
                    c = w - 3
                    pool.wait_ge(slot_ok, c + 1)
                    for t in range(c * TC, (c + 1) * TC):
                        for k in range(2):
                            pool.indirect_dma_start(
                                g.slots_dram, bass.IndirectOffsetOnAxis(ap=sloti[:, k, t:t + 1], axis=0),
                                drow[:, t, :], None, bounds_check=NE * CAP - 1, oob_is_err=False).then_inc(disp, 16)
            pool.wait_ge(disp, 16 * 2 * NT)

        @block.vector
        def _(dve):
            chain = [0]

            def link(ins):
                chain[0] += 1
                ins.then_inc(dch, 1)
                dve.wait_ge(dch, chain[0])

            v = nc.vector

            def x1(c):
                dve.wait_ge(full, step["proj", c] + 1)
                dve.wait_ge(xb_ok, c + 1)
                v.tensor_tensor(xr[:, tl(c), :], buf(("proj", c)).rearrange("p (t e) -> p t e", e=E), xr[:, tl(c), :],
                                ALU.add).then_inc(x1_ok, 1)

            def norm(c):
                b = c * TC // BT
                dve.wait_ge(full, step["y", c] + 1)
                dve.wait_ge(xbu_ok, c + 1)
                v.tensor_tensor(y[:, c % 2, :, :], buf(("y", c)).rearrange("p (t e) -> p t e", e=E), xbu[:, c % 2, :, :],
                                ALU.add).then_inc(y_ok, 1)
                dve.wait_ge(y_ok, c + 1)
                for j in range(TC):
                    last = v.bn_stats(stats[:, c * TC + j, :], y[:, c % 2, j, :])
                link(last)
                for j in range(TC):
                    last = v.bn_aggr(mv[:, c * TC + j, :], stats[:, c * TC + j, :])
                last.then_inc(var_ok, 1)
                dve.wait_ge(var_ok, c + 1)
                dve.wait_ge(sd_ok, c + 1)
                link(v.reciprocal(sd[:, 1, tl(c)], sd[:, 0, tl(c)]))
                for j in range(TC):
                    t = c * TC + j
                    last = v.tensor_scalar(y[:, c % 2, j, :], y[:, c % 2, j, :], mv[:, t, 0:1], sd[:, 1, t:t + 1],
                                           ALU.subtract, ALU.mult)
                link(last)
                link(v.tensor_tensor(y[:, c % 2, :, :], y[:, c % 2, :, :], rowp[:, b, 1:2, :].to_broadcast([P, TC, E]), ALU.mult))
                v.tensor_tensor(drow[:, tl(c), 0:E], y[:, c % 2, :, :], rowp[:, b, 2:3, :].to_broadcast([P, TC, E]),
                                ALU.add).then_inc(xf_ok, 1)

            def choose(c):
                ts = tl(c)
                dve.wait_ge(full, step["lg", c] + 1)
                v.tensor_copy(lg[:, ts, :], buf(("lg", c))[:, 0:TC * NE].rearrange("p (t e) -> p t e", e=NE)).then_inc(lg_ok, 1)
                dve.wait_ge(lg_ok, c + 1)
                for t in range(c * TC, (c + 1) * TC):
                    last = v.max(mx[:, t, :], lg[:, t, :])
                link(last)
                v.tensor_tensor(dl[:, ts, 0:NE], lg[:, ts, :], mx[:, ts, 0:1].to_broadcast([P, TC, NE]), ALU.subtract)
                v.tensor_tensor(dl[:, ts, NE:NE + 1], mx[:, ts, 1:2], mx[:, ts, 0:1], ALU.subtract).then_inc(dl_ok, 1)
                for t in range(c * TC, (c + 1) * TC):
                    last = v.max_index(ix[:, t, :], mx[:, t, :], lg[:, t, :])
                link(last)
                for k in range(2):
                    last = v.tensor_copy(ixf[:, k, ts], ix[:, ts, k])
                link(last)
                for k in range(2):
                    last = v.tensor_tensor(oh[:, k, ts, :], ixf[:, k, ts].unsqueeze(2).to_broadcast([P, TC, NE]),
                                           iota_e[:, :].unsqueeze(1).to_broadcast([P, TC, NE]), ALU.is_equal)
                link(last)
                v.tensor_tensor(chosen[:, ts, :], oh[:, 0, ts, :], oh[:, 1, ts, :], ALU.add).then_inc(ch_ok, 1)
                v.tensor_copy(drow[:, ts, E + 3], ixf[:, 0, ts])
                dve.wait_ge(ex_ok, c + 1)
                link(v.tensor_reduce(zz[:, ts, 0], ex[:, ts, 0:NE], AX_X, ALU.add))
                link(v.reciprocal(zz[:, ts, 1], zz[:, ts, 0]))
                v.tensor_copy(drow[:, ts, E + 1], zz[:, ts, 1])
                link(v.tensor_tensor(drow[:, ts, E + 2], ex[:, ts, NE], zz[:, ts, 1], ALU.mult))

            def slots(c):
                ts = tl(c)
                dve.wait_ge(full, step["pre", c] + 1)
                pre = buf(("pre", c))
                for j in range(TC):
                    t = c * TC + j
                    link(v.tensor_tensor(base[:, t + 1, :], pre[:, 512 + NE * j:512 + NE * (j + 1)], base[:, t, :], ALU.add))
                v.tensor_tensor(off[:, ts, :], pre[:, 0:TC * NE].rearrange("p (t e) -> p t e", e=NE),
                                base[:, ts, :], ALU.add).then_inc(off_ok, 1)
                dve.wait_ge(off_ok, c + 1)
                for k in range(2):
                    last = v.tensor_tensor(tmp[:, k, ts, :], off[:, ts, :], oh[:, k, ts, :], ALU.mult)
                link(last)
                link(v.tensor_reduce(offk[:, :, ts], tmp[:, :, ts, :], AX_X, ALU.add))
                v.tensor_scalar(over[:, :, ts], offk[:, :, ts], float(CAP), float(OOB), ALU.is_ge, ALU.mult)
                link(v.scalar_tensor_tensor(slotf[:, :, ts], ixf[:, :, ts], float(CAP), offk[:, :, ts], ALU.mult, ALU.add))
                v.tensor_tensor(sloti[:, :, ts], slotf[:, :, ts], over[:, :, ts], ALU.add).then_inc(slot_ok, 1)

            dve.wait_ge(w_d, 16 * 6 * B)
            dve.wait_ge(cst, 6)
            stages = {"proj": x1, "y": norm, "lg": choose, "pre": slots}
            for st, c in order:
                if st in stages:
                    stages[st](c)

        @block.scalar
        def _(act):
            a = nc.scalar.activation

            def t1(c):
                act.wait_ge(full, step["t1", c] + 1)
                if c >= 2:
                    act.wait_ge(full, step["z", c - 2] + 1)
                a(x1T[:, c % 2, :, :].rearrange("p k t -> p (k t)"), buf(("t1", c)), ACT.Copy).then_inc(t1_ok, 1)

            def z(c):
                b = c * TC // BT
                act.wait_ge(full, step["z", c] + 1)
                if c >= 2:
                    act.wait_ge(full, step["y", c - 2] + 1)
                act.wait_ge(w_d, 16 * 6 * B)
                a(zT[:, c % 2, :], buf(("z", c))[:, 0:TC * P], ACT.Relu, bias=bd[:, b:b + 1]).then_inc(z_ok, 1)

            def root(c):
                act.wait_ge(var_ok, c + 1)
                a(sd[:, 0, tl(c)], mv[:, tl(c), 1], ACT.Sqrt, bias=g.eps_sb[:, :]).then_inc(sd_ok, 1)

            def t2(c):
                act.wait_ge(full, step["t2", c] + 1)
                if c >= 2:
                    act.wait_ge(full, step["lg", c - 2] + 1)
                a(xfT[:, c % 2, :, :].rearrange("p k t -> p (k t)"), buf(("t2", c)), ACT.Copy).then_inc(t2_ok, 1)

            def soft(c):
                act.wait_ge(dl_ok, c + 1)
                a(ex[:, tl(c), :], dl[:, tl(c), :], ACT.Exp).then_inc(ex_ok, 1)

            stages = {"t1": t1, "z": z, "y": root, "t2": t2, "lg": soft}
            for st, c in order:
                if st in stages:
                    stages[st](c)

        read_of = {"proj": x1_ok, "t1": t1_ok, "z": z_ok, "y": y_ok, "t2": t2_ok, "lg": lg_ok, "pre": off_ok}

        @block.tensor
        def _(pe):
            def start(o):
                if step[o] >= 4:
                    st, c = order[step[o] - 4]
                    pe.wait_ge(read_of[st], c + 1)

            def transposed(c, src):
                for k in range(CT):
                    for j in range(TC):
                        last = nc.tensor.transpose(buf_of[:, (k * TC + j) * P:(k * TC + j + 1) * P], src(j, k), ident[:, :])
                last.then_inc(full, 1)

            pe.wait_ge(w_o, 16 * B * CT)
            pe.wait_ge(w_d, 16 * 6 * B)
            pe.wait_ge(w_r, 16)
            pe.wait_ge(cst, 6)
            for o in order:
                st, c = o
                start(o)
                buf_of = buf(o)
                b = c * TC // BT
                if st == "proj":
                    for j in range(TC):
                        t = c * TC + j
                        for k in range(CT):
                            last = nc.tensor.matmul(buf_of[:, j * E:(j + 1) * E], oT[:, k, t * P:(t + 1) * P],
                                                    g.wproj_sb[:, k, :], start=(k == 0), stop=(k == CT - 1))
                    last.then_inc(full, 1)
                elif st == "t1":
                    pe.wait_ge(x1_ok, c + 1)
                    transposed(c, lambda j, k: xr[:, c * TC + j, k * P:(k + 1) * P])
                elif st == "z":
                    pe.wait_ge(t1_ok, c + 1)
                    for k in range(CT):
                        last = nc.tensor.matmul(buf_of[:, 0:TC * P], wd[:, b, k, :], x1T[:, c % 2, k, :], start=(k == 0),
                                                stop=(k == CT - 1))
                    last.then_inc(full, 1)
                elif st == "y":
                    pe.wait_ge(z_ok, c + 1)
                    for j in range(TC):
                        last = nc.tensor.matmul(buf_of[:, j * E:(j + 1) * E], zT[:, c % 2, j * P:(j + 1) * P], wu[:, b, :],
                                                start=True, stop=True)
                    last.then_inc(full, 1)
                elif st == "t2":
                    pe.wait_ge(xf_ok, c + 1)
                    transposed(c, lambda j, k: drow[:, c * TC + j, k * P:(k + 1) * P])
                elif st == "lg":
                    pe.wait_ge(t2_ok, c + 1)
                    for j in range(TC):
                        for k in range(CT):
                            last = nc.tensor.matmul(buf_of[:, j * NE:(j + 1) * NE], xfT[:, c % 2, k, j * P:(j + 1) * P],
                                                    wr[:, k, :], start=(k == 0), stop=(k == CT - 1))
                    last.then_inc(full, 1)
                else:
                    pe.wait_ge(ch_ok, c + 1)
                    ch = chosen[:, tl(c), :].rearrange("p t e -> p (t e)")
                    nc.tensor.matmul(buf_of[:, 0:TC * NE], before[:, :], ch, start=True, stop=True)
                    nc.tensor.matmul(buf_of[:, 512:512 + TC * NE], ones[:, :], ch, start=True, stop=True).then_inc(full, 1)


def block_d(nc, s, sem, sbuf, g):
    xin = [sbuf(s, f"xin{i}", [P, ST, ROW]) for i in range(2)]
    w1s = [sbuf(s, f"w1s{i}", [P, CT, FF]) for i in range(2)]
    w2s = [sbuf(s, f"w2s{i}", [P, FT, E]) for i in range(2)]
    xeT = [sbuf(s, f"xeT{i}", [P, CT, CAP]) for i in range(2)]
    hidT = [sbuf(s, f"hidT{i}", [P, FT, CAP]) for i in range(2)]
    ye = [sbuf(s, f"ye{i}", [P, ST, E]) for i in range(2)]
    wsel = [sbuf(s, f"wsel{i}", [P, 4, ST]) for i in range(2)]
    tok = [sbuf(s, f"tok{i}", [P, ST], U32) for i in range(2)]
    expert = sbuf(s, "expert", [P, 1])
    ps_t = s.enter_context(nc.psum_tensor("ps_t", [P, CT * CAP], F32))
    ps_h = s.enter_context(nc.psum_tensor("ps_h", [P, 4, CAP], F32))
    ps_y = s.enter_context(nc.psum_tensor("ps_y", [P, ST * E], F32))
    xl = [sem(f"slot_rows_loaded{i}") for i in range(2)]
    wl = [sem(f"expert_weights_loaded{i}") for i in range(2)]
    tr, trc, hid, gel, yp, yc, sel, added, ech = (sem("x_transposed"), sem("xeT_ok"), sem("hidden_ready"), sem("gelu_done"),
                                                 sem("y_ready"), sem("y_weighted"), sem("weights_selected"),
                                                 sem("rows_added"), sem("expert_counter"))
    dch = sem("dve_d_chain")

    with nc.Block() as block:
        @block.sync
        def _(sp):
            for e in range(NE):
                i = e % 2
                if e >= 2:
                    sp.wait_ge(yp, e - 1)
                    sp.wait_ge(tr, e - 1)
                    sp.wait_ge(sel, e - 1)
                sp.dma_start(xin[i][:, :, :], g.slots_dram[e * CAP:(e + 1) * CAP, :].rearrange("(t p) r -> p t r", p=P)).then_inc(xl[i], 16)
                sp.dma_start(w1s[i][:, :, :], g.w1[e].rearrange("(k p) f -> p k f", p=P)).then_inc(wl[i], 16)
                sp.dma_start(w2s[i][:, :, :], g.w2[e].rearrange("(k p) n -> p k n", p=P)).then_inc(wl[i], 16)

        @block.gpsimd
        def _(pool):
            for e in range(NE):
                pool.wait_ge(yc, e + 1)
                for t in range(ST):
                    if e or t:
                        pool.wait_ge(added, 16 * (ST * e + t))
                    pool.indirect_dma_start(g.out, bass.IndirectOffsetOnAxis(ap=tok[e % 2][:, t:t + 1], axis=0),
                                            ye[e % 2][:, t, :], None, bounds_check=NROWS - 1, oob_is_err=True,
                                            compute_op=ALU.add).then_inc(added, 16)
            pool.wait_ge(added, 16 * ST * NE)

        @block.vector
        def _(dve):
            chain = [0]

            def link(ins):
                chain[0] += 1
                ins.then_inc(dch, 1)
                dve.wait_ge(dch, chain[0])

            v = nc.vector

            def take(e):
                i = e % 2
                dve.wait_ge(tr, e + 1)
                if e >= 2:
                    dve.wait_ge(hid, FT * (e - 1))
                v.tensor_copy(xeT[i][:, :, :].rearrange("p k s -> p (k s)"), ps_t[:, :]).then_inc(trc, 1)
                if e >= 2:
                    dve.wait_ge(added, 16 * ST * (e - 1))
                v.tensor_copy(tok[i][:, :], xin[i][:, :, E].bitcast(U32))
                link(v.tensor_scalar(wsel[i][:, 0, :], xin[i][:, :, E + 3], float(e), None, ALU.is_equal))
                link(v.tensor_tensor(wsel[i][:, 1, :], wsel[i][:, 0, :], xin[i][:, :, E + 1], ALU.mult))
                link(v.tensor_scalar(wsel[i][:, 2, :], wsel[i][:, 0, :], -1.0, 1.0, ALU.mult, ALU.add))
                link(v.tensor_tensor(wsel[i][:, 2, :], wsel[i][:, 2, :], xin[i][:, :, E + 2], ALU.mult))
                v.tensor_tensor(wsel[i][:, 3, :], wsel[i][:, 1, :], wsel[i][:, 2, :], ALU.add).then_inc(sel, 1)

            take(0)
            for e in range(NE):
                i = e % 2
                if e + 1 < NE:
                    take(e + 1)
                dve.wait_ge(yp, e + 1)
                dve.wait_ge(sel, e + 1)
                if e >= 2:
                    dve.wait_ge(added, 16 * ST * (e - 1))
                for t in range(ST):
                    last = v.tensor_scalar(ye[i][:, t, :], ps_y[:, t * E:(t + 1) * E], wsel[i][:, 3, t:t + 1], None, ALU.mult)
                last.then_inc(yc, 1)

        @block.scalar
        def _(act):
            for e in range(NE):
                for f in range(FT):
                    act.wait_ge(hid, FT * e + f + 1)
                    if f == 0 and e >= 2:
                        act.wait_ge(yp, e - 1)
                    nc.scalar.activation(hidT[e % 2][:, f, :], ps_h[:, f % 4, :], ACT.Gelu_apprx_tanh).then_inc(gel, 1)

        @block.tensor
        def _(pe):
            def turn(e):
                pe.wait_ge(xl[e % 2], 16 * (e // 2 + 1))
                if e:
                    pe.wait_ge(trc, e)
                for k in range(CT):
                    for t in range(ST):
                        last = nc.tensor.transpose(ps_t[:, k * CAP + t * P:k * CAP + (t + 1) * P],
                                                   xin[e % 2][:, t, k * P:(k + 1) * P], g.ident[:, :])
                last.then_inc(tr, 1)

            turn(0)
            for e in range(NE):
                i = e % 2
                pe.wait_ge(wl[i], 32 * (e // 2 + 1))
                pe.wait_ge(trc, e + 1)
                for f in range(FT):
                    if e or f >= 4:
                        pe.wait_ge(gel, FT * e + f - 3)
                    for k in range(CT):
                        last = nc.tensor.matmul(ps_h[:, f % 4, :], w1s[i][:, k, f * P:(f + 1) * P], xeT[i][:, k, :],
                                                start=(k == 0), stop=(k == CT - 1))
                    last.then_inc(hid, 1)
                if e + 1 < NE:
                    turn(e + 1)
                pe.wait_ge(gel, FT * (e + 1))
                if e:
                    pe.wait_ge(yc, e)
                for t in range(ST):
                    for f in range(FT):
                        last = nc.tensor.matmul(ps_y[:, t * E:(t + 1) * E], hidT[i][:, f, t * P:(t + 1) * P], w2s[i][:, f, :],
                                                start=(f == 0), stop=(f == FT - 1))
                last.then_inc(yp, 1)


def kernel(**inputs):
    import numpy as np
    import concourse.bacc as bacc
    from concourse.bass_utils import run_bass_kernel_spmd

    a = {k: np.asarray(v) for k, v in inputs.items()}
    f = lambda n: a["L0_" + n]
    tile = lambda v: v.reshape(-1, P).T
    every = lambda v: np.broadcast_to(v.reshape(1, -1), (P, v.size))
    bqkv = f("attn_bqkv")
    cols = np.concatenate([
        tile(f("cond_bg")), tile(f("cond_bsoma")), tile(f("cond_btemp")), tile(f("cond_gamma")), tile(f("cond_beta")),
        tile(bqkv[0:E]), tile(bqkv[E:2 * E]), tile(a["cond_1024"].reshape(-1)),
        np.pad(f("cond_bn1"), (0, P - HID)).reshape(P, 1), every(f("cond_tau_ctx")), every(a["condB_tauraws"]),
        every(a["condB_bn2"]), every(f("attn_r_sigma"))], axis=1)
    rows = np.stack([bqkv[2 * E:], f("attn_bproj"), f("ffn_bias").reshape(-1)])
    x = a["x"].reshape(N, E)
    arrays = {
        "x": x, "xT": x.T, "cols": cols, "rows": rows, "pid": a["itok_B_0_6"].reshape(1, B),
        "WgT": f("cond_Wg").T, "Wn1T": f("cond_Wn1").T, "Wn2T": a["cond_256"].T, "WsomaT": f("cond_Wsoma").T,
        "WtempT": f("cond_Wtemp").T, "WoutT": f("cond_Wout").T, "Wqkv": f("attn_Wqkv"), "Wproj": f("attn_Wproj"),
        "down_w": f("cond2_down_w"), "down_b": f("cond2_down_b"), "up_w": f("cond2_up_w"), "up_b": f("cond2_up_b"),
        "ln_g": f("cond2_ln_g"), "ln_b": f("cond2_ln_b"), "Wr": f("ffn_w_router"), "w1": f("ffn_w1"), "w2": f("ffn_w2")}
    arrays = {k: np.ascontiguousarray(v) for k, v in arrays.items()}
    nc = bacc.Bacc("TRN2", target_bir_lowering=False, num_devices=1)
    aps = {k: nc.dram_tensor(f"in_{k}", v.shape, mybir.dt.from_np(v.dtype), kind="ExternalInput").ap() for k, v in arrays.items()}
    out = nc.dram_tensor("out_rows", (NROWS, E), F32, kind="ExternalOutput").ap()
    aps["out"] = out
    build(nc, aps)
    r = run_bass_kernel_spmd(nc, [{f"in_{k}": v for k, v in arrays.items()}], core_ids=[0])
    return r.results[0]["out_rows"][:N].reshape(B, T, E)
```

```python
from contextlib import ExitStack

import concourse.bass as bass
from concourse import mybir

F32 = mybir.dt.float32
F32R = mybir.dt.float32r
BF16 = mybir.dt.bfloat16
I32 = mybir.dt.int32
U32 = mybir.dt.uint32
ALU = mybir.AluOpType
ACT = mybir.ActivationFunctionType
AX_X = mybir.AxisListType.X

P = 128
B, T, E = 2, 1024, 256
N = B * T
CT = E // P
NT = N // P
BT = T // P
H, HD = 16, 16
HG = 4
NG = B * H // HG
HID = E // 4
D = 2
VW = HG * HD + HD
KQ = 6 * HD + 6
BOT = 128
NPROF = 8
NE, FF = 8, 1024
FT = FF // P
CAP = 2 * N // NE
ST = CAP // P
CH = 4
TC = NT // CH
ROW = E + 4
EPS = 1e-5
OOB = 8192
NROWS = N + P

C_BG, C_BSOMA, C_BTEMP, C_GAMMA, C_BETA, C_BQ, C_BK, C_BLEND, C_BN1, C_TAU, C_BN2, C_R = (
    0, 2, 4, 6, 8, 10, 12, 14, 18, 19, 22, 24)
NCOLS = 25


class Shared:

    def __init__(self, arrays):
        self.x = arrays["x"]
        self.xT = arrays["xT"]
        self.cols = arrays["cols"]
        self.rows = arrays["rows"]
        self.pid = arrays["pid"]
        self.WgT = arrays["WgT"]
        self.Wn1T = arrays["Wn1T"]
        self.Wn2T = arrays["Wn2T"]
        self.WsomaT = arrays["WsomaT"]
        self.WtempT = arrays["WtempT"]
        self.WoutT = arrays["WoutT"]
        self.Wqkv = arrays["Wqkv"]
        self.Wproj = arrays["Wproj"]
        self.down_w = arrays["down_w"]
        self.down_b = arrays["down_b"]
        self.up_w = arrays["up_w"]
        self.up_b = arrays["up_b"]
        self.ln_g = arrays["ln_g"]
        self.ln_b = arrays["ln_b"]
        self.Wr = arrays["Wr"]
        self.w1 = arrays["w1"]
        self.w2 = arrays["w2"]
        self.out = arrays["out"]


def build(nc, arrays):
    q_dram = nc.dram_tensor("q_parts", (3, B * E, T), BF16, kind="Internal").ap()
    k_dram = nc.dram_tensor("k_parts", (3, B * E, T), BF16, kind="Internal").ap()
    n_dram = nc.dram_tensor("norm_parts", (3, 2, B * H, T), BF16, kind="Internal").ap()
    o_dram = nc.dram_tensor("attn_out", (B * E, T), F32, kind="Internal").ap()
    slots_dram = nc.dram_tensor("slot_rows", (NE * CAP, ROW), F32, kind="Internal").ap()

    top = ExitStack()

    def sem(name):
        return top.enter_context(nc.semaphore(name))

    def sbuf(stack, name, shape, dt=F32):
        return stack.enter_context(nc.sbuf_tensor(name, shape, dt))

    with top:
        ident = sbuf(top, "ident", [P, P])
        cols_sb = sbuf(top, "cols_sb", [P, NCOLS])
        rows_sb = sbuf(top, "rows_sb", [P, 3, E])
        eps_sb = sbuf(top, "eps_sb", [P, 1])
        wproj_sb = sbuf(top, "wproj_sb", [P, CT, E])
        ones_bf = sbuf(top, "ones_bf", [3, T], BF16)
        fill = sbuf(top, "fill", [P, ROW])
        vals = sbuf(top, "vals", [P, NG, BT, VW])
        g = Shared(arrays)
        g.ones_bf, g.fill = ones_bf, fill
        g.q_dram, g.k_dram, g.n_dram, g.o_dram, g.slots_dram = q_dram, k_dram, n_dram, o_dram, slots_dram
        g.ident, g.cols_sb, g.rows_sb, g.eps_sb, g.wproj_sb, g.vals = ident, cols_sb, rows_sb, eps_sb, wproj_sb, vals

        with ExitStack() as s:
            block_a(nc, s, sem, sbuf, g)
        g.raw1 = [sbuf(top, f"raw1_{i}", [P, CT, FF]) for i in range(2)]
        g.raw2 = [sbuf(top, f"raw2_{i}", [P, FT, E]) for i in range(2)]
        g.wl = [sem(f"expert_weights_loaded{i}") for i in range(2)]
        with ExitStack() as shared:
            g.oT = sbuf(shared, "oT", [P, CT, N])
            g.xr = sbuf(shared, "xr", [P, NT, E])
            g.xbu = sbuf(shared, "xbu", [P, NT, E])
            g.xb_ok = sem("x_plus_bias_ok")
            g.wd = sbuf(shared, "wd", [P, B, CT, BOT])
            g.bd = sbuf(shared, "bd", [P, B])
            g.wu = sbuf(shared, "wu", [P, B, E])
            g.rowp = sbuf(shared, "rowp", [P, B, 3, E])
            g.wr = sbuf(shared, "wr", [P, CT, NE])
            g.w_d, g.w_o, g.w_x, g.w_r = sem("adapter_loaded"), sem("attn_loaded"), sem("x_rows_loaded"), sem("router_loaded")
            with ExitStack() as s:
                block_b(nc, s, sem, sbuf, g)
            with ExitStack() as s:
                block_c(nc, s, sem, sbuf, g)
        with ExitStack() as s:
            block_d(nc, s, sem, sbuf, g)


def block_a(nc, s, sem, sbuf, g):
    ident, eps_sb, vals = g.ident, g.eps_sb, g.vals
    col = lambda c, n=1: g.cols_sb[:, c:c + n]
    wg_sb = sbuf(s, "wg_sb", [P, 2 * CT, E])
    wn1_sb = sbuf(s, "wn1_sb", [P, CT, HID])
    wn2_sb = sbuf(s, "wn2_sb", [HID, D])
    wn2_rep = sbuf(s, "wn2_rep", [HID, D, P])
    wsoma_sb = sbuf(s, "wsoma_sb", [P, CT, E])
    wtemp_sb = sbuf(s, "wtemp_sb", [P, CT, E])
    wout_sb = sbuf(s, "wout_sb", [P, CT, E])
    wqkv_sb = sbuf(s, "wqkv_sb", [P, CT, 3 * E])
    small = sbuf(s, "small", [P, 40])
    head_sel = sbuf(s, "head_sel", [P, 32])
    xT_sb = sbuf(s, "xT_sb", [P, CT, N])
    somaT = sbuf(s, "somaT", [P, CT, N])
    wgT = sbuf(s, "wgT", [P, CT, N])
    modT = sbuf(s, "modT", [P, D, N])
    ctxT = sbuf(s, "ctxT", [P, CT, N])
    traces = sbuf(s, "traces", [P, D, CT, N])
    h1T = sbuf(s, "h1T", [HID, N])
    parts = sbuf(s, "parts", [P, 2, 3, T], BF16)
    nparts = sbuf(s, "nparts", [P, 3, T], BF16)
    stats = sbuf(s, "stats", [P, NT, 6])
    mv = sbuf(s, "mv", [P, NT, 2])
    rstd = sbuf(s, "rstd", [P, 2, NT])
    cond = ctxT[:, :, :].rearrange("p c n -> p (c n)").rearrange("p (t e) -> p t e", e=E)
    hT = modT
    work = traces[:, :, :, :].rearrange("p d c n -> p (d c n)").rearrange("p (k t) -> p k t", t=T)
    squares, scaled, rest, norms = work[:, 0:4], work[:, 4:6], work[:, 6], work[:, 7]
    ps = s.enter_context(nc.psum_tensor("ps_a", [P, 4, T], F32))

    ALPHA, BW, R2, BQ2, T0 = small[:, 0:3], small[:, 4:8], small[:, 8:9], small[:, 10:12], small[:, 16:32]
    NEGR = small[:, 9:10]

    w_x, w_a, w_c, w_q = [sem(f"x_loaded{b}") for b in range(B)], sem("early_weights_loaded"), sem("cols_loaded"), sem("late_weights_loaded")
    idt, dch = sem("ident_built"), sem("dve_a_chain")
    full = sem("ps_a_full")
    h1_ok, soma_ok, wg_ok, mod_ok, gate_ok = sem("h1_ok"), sem("soma_ok"), sem("wg_ok"), sem("mod_ok"), sem("gate_ok")
    ctx_ok, temp_ok, sg_ok, cond_ok, std_ok, ln_ok, hT_ok = (
        sem("ctx_ok"), sem("temp_ok"), sem("sg_ok"), sem("cond_ok"), sem("std_ok"), sem("ln_ok"), sem("hT_ok"))
    tau_ok, bl_ok, etau_ok, var_ok, rep_ok, sel_ok, coef_ok = (
        sem("tau_ok"), sem("blend_exp_ok"), sem("tau_exp_ok"), sem("var_ok"), sem("wn2_rep_ok"), sem("head_sel_ok"),
        sem("coef_ok"))
    sq_ok, scaled_ok, part1_ok, split_ok, stored, nrm_ok, nsplit_ok, nstored, val_ok = (
        sem("squares_ok"), sem("scaled_ok"), sem("part1_ok"), sem("split_ok"), [sem(f"parts_stored{i}") for i in range(2)], sem("norms_ok"),
        sem("norms_split"), sem("norms_stored"), sem("values_ok"))
    small_ok, filled, fill_out = sem("blend_shift_ok"), sem("fill_ready"), sem("fill_out")

    order = [("h1", b, 0) for b in range(B)]
    for b in range(B):
        order += [("wg", b, 0), ("wg", b, 1), ("mod", b, 0), ("mod", b, 1)]
    for kind in ("soma", "gate", "out"):
        order += [(kind, b, i) for b in range(B) for i in range(CT)]
    for b in range(B):
        order += [("tr", b, 0), ("tr", b, 1), ("q", b, 0), ("q", b, 1), ("k", b, 0), ("k", b, 1), ("n", b, 0)]
    order += [("v", b, i) for b in range(B) for i in range(CT)]
    step = {o: i for i, o in enumerate(order)}
    buf = lambda o: ps[:, step[o] % 4]
    bs = lambda b: slice(b * T, (b + 1) * T)

    with nc.Block() as block:
        @block.sync
        def _(sp):
            for b in range(B):
                for i in range(CT):
                    sp.dma_start(xT_sb[:, i, bs(b)], g.xT[i * P:(i + 1) * P, bs(b)]).then_inc(w_x[b], 16)
            for dst, src, k in ((wn1_sb, g.Wn1T, CT), (wsoma_sb, g.WsomaT, CT), (wg_sb, g.WgT, 2 * CT)):
                sp.dma_start(dst[:, :, :], src.rearrange("(k p) n -> p k n", p=P)).then_inc(w_a, 16)
            for dst, src in ((wtemp_sb, g.WtempT), (wout_sb, g.WoutT), (wqkv_sb, g.Wqkv), (g.wproj_sb, g.Wproj)):
                sp.dma_start(dst[:, :, :], src.rearrange("(k p) n -> p k n", p=P)).then_inc(w_q, 16)
            for u, (b, kind, i) in enumerate((b, kind, i) for b in range(B) for kind in "qk" for i in range(CT)):
                dst = g.q_dram if kind == "q" else g.k_dram
                sp.wait_ge(split_ok, u + 1)
                for j in range(3):
                    sp.dma_start(dst[j, b * E + i * P:b * E + (i + 1) * P, :], parts[:, u % 2, j, :]).then_inc(stored[u % 2], 16)
                if u % 4 == 3:
                    sp.wait_ge(nsplit_ok, b + 1)
                    for w in range(4):
                        kk, ii = w // 2, w % 2
                        for j in range(3):
                            sp.dma_start(g.n_dram[j, kk, b * H + 8 * ii:b * H + 8 * ii + 8, :],
                                         nparts[32 * w:32 * w + 8, j, :]).then_inc(nstored, 16)
            for i in range(2):
                sp.wait_ge(stored[i], 16 * 3 * 4)
            sp.wait_ge(nstored, 16 * 12 * B)

        @block.gpsimd
        def _(pool):
            pool.dma_start(g.cols_sb[:, :], g.cols).then_inc(w_c, 16)
            pool.dma_start(wn2_sb[:, :], g.Wn2T).then_inc(w_c, 16)
            pool.dma_start(g.rows_sb[:, :, :], g.rows.rearrange("(o r) e -> o r e", o=1).broadcast_to([P, 3, E])).then_inc(w_c, 16)
            nc.gpsimd.memset(ident[:, :], 0.0).then_inc(idt, 1)
            nc.gpsimd.memset(vals[:, :, :, :], 0.0).then_inc(idt, 1)
            pool.wait_ge(idt, 1)
            nc.gpsimd.affine_select(out=ident[:, :], in_=ident[:, :], compare_op=ALU.not_equal, fill=1.0, base=0,
                                    pattern=[[-1, P]], channel_multiplier=1).then_inc(idt, 1)
            nc.gpsimd.memset(eps_sb[:, :], EPS).then_inc(idt, 1)
            nc.gpsimd.memset(g.ones_bf[:, :], 1.0).then_inc(filled, 1)
            nc.gpsimd.memset(g.fill[:, :], 0.0).then_inc(filled, 1)
            pool.wait_ge(filled, 2)
            nc.gpsimd.iota(g.fill[:, E:E + 1].bitcast(I32), [[0, 1]], base=N, channel_multiplier=1).then_inc(filled, 1)
            pool.wait_ge(filled, 3)
            pool.wait_ge(wg_ok, 1)
            for c in range(NE * CAP // P):
                pool.dma_start(g.slots_dram[c * P:(c + 1) * P, :], g.fill[:, :]).then_inc(fill_out, 16)
            pool.dma_start(g.out[N:NROWS, :], g.fill[:, 0:E]).then_inc(fill_out, 16)
            pool.wait_ge(fill_out, 16 * (NE * CAP // P + 1))

        @block.vector
        def _(dve):
            chain = [0]

            def link(ins):
                chain[0] += 1
                ins.then_inc(dch, 1)
                dve.wait_ge(dch, chain[0])

            v = nc.vector
            dve.wait_ge(w_c, 48)
            link(v.tensor_tensor(T0[:, 0:2], col(C_BLEND, 2), col(C_BLEND + 2, 2), ALU.max))
            for d in range(D):
                last = v.tensor_tensor(T0[:, 2 + 2 * d:4 + 2 * d], col(C_BLEND + 2 * d, 2), T0[:, 0:2], ALU.subtract)
            last.then_inc(small_ok, 1)
            link(v.tensor_scalar(NEGR, col(C_R), -1.0, None, ALU.mult))
            dve.wait_ge(idt, 4)
            link(v.memset(head_sel[:, :], 0.0))
            link(v.tensor_reduce(head_sel[:, 0:8], ident[:, :].rearrange("p (h d) -> p h d", d=HD), AX_X, ALU.add))
            v.tensor_scalar(head_sel[:, 0:8], head_sel[:, 0:8], NEGR, None, ALU.mult).then_inc(sel_ok, 1)
            for d in range(D):
                last = v.tensor_copy(wn2_rep[:, d, :], wn2_sb[:, d:d + 1].to_broadcast([HID, P]))
            last.then_inc(rep_ok, 1)
            link(v.tensor_scalar(R2, col(C_R), 2.0, None, ALU.mult))
            v.tensor_scalar(BQ2, col(C_BQ, 2), R2, None, ALU.mult).then_inc(coef_ok, 1)
            dve.wait_ge(etau_ok, 2)
            link(v.tensor_scalar(T0[:, 6:9], small[:, 12:15], 1.0, None, ALU.add))
            link(v.reciprocal(ALPHA, T0[:, 6:9]))
            link(v.tensor_tensor(T0[:, 10:12], T0[:, 12:14], T0[:, 14:16], ALU.add))
            link(v.reciprocal(T0[:, 10:12], T0[:, 10:12]))
            for d in range(D):
                last = v.tensor_tensor(BW[:, 2 * d:2 * d + 2], T0[:, 12 + 2 * d:14 + 2 * d], T0[:, 10:12], ALU.mult)
            link(last)
            for b in range(B):
                dve.wait_ge(w_x[b], 32)
                for i in range(CT):
                    last = v.tensor_tensor_scan(ctxT[:, i, bs(b)], small[:, 0:1].to_broadcast([P, T]),
                                                xT_sb[:, i, bs(b)], 0.0, ALU.mult, ALU.add)
                last.then_inc(ctx_ok, 1)
            for b in range(B):
                dve.wait_ge(wg_ok, CT * (b + 1))
                link(v.tensor_tensor(wgT[:, :, bs(b)], wgT[:, :, bs(b)], xT_sb[:, :, bs(b)], ALU.mult))
                dve.wait_ge(mod_ok, D * (b + 1))
                for d in range(D):
                    for i in range(CT):
                        last = v.scalar_tensor_tensor(traces[:, d, i, bs(b)], modT[:, d, bs(b)], 0.5, wgT[:, i, bs(b)],
                                                      ALU.add, ALU.mult)
                link(last)
                for d in range(D):
                    for i in range(CT):
                        last = v.tensor_tensor_scan(traces[:, d, i, bs(b)], small[:, 1 + d:2 + d].to_broadcast([P, T]),
                                                    traces[:, d, i, bs(b)], 0.0, ALU.mult, ALU.add)
                link(last)
                for i in range(CT):
                    last = v.tensor_scalar(traces[:, 0, i, bs(b)], traces[:, 0, i, bs(b)], BW[:, i:i + 1], None, ALU.mult)
                link(last)
                for i in range(CT):
                    last = v.scalar_tensor_tensor(traces[:, 0, i, bs(b)], traces[:, 1, i, bs(b)], BW[:, 2 + i:3 + i],
                                                  traces[:, 0, i, bs(b)], ALU.mult, ALU.add)
                last.then_inc(temp_ok, 1)
            for b in range(B):
                dve.wait_ge(gate_ok, CT * (b + 1))
                dve.wait_ge(soma_ok, CT * (b + 1))
                v.tensor_tensor(somaT[:, :, bs(b)], somaT[:, :, bs(b)], wgT[:, :, bs(b)], ALU.mult).then_inc(sg_ok, 1)
            for b in range(B):
                tiles = range(b * BT, (b + 1) * BT)
                dve.wait_ge(cond_ok, 2 * (b + 1))
                for t in tiles:
                    last = v.bn_stats(stats[:, t, :], cond[:, t, :])
                link(last)
                for t in tiles:
                    last = v.bn_aggr(mv[:, t, :], stats[:, t, :])
                last.then_inc(var_ok, 1)
                dve.wait_ge(std_ok, b + 1)
                dve.wait_ge(var_ok, b + 1)
                link(v.reciprocal(rstd[:, 1, b * BT:(b + 1) * BT], rstd[:, 0, b * BT:(b + 1) * BT]))
                for t in tiles:
                    last = v.tensor_scalar(cond[:, t, :], cond[:, t, :], mv[:, t, 0:1], rstd[:, 1, t:t + 1],
                                           ALU.subtract, ALU.mult)
                last.then_inc(ln_ok, 1)

            def to_T(b):
                for i in range(CT):
                    o = ("tr", b, i)
                    dve.wait_ge(full, step[o] + 1)
                    v.tensor_scalar(hT[:, i, bs(b)], buf(o), col(C_GAMMA + i), col(C_BETA + i), ALU.mult,
                                    ALU.add).then_inc(hT_ok, 1)

            u = 0
            for b in range(B):
                to_T(b)
                for kind in "qk":
                    for i in range(CT):
                        dve.wait_ge(part1_ok, u + 1)
                        link(v.tensor_tensor(rest, scaled[:, u % 2], parts[:, u % 2, 0, :], ALU.subtract))
                        if u >= 2:
                            dve.wait_ge(stored[u % 2], 48 * (u // 2))
                        link(v.tensor_copy(parts[:, u % 2, 1, :], rest))
                        v.tensor_tensor(parts[:, u % 2, 2, :], rest, parts[:, u % 2, 1, :], ALU.subtract).then_inc(split_ok, 1)
                        u += 1
                        dve.wait_ge(split_ok, u)
                dve.wait_ge(nrm_ok, b + 1)
                if b:
                    dve.wait_ge(nstored, 16 * 12 * b)
                link(v.tensor_copy(nparts[:, 0, :], norms))
                link(v.tensor_tensor(rest, norms, nparts[:, 0, :], ALU.subtract))
                link(v.tensor_copy(nparts[:, 1, :], rest))
                v.tensor_tensor(nparts[:, 2, :], rest, nparts[:, 1, :], ALU.subtract).then_inc(nsplit_ok, 1)
                dve.wait_ge(nsplit_ok, b + 1)
            for b in range(B):
                for j in range(2):
                    o = ("v", b, j)
                    dve.wait_ge(full, step[o] + 1)
                    for hg in range(4):
                        last = v.tensor_tensor(
                            vals[:, 4 * b + hg, 4 * j:4 * j + 4, 0:HG * HD],
                            buf(o).rearrange("p (t e) -> p t e", e=E)[:, :, 64 * hg:64 * hg + 64],
                            g.rows_sb[:, 0:1, 64 * hg:64 * hg + 64].to_broadcast([P, 4, 64]), ALU.add)
                    last.then_inc(val_ok, 1)

        @block.scalar
        def _(act):
            a = nc.scalar.activation
            act.wait_ge(w_c, 48)
            a(small[:, 12:15], col(C_TAU, 3), ACT.Exp).then_inc(etau_ok, 1)
            act.wait_ge(small_ok, 1)
            a(T0[:, 12:16], T0[:, 2:6], ACT.Exp).then_inc(etau_ok, 1)

            def evacuate(o, ok, dst, src, func, **kw):
                act.wait_ge(full, step[o] + 1)
                a(dst, src, func, **kw).then_inc(ok, 1)

            for b in range(B):
                evacuate(("h1", b, 0), h1_ok, h1T[:, bs(b)], buf(("h1", b, 0))[0:HID, :], ACT.Gelu,
                         bias=g.cols_sb[0:HID, C_BN1:C_BN1 + 1])
            for b in range(B):
                for i in range(CT):
                    evacuate(("wg", b, i), wg_ok, wgT[:, i, bs(b)], buf(("wg", b, i)), ACT.Sigmoid, bias=col(C_BG + i))
                for d in range(D):
                    evacuate(("mod", b, d), mod_ok, modT[:, d, bs(b)], buf(("mod", b, d)), ACT.Sigmoid, bias=col(C_BN2 + d))
            for b in range(B):
                for i in range(CT):
                    evacuate(("soma", b, i), soma_ok, somaT[:, i, bs(b)], buf(("soma", b, i)), ACT.Gelu, bias=col(C_BSOMA + i))
            for b in range(B):
                for i in range(CT):
                    act.wait_ge(temp_ok, b + 1)
                    evacuate(("gate", b, i), gate_ok, wgT[:, i, bs(b)], buf(("gate", b, i)), ACT.Sigmoid, bias=col(C_BTEMP + i))
            act.wait_ge(idt, 4)
            for b in range(B):
                for j in range(2):
                    o = ("out", b, j)
                    evacuate(o, cond_ok, cond[:, b * BT + 4 * j:b * BT + 4 * j + 4, :].rearrange("p t e -> p (t e)"),
                             buf(o), ACT.Identity)
                act.wait_ge(var_ok, b + 1)
                a(rstd[:, 0, b * BT:(b + 1) * BT], mv[:, b * BT:(b + 1) * BT, 1], ACT.Sqrt, bias=eps_sb[:, :]).then_inc(std_ok, 1)
            act.wait_ge(coef_ok, 1)
            u = 0
            for b in range(B):
                for kind in "qk":
                    for i in range(CT):
                        o = (kind, b, i)
                        act.wait_ge(full, step[o] + 1)
                        if b:
                            act.wait_ge(full, step[("n", b - 1, 0)] + 1)
                        bias = col((C_BQ if kind == "q" else C_BK) + i)
                        a(squares[:, 2 * (kind == "k") + i], buf(o), ACT.Square, bias=bias).then_inc(sq_ok, 1)
                        if u >= 2:
                            act.wait_ge(split_ok, u - 1)
                            act.wait_ge(stored[u % 2], 48 * (u // 2))
                        if kind == "q":
                            a(scaled[:, u % 2], buf(o), ACT.Identity, bias=BQ2[:, i:i + 1], scale=R2).then_inc(scaled_ok, 1)
                        else:
                            a(scaled[:, u % 2], buf(o), ACT.Identity, bias=bias).then_inc(scaled_ok, 1)
                        u += 1
                        act.wait_ge(scaled_ok, u)
                        a(parts[:, (u - 1) % 2, 0, :], scaled[:, (u - 1) % 2], ACT.Copy).then_inc(part1_ok, 1)
                o = ("n", b, 0)
                if b:
                    act.wait_ge(nsplit_ok, b)
                evacuate(o, nrm_ok, norms, buf(o), ACT.Identity)

        def read_of(o):
            kind, b, i = o
            return {"h1": (h1_ok, b + 1), "soma": (soma_ok, CT * b + i + 1), "wg": (wg_ok, CT * b + i + 1),
                    "mod": (mod_ok, D * b + i + 1), "gate": (gate_ok, CT * b + i + 1), "out": (cond_ok, 2 * b + i + 1),
                    "tr": (hT_ok, CT * b + i + 1), "q": (scaled_ok, 4 * b + i + 1), "k": (scaled_ok, 4 * b + 2 + i + 1),
                    "n": (nrm_ok, b + 1), "v": (val_ok, 2 * b + i + 1)}[kind]

        @block.tensor
        def _(pe):
            def start(o):
                if step[o] >= 4:
                    pe.wait_ge(*read_of(order[step[o] - 4]))

            def product(o, m, lhsT, rhs, ks):
                start(o)
                for half in range(2):
                    hs = slice(512 * half, 512 * half + 512)
                    for k in range(ks):
                        last = nc.tensor.matmul(buf(o)[0:m, hs], lhsT(k), rhs(k, half), start=(k == 0), stop=(k == ks - 1))
                last.then_inc(full, 1)

            def tok(b, half):
                return slice(b * T + 512 * half, b * T + 512 * half + 512)

            def rows_product(o, t0, lhsT, rhs):
                start(o)
                for j in range(4):
                    for k in range(CT):
                        last = nc.tensor.matmul(buf(o)[:, j * E:(j + 1) * E], lhsT(k, t0 + j), rhs(k), start=(k == 0),
                                                stop=(k == CT - 1))
                last.then_inc(full, 1)

            pe.wait_ge(w_a, 48)
            for b in range(B):
                pe.wait_ge(w_x[b], 32)
                product(("h1", b, 0), HID, lambda k: wn1_sb[:, k, :], lambda k, h: xT_sb[:, k, tok(b, h)], CT)
            pe.wait_ge(rep_ok, 1)
            for b in range(B):
                pe.wait_ge(ctx_ok, b + 1)
                for i in range(CT):
                    product(("wg", b, i), P, lambda k: wg_sb[:, k, i * P:(i + 1) * P],
                            lambda k, h: (xT_sb if k < CT else ctxT)[:, k % CT, tok(b, h)], 2 * CT)
                pe.wait_ge(h1_ok, b + 1)
                for d in range(D):
                    product(("mod", b, d), P, lambda k: wn2_rep[:, d, :], lambda k, h: h1T[:, tok(b, h)], 1)
            for b in range(B):
                for i in range(CT):
                    product(("soma", b, i), P, lambda k: wsoma_sb[:, k, i * P:(i + 1) * P],
                            lambda k, h: xT_sb[:, k, tok(b, h)], CT)
            pe.wait_ge(w_q, 64)
            for b in range(B):
                pe.wait_ge(temp_ok, b + 1)
                for i in range(CT):
                    product(("gate", b, i), P, lambda k: wtemp_sb[:, k, i * P:(i + 1) * P],
                            lambda k, h: traces[:, 0, k, tok(b, h)], CT)
            for b in range(B):
                pe.wait_ge(sg_ok, b + 1)
                for j in range(2):
                    rows_product(("out", b, j), b * BT + 4 * j, lambda k, t: somaT[:, k, t * P:(t + 1) * P],
                                 lambda k: wout_sb[:, k, :])
            pe.wait_ge(idt, 3)
            pe.wait_ge(sel_ok, 1)
            for b in range(B):
                pe.wait_ge(ln_ok, b + 1)
                for i in range(CT):
                    o = ("tr", b, i)
                    start(o)
                    for t in range(BT):
                        last = nc.tensor.transpose(buf(o)[:, t * P:(t + 1) * P], cond[:, b * BT + t, i * P:(i + 1) * P],
                                                   ident[:, :])
                    last.then_inc(full, 1)
                pe.wait_ge(hT_ok, CT * (b + 1))
                for c, kind in enumerate("qk"):
                    for i in range(CT):
                        product((kind, b, i), P, lambda k: wqkv_sb[:, k, c * E + i * P:c * E + (i + 1) * P],
                                lambda k, h: hT[:, k, tok(b, h)], CT)
                o = ("n", b, 0)
                start(o)
                pe.wait_ge(sq_ok, 4 * (b + 1))
                for half in range(2):
                    for w in range(4):
                        last = nc.tensor.matmul(buf(o)[32 * w:32 * w + 32, 512 * half:512 * half + 512], head_sel[:, :],
                                                squares[:, w, 512 * half:512 * half + 512], start=True, stop=True)
                last.then_inc(full, 1)
            for b in range(B):
                for j in range(2):
                    rows_product(("v", b, j), b * BT + 4 * j, lambda k, t: hT[:, k, t * P:(t + 1) * P],
                                 lambda k: wqkv_sb[:, k, 2 * E:3 * E])


def block_b(nc, s, sem, sbuf, g):
    qa = [sbuf(s, f"qa{i}", [KQ, HG, T], BF16) for i in range(2)]
    ka = [sbuf(s, f"ka{i}", [KQ, HG, T], BF16) for i in range(2)]
    vg = [sbuf(s, f"vg{i}", [P, BT, VW]) for i in range(2)]
    probs = sbuf(s, "probs", [P, 2, HG, T])
    ost = [sbuf(s, f"ost{i}", [P, T]) for i in range(2)]
    sc = [s.enter_context(nc.psum_tensor(f"scores{i}", [P, T], F32)) for i in range(2)]
    acc = [s.enter_context(nc.psum_tensor(f"acc{i}", [P, T], F32)) for i in range(2)]
    STEPS = BT * HG
    LOADS = 16 * 15
    loaded = [sem(f"group_loaded{i}") for i in range(2)]
    ones_ok = [sem(f"ones_in_place{i}") for i in range(2)]
    scored, exped, pv, evac = sem("scored"), sem("exped"), sem("pv_done"), sem("acc_evacuated")
    ost_out = [sem(f"ost_out{i}") for i in range(2)]
    PV0 = 8
    EV0 = 2

    pid_sb = sbuf(s, "pid_sb", [1, B], I32)
    w_pid = sem("pid_loaded")

    def prefetch(sp):
        sp.dma_start(pid_sb[:, :], g.pid).then_inc(w_pid, 16)
        sp.wait_ge(w_pid, 16)
        for b in range(B):
            prof = sp.value_load(pid_sb[0:1, b:b + 1], min_val=0, max_val=NPROF - 1)
            one = bass.ds(prof, 1)
            sp.dma_start(g.wd[:, b, :, :], g.down_w[one, :, :].rearrange("o (k p) n -> p (o k) n", p=P)).then_inc(g.w_d, 16)
            sp.dma_start(g.bd[:, b:b + 1], g.down_b[one, :].rearrange("o n -> n o")).then_inc(g.w_d, 16)
            sp.dma_start(g.wu[:, b, :], g.up_w[one, :, :].rearrange("o k n -> (o k) n")).then_inc(g.w_d, 16)
            for j, src in enumerate((g.up_b, g.ln_g, g.ln_b)):
                sp.dma_start(g.rowp[:, b, j, :], src[one, :].broadcast_to([P, E])).then_inc(g.w_d, 16)
        sp.dma_start(g.wr[:, :, :], g.Wr.rearrange("(k p) n -> p k n", p=P)).then_inc(g.w_r, 16)
        sp.dma_start(g.xr[:, :, :], g.x.rearrange("(t p) e -> p t e", p=P)).then_inc(g.w_x, 16)
        for i in range(2):
            load_expert(sp, g, i, i)

    with nc.Block() as block:
        @block.gpsimd
        def _(pool):
            pool.wait_ge(g.w_x, 16)
            pool.wait_ge(g.w_d, 16 * 6 * B)
            for c in range(CH):
                ts = slice(c * TC, (c + 1) * TC)
                nc.gpsimd.tensor_tensor(g.xr[:, ts, :], g.xr[:, ts, :], g.rows_sb[:, 1:2, :].to_broadcast([P, TC, E]),
                                        ALU.add).then_inc(g.xb_ok, 1)
            for c in range(CH):
                ts = slice(c * TC, (c + 1) * TC)
                pool.wait_ge(g.xb_ok, c + 1)
                nc.gpsimd.tensor_tensor(g.xbu[:, ts, :], g.xr[:, ts, :],
                                        g.rowp[:, c * TC // BT, 0:1, :].to_broadcast([P, TC, E]), ALU.add).then_inc(g.xb_ok, 1)

        @block.sync
        def _(sp):
            def load(grp, gg, i):
                if gg is None:
                    for dst in (qa[i][96:99], ka[i][99:102]):
                        sp.dma_start(dst, g.ones_bf[:, :].unsqueeze(1).to_broadcast([3, HG, T])).then_inc(ones_ok[i], 16)
                else:
                    sp.wait_ge(pv, grp * STEPS + (PV0 - STEPS))
                rows = lambda d, j: d[j, bass.ds(grp * (HG * HD), HG * HD), :].rearrange("(h d) t -> d h t", d=HD)
                for r, j in enumerate((0, 1, 2, 0, 1, 0)):
                    sp.dma_start(qa[i][r * HD:(r + 1) * HD, :, :], rows(g.q_dram, j)).then_inc(loaded[i], 16)
                for r, j in enumerate((0, 0, 0, 1, 1, 2)):
                    sp.dma_start(ka[i][r * HD:(r + 1) * HD, :, :], rows(g.k_dram, j)).then_inc(loaded[i], 16)
                for kk, dst in ((0, qa[i][99:102]), (1, ka[i][96:99])):
                    sp.dma_start(dst, g.n_dram[:, kk, bass.ds(grp * HG, HG), :]).then_inc(loaded[i], 16)
                sp.dma_start(vg[i][:, :, :], g.vals[:, bass.ds(grp, 1), :, :].rearrange("p o t w -> p (o t) w")).then_inc(loaded[i], 16)

            def store(grp, i):
                sp.wait_ge(evac, EV0 + 1 + grp)
                for h in range(HG):
                    sp.dma_start(g.o_dram[bass.ds(grp * (HG * HD) + h * HD, HD), :], ost[i][32 * h:32 * h + HD, :]).then_inc(ost_out[i], 16)

            load(0, None, 0)
            load(1, None, 1)
            prefetch(sp)
            with sp.Fori(0, NG // 2 - 1) as gg:
                load(gg * 2 + 2, gg + 1, 0)
                store(gg * 2, 0)
                load(gg * 2 + 3, gg + 1, 1)
                store(gg * 2 + 1, 1)
            store(NG - 2, 0)
            store(NG - 1, 1)
            for i in range(2):
                sp.wait_ge(ost_out[i], 64 + 64 * NG // 2)
            for b in range(B):
                for i in range(CT):
                    sp.dma_start(g.oT[:, i, b * T:(b + 1) * T], g.o_dram[b * E + i * P:b * E + (i + 1) * P, :]).then_inc(g.w_o, 16)

        @block.vector
        def _(dve):
            v = nc.vector
            v.memset(ost[0][:, 0:1], 0.0).then_inc(ost_out[0], 64)
            v.memset(ost[1][:, 0:1], 0.0).then_inc(ost_out[1], 64)
            v.memset(ost[0][:, 1:2], 0.0).then_inc(pv, PV0)
            v.memset(ost[1][:, 1:2], 0.0).then_inc(evac, EV0)
            dve.wait_ge(evac, EV0)

            def evacuate(grp, gg, i):
                dve.wait_ge(pv, grp * STEPS + (PV0 + STEPS))
                dve.wait_ge(ost_out[i], gg * 64 + 64)
                v.tensor_copy(ost[i][:, :], acc[i][:, :]).then_inc(evac, 1)

            with dve.Fori(0, NG // 2) as gg:
                evacuate(gg * 2, gg, 0)
                evacuate(gg * 2 + 1, gg, 1)

        @block.scalar
        def _(act):
            with act.Fori(0, NG // 2) as gg:
                for i in range(2):
                    base = gg * (2 * STEPS) + i * STEPS
                    for n in range(STEPS):
                        t, h = n // HG, n % HG
                        act.wait_ge(scored, base + (n + 1))
                        if h == 0:
                            act.wait_ge(pv, base + (PV0 + HG * t - HG))
                        nc.scalar.activation(probs[:, t % 2, h, :], sc[n % 2][:, :], ACT.Exp).then_inc(exped, 1)

        @block.tensor
        def _(pe):
            def scores(i, n):
                t, h = n // HG, n % HG
                for half in range(2):
                    last = nc.tensor.matmul(sc[n % 2][:, 512 * half:512 * half + 512], qa[i][:, h, t * P:(t + 1) * P],
                                            ka[i][:, h, 512 * half:512 * half + 512], start=True, stop=True)
                last.then_inc(scored, 1)

            def values(i, m):
                t, q = m // 4, m % 4
                for h in range(HG):
                    last = nc.tensor.matmul(acc[i][32 * h:32 * h + 32, 256 * q:256 * q + 256],
                                            vg[i][:, t, HD * h:HD * h + 32], probs[:, t % 2, h, 256 * q:256 * q + 256],
                                            start=(t == 0 and q % 2 == 0), stop=(t == BT - 1), skip_group_check=True)
                last.then_inc(pv, 1)

            def group(grp, gg, i, more, next_gg):
                pe.wait_ge(evac, grp + 1)
                for n in range(STEPS):
                    pe.wait_ge(exped, grp * STEPS + (n + 1))
                    if n + 2 < STEPS:
                        scores(i, n + 2)
                    elif more:
                        if n + 2 == STEPS:
                            pe.wait_ge(loaded[1 - i], next_gg * LOADS + LOADS)
                        scores(1 - i, n + 2 - STEPS)
                    if n >= HG - 1:
                        values(i, n - (HG - 1))
                for m in range(STEPS - HG + 1, STEPS):
                    values(i, m)

            for i in range(2):
                pe.wait_ge(ones_ok[i], 32)
            pe.wait_ge(loaded[0], LOADS)
            scores(0, 0)
            scores(0, 1)
            with pe.Fori(0, NG // 2 - 1) as gg:
                group(gg * 2, gg, 0, True, gg)
                group(gg * 2 + 1, gg, 1, True, gg + 1)
            group(NG - 2, None, 0, True, NG // 2 - 1)
            group(NG - 1, None, 1, False, None)


def block_c(nc, s, sem, sbuf, g):
    ident = g.ident
    oT, xr, wd, bd, wu, rowp, wr = g.oT, g.xr, g.wd, g.bd, g.wu, g.rowp, g.wr
    xbu = g.xbu
    outr = sbuf(s, "outr", [P, 2, TC, E])
    x1T = sbuf(s, "x1T", [P, 2, CT, TC * P])
    zT = sbuf(s, "zT", [P, 2, TC * P])
    y = sbuf(s, "y", [P, 2, TC, E])
    xfT = sbuf(s, "xfT", [P, 2, CT, TC * P])
    drow = sbuf(s, "drow", [P, NT, ROW])
    stats = sbuf(s, "stats_c", [P, NT, 6])
    mv = sbuf(s, "mv_c", [P, NT, 2])
    sd = sbuf(s, "sd_c", [P, 2, NT])
    lg = sbuf(s, "lg", [P, NT, NE])
    mx = sbuf(s, "mx", [P, NT, 8])
    ix = sbuf(s, "ix", [P, NT, 8], U32)
    dl = sbuf(s, "dl", [P, NT, NE + 1])
    ex = sbuf(s, "ex", [P, NT, NE + 1])
    zz = sbuf(s, "zz", [P, NT, 2])
    ixf = sbuf(s, "ixf", [P, 2, NT])
    oh = sbuf(s, "oh", [P, 2, NT, NE])
    chosen = sbuf(s, "chosen", [P, NT, NE])
    off = sbuf(s, "off", [P, NT, NE])
    base = sbuf(s, "base", [P, NT + 1, NE])
    tmp = sbuf(s, "tmp", [P, 2, NT, NE])
    offk = sbuf(s, "offk", [P, 2, NT])
    over = sbuf(s, "over", [P, 2, NT])
    slotf = sbuf(s, "slotf", [P, 2, NT])
    sloti = sbuf(s, "sloti", [P, 2, NT], U32)
    iota_e = sbuf(s, "iota_e", [P, NE])
    iota_i = sbuf(s, "iota_i", [P, NE], I32)
    before = sbuf(s, "before", [P, P])
    ones = sbuf(s, "ones", [P, P])
    ps = s.enter_context(nc.psum_tensor("ps_c", [P, 4, T], F32))

    w_d, w_o, w_r = g.w_d, g.w_o, g.w_r
    nm_ok, yn_ok = sem("neg_mean_ok"), sem("y_normed")
    cst, dch = sem("c_constants"), sem("dve_c_chain")
    full = sem("ps_c_full")
    x1_ok, t1_ok, z_ok, y_ok, var_ok, sd_ok, xf_ok, t2_ok, lg_ok, dl_ok, ex_ok, ch_ok, slot_ok, xbu_ok, out_ok, disp, outd, off_ok = (
        sem("x1_ok"), sem("x1T_ok"), sem("z_ok"), sem("y_ok"), sem("var_c_ok"), sem("sd_c_ok"), sem("xf_ok"), sem("xfT_ok"),
        sem("logits_ok"), sem("shifted_ok"), sem("expd_ok"), sem("chosen_ok"), sem("slots_ok"), sem("xbu_ok"), sem("outr_ok"),
        sem("dispatched"), [sem(f"out_started{i}") for i in range(2)], sem("offsets_ok"))

    LAG = {"t2": 2, "t1": 1, "pre": 3, "z": 1, "lg": 2, "y": 1, "proj": 0}
    order = [(st, w - lag) for w in range(CH + 3) for st, lag in LAG.items() if 0 <= w - lag < CH]
    step = {o: i for i, o in enumerate(order)}
    buf = lambda o: ps[:, step[o] % 4]
    tl = lambda c: slice(c * TC, (c + 1) * TC)

    with nc.Block() as block:
        @block.sync
        def _(sp):
            for c in range(CH):
                sp.wait_ge(out_ok, c + 1)
                sp.dma_start(g.out[c * TC * P:(c + 1) * TC * P, :].rearrange("(t p) e -> p t e", p=P),
                             outr[:, c % 2, :, :]).then_inc(outd[c % 2], 16)
            for i in range(2):
                sp.wait_ge(outd[i], 16 * CH // 2)

        @block.gpsimd
        def _(pool):
            p = nc.gpsimd
            p.memset(before[:, :], 1.0).then_inc(cst, 1)
            p.memset(ones[:, :], 1.0)
            p.memset(base[:, 0, :], 0.0).then_inc(cst, 1)
            p.iota(iota_i[:, :], [[1, NE]], base=0, channel_multiplier=0).then_inc(cst, 1)
            for t in range(NT):
                last = p.iota(drow[:, t, E:E + 1].bitcast(I32), [[0, 1]], base=t * P, channel_multiplier=1)
            last.then_inc(cst, 1)
            pool.wait_ge(cst, 4)
            p.tensor_copy(iota_e[:, :], iota_i[:, :]).then_inc(cst, 1)
            p.affine_select(out=before[:, :], in_=before[:, :], compare_op=ALU.is_gt, fill=0.0, base=0,
                            pattern=[[1, P]], channel_multiplier=-1).then_inc(cst, 1)
            for w in range(CH + 3):
                if w < CH:
                    c = w
                    pool.wait_ge(x1_ok, c + 1)
                    if c >= 2:
                        pool.wait_ge(outd[c % 2], 16 * (c // 2))
                    p.tensor_tensor(outr[:, c % 2, :, :], xr[:, tl(c), :], g.rows_sb[:, 2:3, :].to_broadcast([P, TC, E]),
                                    ALU.add).then_inc(out_ok, 1)
                if w >= 3:
                    c = w - 3
                    pool.wait_ge(slot_ok, c + 1)
                    for t in range(c * TC, (c + 1) * TC):
                        for k in range(2):
                            pool.indirect_dma_start(
                                g.slots_dram, bass.IndirectOffsetOnAxis(ap=sloti[:, k, t:t + 1], axis=0),
                                drow[:, t, :], None, bounds_check=NE * CAP - 1, oob_is_err=False).then_inc(disp, 16)
            pool.wait_ge(disp, 16 * 2 * NT)

        @block.vector
        def _(dve):
            chain = [0]

            def link(ins):
                chain[0] += 1
                ins.then_inc(dch, 1)
                dve.wait_ge(dch, chain[0])

            v = nc.vector

            def x1(c):
                dve.wait_ge(full, step["proj", c] + 1)
                dve.wait_ge(g.xb_ok, 2 * CH)
                attn = buf(("proj", c)).rearrange("p (t e) -> p t e", e=E)
                v.tensor_tensor(xr[:, tl(c), :], attn, xr[:, tl(c), :], ALU.add).then_inc(x1_ok, 1)
                v.tensor_tensor(xbu[:, tl(c), :], attn, xbu[:, tl(c), :], ALU.add).then_inc(xbu_ok, 1)

            def norm(c):
                b = c * TC // BT
                dve.wait_ge(full, step["y", c] + 1)
                dve.wait_ge(xbu_ok, c + 1)
                v.tensor_tensor(y[:, c % 2, :, :], buf(("y", c)).rearrange("p (t e) -> p t e", e=E), xbu[:, tl(c), :],
                                ALU.add).then_inc(y_ok, 1)
                dve.wait_ge(y_ok, c + 1)
                for j in range(TC):
                    last = v.bn_stats(stats[:, c * TC + j, :], y[:, c % 2, j, :])
                link(last)
                for j in range(TC):
                    last = v.bn_aggr(mv[:, c * TC + j, :], stats[:, c * TC + j, :])
                last.then_inc(var_ok, 1)
                dve.wait_ge(var_ok, c + 1)
                dve.wait_ge(sd_ok, c + 1)
                link(v.reciprocal(sd[:, 1, tl(c)], sd[:, 0, tl(c)]))
                v.scalar_tensor_tensor(sd[:, 0, tl(c)], mv[:, tl(c), 0], -1.0, sd[:, 1, tl(c)], ALU.mult,
                                       ALU.mult).then_inc(nm_ok, 1)
                dve.wait_ge(yn_ok, TC * (c + 1))
                link(v.tensor_tensor(y[:, c % 2, :, :], y[:, c % 2, :, :], rowp[:, b, 1:2, :].to_broadcast([P, TC, E]), ALU.mult))
                v.tensor_tensor(drow[:, tl(c), 0:E], y[:, c % 2, :, :], rowp[:, b, 2:3, :].to_broadcast([P, TC, E]),
                                ALU.add).then_inc(xf_ok, 1)

            def choose(c):
                ts = tl(c)
                dve.wait_ge(full, step["lg", c] + 1)
                v.tensor_copy(lg[:, ts, :], buf(("lg", c))[:, 0:TC * NE].rearrange("p (t e) -> p t e", e=NE)).then_inc(lg_ok, 1)
                dve.wait_ge(lg_ok, c + 1)
                for t in range(c * TC, (c + 1) * TC):
                    last = v.max(mx[:, t, :], lg[:, t, :])
                link(last)
                v.tensor_tensor(dl[:, ts, 0:NE], lg[:, ts, :], mx[:, ts, 0:1].to_broadcast([P, TC, NE]), ALU.subtract)
                v.tensor_tensor(dl[:, ts, NE:NE + 1], mx[:, ts, 1:2], mx[:, ts, 0:1], ALU.subtract).then_inc(dl_ok, 1)
                for t in range(c * TC, (c + 1) * TC):
                    last = v.max_index(ix[:, t, :], mx[:, t, :], lg[:, t, :])
                link(last)
                for k in range(2):
                    last = v.tensor_copy(ixf[:, k, ts], ix[:, ts, k])
                link(last)
                for k in range(2):
                    last = v.tensor_tensor(oh[:, k, ts, :], ixf[:, k, ts].unsqueeze(2).to_broadcast([P, TC, NE]),
                                           iota_e[:, :].unsqueeze(1).to_broadcast([P, TC, NE]), ALU.is_equal)
                link(last)
                v.tensor_tensor(chosen[:, ts, :], oh[:, 0, ts, :], oh[:, 1, ts, :], ALU.add).then_inc(ch_ok, 1)
                v.tensor_copy(drow[:, ts, E + 3], ixf[:, 0, ts])
                dve.wait_ge(ex_ok, c + 1)
                link(v.tensor_reduce(zz[:, ts, 0], ex[:, ts, 0:NE], AX_X, ALU.add))
                link(v.reciprocal(zz[:, ts, 1], zz[:, ts, 0]))
                v.tensor_copy(drow[:, ts, E + 1], zz[:, ts, 1])
                link(v.tensor_tensor(drow[:, ts, E + 2], ex[:, ts, NE], zz[:, ts, 1], ALU.mult))

            def slots(c):
                ts = tl(c)
                dve.wait_ge(full, step["pre", c] + 1)
                pre = buf(("pre", c))
                for j in range(TC):
                    t = c * TC + j
                    link(v.tensor_tensor(base[:, t + 1, :], pre[:, 512 + NE * j:512 + NE * (j + 1)], base[:, t, :], ALU.add))
                v.tensor_tensor(off[:, ts, :], pre[:, 0:TC * NE].rearrange("p (t e) -> p t e", e=NE),
                                base[:, ts, :], ALU.add).then_inc(off_ok, 1)
                dve.wait_ge(off_ok, c + 1)
                for k in range(2):
                    last = v.tensor_tensor(tmp[:, k, ts, :], off[:, ts, :], oh[:, k, ts, :], ALU.mult)
                link(last)
                link(v.tensor_reduce(offk[:, :, ts], tmp[:, :, ts, :], AX_X, ALU.add))
                v.tensor_scalar(over[:, :, ts], offk[:, :, ts], float(CAP), float(OOB), ALU.is_ge, ALU.mult)
                link(v.scalar_tensor_tensor(slotf[:, :, ts], ixf[:, :, ts], float(CAP), offk[:, :, ts], ALU.mult, ALU.add))
                v.tensor_tensor(sloti[:, :, ts], slotf[:, :, ts], over[:, :, ts], ALU.add).then_inc(slot_ok, 1)

            dve.wait_ge(w_d, 16 * 6 * B)
            dve.wait_ge(cst, 6)
            stages = {"proj": x1, "y": norm, "lg": choose, "pre": slots}
            for st, c in order:
                if st in stages:
                    stages[st](c)

        @block.scalar
        def _(act):
            a = nc.scalar.activation

            def t1(c):
                act.wait_ge(full, step["t1", c] + 1)
                if c >= 2:
                    act.wait_ge(full, step["z", c - 2] + 1)
                a(x1T[:, c % 2, :, :].rearrange("p k t -> p (k t)"), buf(("t1", c)), ACT.Copy).then_inc(t1_ok, 1)

            def z(c):
                b = c * TC // BT
                act.wait_ge(full, step["z", c] + 1)
                if c >= 2:
                    act.wait_ge(full, step["y", c - 2] + 1)
                act.wait_ge(w_d, 16 * 6 * B)
                a(zT[:, c % 2, :], buf(("z", c))[:, 0:TC * P], ACT.Relu, bias=bd[:, b:b + 1]).then_inc(z_ok, 1)

            def root(c):
                act.wait_ge(var_ok, c + 1)
                a(sd[:, 0, tl(c)], mv[:, tl(c), 1], ACT.Sqrt, bias=g.eps_sb[:, :]).then_inc(sd_ok, 1)
                act.wait_ge(nm_ok, c + 1)
                for j in range(TC):
                    t = c * TC + j
                    a(y[:, c % 2, j, :], y[:, c % 2, j, :], ACT.Identity, bias=sd[:, 0, t:t + 1],
                      scale=sd[:, 1, t:t + 1]).then_inc(yn_ok, 1)

            def t2(c):
                act.wait_ge(full, step["t2", c] + 1)
                if c >= 2:
                    act.wait_ge(full, step["lg", c - 2] + 1)
                a(xfT[:, c % 2, :, :].rearrange("p k t -> p (k t)"), buf(("t2", c)), ACT.Copy).then_inc(t2_ok, 1)

            def soft(c):
                act.wait_ge(dl_ok, c + 1)
                a(ex[:, tl(c), :], dl[:, tl(c), :], ACT.Exp).then_inc(ex_ok, 1)

            stages = {"t1": t1, "z": z, "y": root, "t2": t2, "lg": soft}
            for st, c in order:
                if st in stages:
                    stages[st](c)

        read_of = {"proj": x1_ok, "t1": t1_ok, "z": z_ok, "y": y_ok, "t2": t2_ok, "lg": lg_ok, "pre": off_ok}
        extra = {"proj": xbu_ok}

        @block.tensor
        def _(pe):
            def start(o):
                if step[o] >= 4:
                    st, c = order[step[o] - 4]
                    pe.wait_ge(extra.get(st, read_of[st]), c + 1)

            def transposed(c, src):
                for k in range(CT):
                    for j in range(TC):
                        last = nc.tensor.transpose(buf_of[:, (k * TC + j) * P:(k * TC + j + 1) * P], src(j, k), ident[:, :])
                last.then_inc(full, 1)

            pe.wait_ge(w_o, 16 * B * CT)
            pe.wait_ge(w_d, 16 * 6 * B)
            pe.wait_ge(w_r, 16)
            pe.wait_ge(cst, 6)
            for o in order:
                st, c = o
                start(o)
                buf_of = buf(o)
                b = c * TC // BT
                if st == "proj":
                    for j in range(TC):
                        t = c * TC + j
                        for k in range(CT):
                            last = nc.tensor.matmul(buf_of[:, j * E:(j + 1) * E], oT[:, k, t * P:(t + 1) * P],
                                                    g.wproj_sb[:, k, :], start=(k == 0), stop=(k == CT - 1))
                    last.then_inc(full, 1)
                elif st == "t1":
                    pe.wait_ge(x1_ok, c + 1)
                    transposed(c, lambda j, k: xr[:, c * TC + j, k * P:(k + 1) * P])
                elif st == "z":
                    pe.wait_ge(t1_ok, c + 1)
                    for k in range(CT):
                        last = nc.tensor.matmul(buf_of[:, 0:TC * P], wd[:, b, k, :], x1T[:, c % 2, k, :], start=(k == 0),
                                                stop=(k == CT - 1))
                    last.then_inc(full, 1)
                elif st == "y":
                    pe.wait_ge(z_ok, c + 1)
                    for j in range(TC):
                        last = nc.tensor.matmul(buf_of[:, j * E:(j + 1) * E], zT[:, c % 2, j * P:(j + 1) * P], wu[:, b, :],
                                                start=True, stop=True)
                    last.then_inc(full, 1)
                elif st == "t2":
                    pe.wait_ge(xf_ok, c + 1)
                    transposed(c, lambda j, k: drow[:, c * TC + j, k * P:(k + 1) * P])
                elif st == "lg":
                    pe.wait_ge(t2_ok, c + 1)
                    for j in range(TC):
                        for k in range(CT):
                            last = nc.tensor.matmul(buf_of[:, j * NE:(j + 1) * NE], xfT[:, c % 2, k, j * P:(j + 1) * P],
                                                    wr[:, k, :], start=(k == 0), stop=(k == CT - 1))
                    last.then_inc(full, 1)
                else:
                    pe.wait_ge(ch_ok, c + 1)
                    ch = chosen[:, tl(c), :].rearrange("p t e -> p (t e)")
                    nc.tensor.matmul(buf_of[:, 0:TC * NE], before[:, :], ch, start=True, stop=True)
                    nc.tensor.matmul(buf_of[:, 512:512 + TC * NE], ones[:, :], ch, start=True, stop=True).then_inc(full, 1)


def load_expert(sp, g, e, i):
    one = bass.ds(e, 1)
    sp.dma_start(g.raw1[i][:, :, :], g.w1[one, :, :].rearrange("o (k p) f -> p (o k) f", p=P)).then_inc(g.wl[i], 16)
    sp.dma_start(g.raw2[i][:, :, :], g.w2[one, :, :].rearrange("o (k p) n -> p (o k) n", p=P)).then_inc(g.wl[i], 16)


def block_d(nc, s, sem, sbuf, g):
    raw1, raw2 = g.raw1, g.raw2
    w1p = [sbuf(s, f"w1p{i}", [P, 2, CT, FF], F32R) for i in range(2)]
    w2p = [sbuf(s, f"w2p{i}", [P, 2, FT, E], F32R) for i in range(2)]
    xin = [sbuf(s, f"xin{i}", [P, ST, ROW]) for i in range(2)]
    xp = [sbuf(s, f"xp{i}", [P, 2, CT * CAP], F32R) for i in range(2)]
    stage = sbuf(s, "stage", [P, 4, CAP])
    hp = sbuf(s, "hp", [P, 2, FT, CAP], F32R)
    ye = [sbuf(s, f"ye{i}", [P, ST, E]) for i in range(2)]
    wsel = [sbuf(s, f"wsel{i}", [P, 4, ST]) for i in range(2)]
    tok = [sbuf(s, f"tok{i}", [P, ST], U32) for i in range(2)]
    expert = sbuf(s, "expert", [P, 2])
    start_sb = sbuf(s, "start_sb", [P, 4 + NE])
    ps_t = s.enter_context(nc.psum_tensor("ps_t", [P, CT * CAP], F32))
    ps_h = s.enter_context(nc.psum_tensor("ps_h", [P, 4, CAP], F32))
    ps_y = s.enter_context(nc.psum_tensor("ps_y", [P, ST * E], F32))
    xl = [sem(f"slot_rows_loaded{i}") for i in range(2)]
    wl = g.wl
    tr, hid, yp, yc, sel = sem("x_transposed"), sem("hidden_ready"), sem("y_ready"), sem("y_weighted"), sem("weights_selected")
    added, sums, dch = sem("rows_added"), sem("expert_summed"), sem("dve_d_chain")
    gel, hhi, hlo = sem("gelu_done"), sem("hidden_high"), sem("hidden_low")
    whi, wlo, xhi, xlo = sem("weights_high"), sem("weights_low"), sem("x_high"), sem("x_low")
    YP0, YC0, HL0, SUM0 = 4, 2, 4, 2
    K = 5

    def experts(engine, body):
        with engine.Fori(0, NE // 2 - 1) as pair:
            for i in range(2):
                body(pair * 2 + i, i, pair, True)
        for i in range(2):
            body(NE - 2 + i, i, NE // 2 - 1, i == 0)

    with nc.Block() as block:
        @block.sync
        def _(sp):
            def rows(e, i):
                sp.dma_start(xin[i][:, :, :], g.slots_dram[bass.ds(e * CAP, CAP), :].rearrange("(t p) r -> p t r", p=P)).then_inc(xl[i], 16)

            for i in range(2):
                rows(i, i)
            with sp.Fori(0, NE // 2 - 1) as pair:
                for i in range(2):
                    e = pair * 2 + i
                    sp.wait_ge(xlo, e + 1)
                    sp.wait_ge(sel, e + 1)
                    rows(e + 2, i)
                    sp.wait_ge(wlo, e + 1)
                    load_expert(sp, g, e + 2, i)

        @block.gpsimd
        def _(pool):
            nc.gpsimd.memset(start_sb[:, 0:1], 0.0).then_inc(yp, YP0)
            nc.gpsimd.memset(start_sb[:, 1:2], 0.0).then_inc(hlo, HL0)
            nc.gpsimd.memset(start_sb[:, 2:3], 0.0).then_inc(sums, SUM0)
            pool.wait_ge(sums, SUM0)
            nc.gpsimd.memset(start_sb[:, 3:4], 0.0).then_inc(yc, YC0)

            for e in range(NE):
                i = e % 2
                for t in range(ST):
                    pool.wait_ge(yc, 2 * e + t // 2 + YC0 + 1)
                    pool.indirect_dma_start(g.out, bass.IndirectOffsetOnAxis(ap=tok[i][:, t:t + 1], axis=0),
                                            ye[i][:, t, :], None, bounds_check=NROWS - 1, oob_is_err=True,
                                            compute_op=ALU.add).then_inc(added, 16)
                    pool.wait_ge(added, 16 * (ST * e + t + 1))
                nc.gpsimd.memset(start_sb[:, 4 + e:5 + e], 0.0).then_inc(sums, 1)


        @block.vector
        def _(dve):
            v = nc.vector

            def low(e, i, xturn, wturn):
                links = [0]

                def link(ins):
                    links[0] += 1
                    ins.then_inc(dch, 1)
                    dve.wait_ge(dch, e * K + (1 + links[0]))

                dve.wait_ge(xhi, e + 1)
                v.tensor_tensor(xp[i][:, 1, :], ps_t[:, :], xp[i][:, 0, :].bitcast(F32), ALU.subtract).then_inc(xlo, 1)
                dve.wait_ge(whi, e + 1)
                v.tensor_tensor(w1p[i][:, 1, :, :], raw1[i][:, :, :], w1p[i][:, 0, :, :].bitcast(F32), ALU.subtract)
                v.tensor_tensor(w2p[i][:, 1, :, :], raw2[i][:, :, :], w2p[i][:, 0, :, :].bitcast(F32), ALU.subtract).then_inc(wlo, 1)
                dve.wait_ge(xl[i], xturn)
                dve.wait_ge(sums, e + (SUM0 - 1))
                v.tensor_copy(tok[i][:, :], xin[i][:, :, E].bitcast(U32))
                link(v.tensor_scalar(wsel[i][:, 0, :], xin[i][:, :, E + 3], expert[:, 0:1], None, ALU.is_equal))
                v.tensor_scalar(expert[:, 0:1], expert[:, 0:1], 1.0, None, ALU.add)
                link(v.tensor_tensor(wsel[i][:, 1, :], wsel[i][:, 0, :], xin[i][:, :, E + 1], ALU.mult))
                link(v.tensor_scalar(wsel[i][:, 2, :], wsel[i][:, 0, :], -1.0, 1.0, ALU.mult, ALU.add))
                link(v.tensor_tensor(wsel[i][:, 2, :], wsel[i][:, 2, :], xin[i][:, :, E + 2], ALU.mult))
                link(v.tensor_tensor(wsel[i][:, 3, :], wsel[i][:, 1, :], wsel[i][:, 2, :], ALU.add))
                assert links[0] == K
                v.tensor_copy(wsel[i][:, 0, :], wsel[i][:, 3, :]).then_inc(sel, 1)

            def one(e, i, pair, more):
                for f in range(FT):
                    dve.wait_ge(hhi, e * FT + (f + 1))
                    v.tensor_tensor(hp[:, 1, f, :], stage[:, f % 4, :], hp[:, 0, f, :].bitcast(F32),
                                    ALU.subtract).then_inc(hlo, 1)
                if more:
                    n = (pair + (1 if i else 0)) * 16 + 16
                    low(e + 1, 1 - i, n, n)
                dve.wait_ge(sel, e + 1)
                for h in range(2):
                    dve.wait_ge(yp, e * 2 + (YP0 + 1 + h))
                    for t in (2 * h, 2 * h + 1):
                        last = v.tensor_scalar(ye[i][:, t, :], ps_y[:, t * E:(t + 1) * E], wsel[i][:, 0, t:t + 1], None, ALU.mult)
                    last.then_inc(yc, 1)

            v.memset(expert[:, 0:1], 0.0).then_inc(dch, 1)
            dve.wait_ge(dch, 1)
            low(0, 0, 16, 32)
            experts(dve, one)

        @block.scalar
        def _(act):
            a = nc.scalar.activation

            def high(e, i, wturn):
                act.wait_ge(tr, e + 1)
                act.wait_ge(yp, e * 2 + (YP0 - 2))
                a(xp[i][:, 0, :], ps_t[:, :], ACT.Copy).then_inc(xhi, 1)
                act.wait_ge(wl[i], wturn)
                a(w1p[i][:, 0, :, :], raw1[i][:, :, :], ACT.Copy)
                a(w2p[i][:, 0, :, :], raw2[i][:, :, :], ACT.Copy).then_inc(whi, 1)

            def one(e, i, pair, more):
                for f in range(FT):
                    act.wait_ge(hid, e * FT + (f + 1))
                    act.wait_ge(hlo, e * FT + (f + 1 + HL0 - 4))
                    a(stage[:, f % 4, :], ps_h[:, f % 4, :], ACT.Gelu_apprx_tanh).then_inc(gel, 1)
                    act.wait_ge(gel, e * FT + (f + 1))
                    a(hp[:, 0, f, :], stage[:, f % 4, :], ACT.Copy).then_inc(hhi, 1)
                if more:
                    high(e + 1, 1 - i, (pair + (1 if i else 0)) * 32 + 32)

            high(0, 0, 32)
            experts(act, one)

        @block.tensor
        def _(pe):
            terms = ((0, 0), (0, 1), (1, 0))

            def turn(e, i, xturn):
                pe.wait_ge(xl[i], xturn)
                for k in range(CT):
                    for t in range(ST):
                        last = nc.tensor.transpose(ps_t[:, k * CAP + t * P:k * CAP + (t + 1) * P],
                                                   xin[i][:, t, k * P:(k + 1) * P], g.ident[:, :])
                last.then_inc(tr, 1)

            def one(e, i, pair, more):
                pe.wait_ge(xlo, e + 1)
                pe.wait_ge(wlo, e + 1)
                for f in range(FT):
                    if f < 4:
                        pe.wait_ge(hlo, e * FT + (f + 1 + HL0 - 4))
                    else:
                        pe.wait_ge(gel, e * FT + (f - 3))
                    n = 0
                    for k in range(CT):
                        for u, w in terms:
                            last = nc.tensor.matmul(ps_h[:, f % 4, :], w1p[i][:, u, k, f * P:(f + 1) * P],
                                                    xp[i][:, w, k * CAP:(k + 1) * CAP], start=(n == 0), stop=(n == 3 * CT - 1))
                            n += 1
                    last.then_inc(hid, 1)
                if more:
                    turn(e + 1, 1 - i, (pair + (1 if i else 0)) * 16 + 16)
                pe.wait_ge(hlo, e * FT + (FT + HL0))
                for t in range(ST):
                    if t % 2 == 0:
                        pe.wait_ge(yc, e * 2 + (YC0 - 1 + t // 2))
                    n = 0
                    for f in range(FT):
                        for u, w in terms:
                            last = nc.tensor.matmul(ps_y[:, t * E:(t + 1) * E], hp[:, u, f, t * P:(t + 1) * P],
                                                    w2p[i][:, w, f, :], start=(n == 0), stop=(n == 3 * FT - 1))
                            n += 1
                    if t % 2:
                        last.then_inc(yp, 1)

            turn(0, 0, 16)
            experts(pe, one)


def kernel(**inputs):
    import numpy as np
    import concourse.bacc as bacc
    from concourse.bass_utils import run_bass_kernel_spmd

    a = {k: np.asarray(v) for k, v in inputs.items()}
    f = lambda n: a["L0_" + n]
    tile = lambda v: v.reshape(-1, P).T
    every = lambda v: np.broadcast_to(v.reshape(1, -1), (P, v.size))
    bqkv = f("attn_bqkv")
    cols = np.concatenate([
        tile(f("cond_bg")), tile(f("cond_bsoma")), tile(f("cond_btemp")), tile(f("cond_gamma")), tile(f("cond_beta")),
        tile(bqkv[0:E]), tile(bqkv[E:2 * E]), tile(a["cond_1024"].reshape(-1)),
        np.pad(f("cond_bn1"), (0, P - HID)).reshape(P, 1), every(f("cond_tau_ctx")), every(a["condB_tauraws"]),
        every(a["condB_bn2"]), every(f("attn_r_sigma"))], axis=1)
    rows = np.stack([bqkv[2 * E:], f("attn_bproj"), f("ffn_bias").reshape(-1)])
    x = a["x"].reshape(N, E)
    arrays = {
        "x": x, "xT": x.T, "cols": cols, "rows": rows, "pid": a["itok_B_0_6"].reshape(1, B),
        "WgT": f("cond_Wg").T, "Wn1T": f("cond_Wn1").T, "Wn2T": a["cond_256"].T, "WsomaT": f("cond_Wsoma").T,
        "WtempT": f("cond_Wtemp").T, "WoutT": f("cond_Wout").T, "Wqkv": f("attn_Wqkv"), "Wproj": f("attn_Wproj"),
        "down_w": f("cond2_down_w"), "down_b": f("cond2_down_b"), "up_w": f("cond2_up_w"), "up_b": f("cond2_up_b"),
        "ln_g": f("cond2_ln_g"), "ln_b": f("cond2_ln_b"), "Wr": f("ffn_w_router"), "w1": f("ffn_w1"), "w2": f("ffn_w2")}
    arrays = {k: np.ascontiguousarray(v) for k, v in arrays.items()}
    nc = bacc.Bacc("TRN2", target_bir_lowering=False, num_devices=1)
    aps = {k: nc.dram_tensor(f"in_{k}", v.shape, mybir.dt.from_np(v.dtype), kind="ExternalInput").ap() for k, v in arrays.items()}
    out = nc.dram_tensor("out_rows", (NROWS, E), F32, kind="ExternalOutput").ap()
    aps["out"] = out
    build(nc, aps)
    r = run_bass_kernel_spmd(nc, [{f"in_{k}": v for k, v in arrays.items()}], core_ids=[0])
    return r.results[0]["out_rows"][:N].reshape(B, T, E)
```

```python
from contextlib import ExitStack

import concourse.bass as bass
from concourse import mybir

F32 = mybir.dt.float32
F32R = mybir.dt.float32r
BF16 = mybir.dt.bfloat16
I32 = mybir.dt.int32
U32 = mybir.dt.uint32
ALU = mybir.AluOpType
ACT = mybir.ActivationFunctionType
AX_X = mybir.AxisListType.X

P = 128
B, T, E = 2, 1024, 256
N = B * T
CT = E // P
NT = N // P
BT = T // P
H, HD = 16, 16
HG = 4
NG = B * H // HG
HID = E // 4
D = 2
VW = HG * HD + HD
KQ = 6 * HD + 6
BOT = 128
NPROF = 8
NE, FF = 8, 1024
FT = FF // P
EV0 = 2
CAP = 2 * N // NE
ST = CAP // P
CH = 4
ACT_TILES = 2
TC = NT // CH
ROW = E + 4
EPS = 1e-5
OOB = 8192
NROWS = N + P

C_BG, C_BSOMA, C_BTEMP, C_GAMMA, C_BETA, C_BQ, C_BK, C_BLEND, C_BN1, C_TAU, C_BN2, C_R = (
    0, 2, 4, 6, 8, 10, 12, 14, 18, 19, 22, 24)
NCOLS = 25


class Shared:

    def __init__(self, arrays):
        self.x = arrays["x"]
        self.xT = arrays["xT"]
        self.cols = arrays["cols"]
        self.rows = arrays["rows"]
        self.pid = arrays["pid"]
        self.WgT = arrays["WgT"]
        self.Wn1T = arrays["Wn1T"]
        self.Wn2T = arrays["Wn2T"]
        self.WsomaT = arrays["WsomaT"]
        self.WtempT = arrays["WtempT"]
        self.WoutT = arrays["WoutT"]
        self.Wqkv = arrays["Wqkv"]
        self.Wproj = arrays["Wproj"]
        self.down_w = arrays["down_w"]
        self.down_b = arrays["down_b"]
        self.up_w = arrays["up_w"]
        self.up_b = arrays["up_b"]
        self.ln_g = arrays["ln_g"]
        self.ln_b = arrays["ln_b"]
        self.Wr = arrays["Wr"]
        self.w1 = arrays["w1"]
        self.w2 = arrays["w2"]
        self.out = arrays["out"]


def build(nc, arrays):
    q_dram = nc.dram_tensor("q_parts", (3, B * E, T), BF16, kind="Internal").ap()
    k_dram = nc.dram_tensor("k_parts", (3, B * E, T), BF16, kind="Internal").ap()
    n_dram = nc.dram_tensor("norm_parts", (3, 2, B * H, T), BF16, kind="Internal").ap()
    slots_dram = nc.dram_tensor("slot_rows", (NE * CAP, ROW), F32, kind="Internal").ap()

    top = ExitStack()

    def sem(name):
        return top.enter_context(nc.semaphore(name))

    def sbuf(stack, name, shape, dt=F32):
        return stack.enter_context(nc.sbuf_tensor(name, shape, dt))

    def right_side(stack, name, shape, dt=F32):
        return stack.enter_context(nc.sbuf_tensor(name, shape, dt, side="right"))

    with top:
        ident = sbuf(top, "ident", [P, P])
        cols_sb = sbuf(top, "cols_sb", [P, NCOLS])
        rows_sb = sbuf(top, "rows_sb", [P, 3, E])
        wproj_sb = sbuf(top, "wproj_sb", [P, CT, E])
        until_c = ExitStack()
        early = right_side(until_c, "group0_operands", [P, 2, HG, T], BF16)
        vals = right_side(until_c, "vals", [P, NG, BT, VW])
        ones_bf = sbuf(top, "ones_bf", [3, T], BF16)
        fill = sbuf(top, "fill", [P, ROW])
        xin0 = sbuf(top, "xin0", [P, ST, ROW])
        g = Shared(arrays)
        g.xin0 = xin0
        g.nparts = right_side(until_c, "nparts", [P, 3, T], BF16)
        g.nstored = sem("norms_stored")
        g.vg0 = right_side(until_c, "vg0", [P, BT, VW])
        g.ones_bf, g.fill = ones_bf, fill
        g.qa0, g.ka0 = early[0:KQ, 0], early[0:KQ, 1]
        g.loaded = [sem(f"group_loaded{i}") for i in range(2)]
        g.ones_ok = [sem(f"ones_in_place{i}") for i in range(2)]
        g.q_dram, g.k_dram, g.n_dram, g.slots_dram = q_dram, k_dram, n_dram, slots_dram
        g.ident, g.cols_sb, g.rows_sb, g.wproj_sb, g.vals = ident, cols_sb, rows_sb, wproj_sb, vals
        g.xl = [sem(f"slot_rows_loaded{i}") for i in range(2)]
        g.whi, g.wlo = sem("weights_high"), sem("weights_low")
        with ExitStack() as s:
            block_a(nc, s, sem, sbuf, g)
        g.raw1 = [sbuf(top, f"raw1_{i}", [P, CT, FF]) for i in range(2)]
        g.raw2 = [sbuf(top, f"raw2_{i}", [P, FT, E]) for i in range(2)]
        g.wl = [sem(f"expert_weights_loaded{i}") for i in range(2)]
        with ExitStack() as shared:
            g.ost = [sbuf(shared, f"ost{i}", [P, T]) for i in range(2)]
            g.evac, g.ost_out = sem("acc_evacuated"), [sem(f"ost_out{i}") for i in range(2)]
            g.oT = sbuf(shared, "oT", [P, B * CT, T])
            g.xr = sbuf(shared, "xr", [P, NT, E])
            g.xb_ok = sem("x_plus_bias_ok")
            g.wd = sbuf(shared, "wd", [P, B, CT, BOT])
            g.bd = sbuf(shared, "bd", [P, B])
            g.wu = sbuf(shared, "wu", [P, B, E])
            g.xbu = sbuf(shared, "xbu", [P, NT, E])
            g.rowp = sbuf(shared, "rowp", [P, B, 3, E])
            g.colp = sbuf(shared, "colp", [P, B, 2, CT])
            g.wr = sbuf(shared, "wr", [P, CT, NE])
            g.w_d, g.w_x, g.w_r = sem("adapter_loaded"), sem("x_rows_loaded"), sem("router_loaded")
            with ExitStack() as s:
                block_b(nc, s, sem, sbuf, g)
            until_c.close()
            g.w1p0 = right_side(top, "w1p0", [P, 2, CT, FF], F32R)
            g.w2p0 = right_side(top, "w2p0", [P, 2, FT, E], F32R)
            with ExitStack() as s:
                block_c(nc, s, sem, sbuf, g)
        with ExitStack() as s:
            block_d(nc, s, sem, sbuf, g)


def inverse_root(v, link, out, variance, var, half, seed):
    link(v.tensor_scalar(var, variance, EPS, None, ALU.add))
    link(v.tensor_scalar(seed, var.bitcast(I32), 1, None, ALU.arith_shift_right))
    link(v.tensor_scalar(out.bitcast(I32), seed, -1.0, float(0x5F3759DF), ALU.mult, ALU.add))
    for _ in range(3):
        link(v.scalar_tensor_tensor(half, out, -0.5, out, ALU.mult, ALU.mult))
        link(v.tensor_tensor(half, half, var, ALU.mult))
        link(v.scalar_tensor_tensor(out, half, 1.5, out, ALU.add, ALU.mult))


def block_a(nc, s, sem, sbuf, g):
    ident, vals = g.ident, g.vals
    col = lambda c, n=1: g.cols_sb[:, c:c + n]
    wg_sb = sbuf(s, "wg_sb", [P, 2 * CT, E])
    wn1_sb = sbuf(s, "wn1_sb", [P, CT, HID])
    wn2_sb = sbuf(s, "wn2_sb", [2 * HID, D])
    wn2_rep = sbuf(s, "wn2_rep", [2 * HID, D, P])
    wsoma_sb = sbuf(s, "wsoma_sb", [P, CT, E])
    wtemp_sb = sbuf(s, "wtemp_sb", [P, CT, E])
    wout_sb = sbuf(s, "wout_sb", [P, CT, E])
    wqkv_sb = sbuf(s, "wqkv_sb", [P, CT, 3 * E])
    small = sbuf(s, "small", [P, 40])
    head_sel = sbuf(s, "head_sel", [P, 32])
    xT_sb = sbuf(s, "xT_sb", [P, CT, N])
    somaT = sbuf(s, "somaT", [P, CT, N])
    wgT = sbuf(s, "wgT", [P, CT, N])
    modT = sbuf(s, "modT", [P, D, N])
    ctxT = sbuf(s, "ctxT", [P, CT, N])
    traces = sbuf(s, "traces", [P, D, CT, N])
    h1T = sbuf(s, "h1T", [2 * HID, B, T // 2])
    dead = [t[:, :, :].rearrange("p c n -> p (c n)").bitcast(BF16) for t in (xT_sb, somaT)]
    parts_of = lambda u: dead[u % 4 // 2][:, u % 2 * 3 * T:(u % 2 * 3 + 3) * T].rearrange("p (j t) -> p j t", t=T)
    part_of = lambda u, j: parts_of(u)[:, j]
    nparts, nstored = g.nparts, g.nstored
    stats = sbuf(s, "stats", [P, NT, 6])
    mv = sbuf(s, "mv", [P, NT, 2])
    rstd = sbuf(s, "rstd", [P, 2, NT])
    variance = sbuf(s, "variance", [P, NT])
    root_seed = sbuf(s, "root_seed", [P, NT], I32)
    cond = ctxT[:, :, :].rearrange("p c n -> p (c n)").rearrange("p (t e) -> p t e", e=E)
    hT = modT
    work = traces[:, :, :, :].rearrange("p d c n -> p (d c n)").rearrange("p (k t) -> p k t", t=T)
    squares, scaled, rest, norms = work[:, 0:4], work[:, 4:6], work[:, 6], work[:, 7]
    ps = s.enter_context(nc.psum_tensor("ps_a", [P, 4, T], F32))

    ALPHA, BW, R2, BQ2, T0 = small[:, 0:3], small[:, 4:8], small[:, 8:9], small[:, 10:12], small[:, 16:32]
    NEGR = small[:, 9:10]

    w_x, w_c, w_q = [sem(f"x_loaded{b}") for b in range(B)], sem("cols_loaded"), sem("late_weights_loaded")
    w_n, w_s, w_g = sem("wn1_loaded"), sem("wsoma_loaded"), sem("wg_loaded")
    idt, dch = sem("ident_built"), sem("dve_a_chain")
    full = sem("ps_a_full")
    h1_ok, soma_ok, wg_ok, mod_ok, gate_ok = sem("h1_ok"), sem("soma_ok"), sem("wg_ok"), sem("mod_ok"), sem("gate_ok")
    ctx_ok, temp_ok, sg_ok, cond_ok, ln_ok, hT_ok = (
        sem("ctx_ok"), sem("temp_ok"), sem("sg_ok"), sem("cond_ok"), sem("ln_ok"), sem("hT_ok"))
    etau_ok, rep_ok, sel_ok, coef_ok = sem("tau_exp_ok"), sem("wn2_rep_ok"), sem("head_sel_ok"), sem("coef_ok")
    sq_ok, scaled_ok, part1_ok, split_ok, nrm_ok, nsplit_ok, val_ok = (
        sem("squares_ok"), sem("scaled_ok"), sem("part1_ok"), sem("split_ok"), sem("norms_ok"), sem("norms_split"),
        sem("values_ok"))
    stored = [sem(f"parts_stored{i}") for i in range(4)]
    small_ok, filled, fill_out = sem("blend_shift_ok"), sem("fill_ready"), sem("fill_out")

    both = lambda kind, b: [(kind, b, 0), (kind, b, 1)]
    order = ([("h1", 0, 0)] + both("soma", 0) + both("wg", 0) + both("mod", 0)
             + [("h1", 1, 0)] + both("wg", 1) + both("mod", 1) + both("gate", 0) + both("soma", 1) + both("out", 0)
             + both("gate", 1) + both("tr", 0) + both("out", 1) + both("q", 0) + both("v", 0) + both("k", 0)
             + both("tr", 1) + [("n", 0, 0)] + both("q", 1) + both("k", 1) + [("v", 1, 0), ("n", 1, 0), ("v", 1, 1)])
    step = {o: i for i, o in enumerate(order)}
    buf = lambda o: ps[:, step[o] % 4]
    bs = lambda b: slice(b * T, (b + 1) * T)

    with nc.Block() as block:
        @block.sync
        def _(sp):
            def load_x(b):
                for i in range(CT):
                    sp.dma_start(xT_sb[:, i, bs(b)], g.xT[i * P:(i + 1) * P, bs(b)]).then_inc(w_x[b], 16)

            def load_weights(dst, src, loaded):
                sp.dma_start(dst[:, :, :], src.rearrange("(k p) n -> p k n", p=P)).then_inc(loaded, 16)

            load_weights(wn1_sb, g.Wn1T, w_n)
            load_x(0)
            load_weights(wsoma_sb, g.WsomaT, w_s)
            load_weights(wg_sb, g.WgT, w_g)
            load_x(1)
            for dst, src in ((wtemp_sb, g.WtempT), (wout_sb, g.WoutT), (wqkv_sb, g.Wqkv), (g.wproj_sb, g.Wproj)):
                load_weights(dst, src, w_q)
            for u, (b, kind, i) in enumerate((b, kind, i) for b in range(B) for kind in "qk" for i in range(CT)):
                dst = g.q_dram if kind == "q" else g.k_dram
                sp.wait_ge(split_ok, u + 1)
                sp.dma_start(dst[:, b * E + i * P:b * E + (i + 1) * P, :].rearrange("j p t -> p j t"),
                             parts_of(u)).then_inc(stored[u % 4], 16)
                if u % 4 == 3:
                    sp.wait_ge(nsplit_ok, b + 1)
                    for w in range(4):
                        kk, ii = w // 2, w % 2
                        sp.dma_start(g.n_dram[:, kk, b * H + 8 * ii:b * H + 8 * ii + 8, :].rearrange("j h t -> h j t"),
                                     nparts[32 * w:32 * w + 8, :, :]).then_inc(nstored, 16)
                if u == 4:
                    sp.wait_ge(filled, 1)
                    place_ones(sp, g, 0, g.qa0, g.ka0)
                    for i in range(4):
                        sp.wait_ge(stored[i], 16)
                    sp.wait_ge(nstored, 16 * 4)
                    load_operands(sp, g, 0, g.qa0, g.ka0, g.loaded[0])
                    sp.wait_ge(val_ok, 2)
                    load_values(sp, g, 0, g.vg0[:, :, :], g.loaded[0])
            for i in range(4):
                sp.wait_ge(stored[i], 16 * B)

        @block.gpsimd
        def _(pool):
            pool.dma_start(g.cols_sb[:, :], g.cols).then_inc(w_c, 16)
            for half in range(2):
                pool.dma_start(wn2_sb[half * HID:(half + 1) * HID, :], g.Wn2T).then_inc(w_c, 16)
            pool.dma_start(g.rows_sb[:, :, :],
                           g.rows.rearrange("(o r) e -> o r e", o=1).broadcast_to([P, 3, E])).then_inc(w_c, 16)
            nc.gpsimd.memset(ident[:, :], 0.0).then_inc(idt, 1)
            nc.gpsimd.memset(vals[:, :, :, :], 0.0).then_inc(idt, 1)
            pool.wait_ge(idt, 1)
            nc.gpsimd.affine_select(out=ident[:, :], in_=ident[:, :], compare_op=ALU.not_equal, fill=1.0, base=0,
                                    pattern=[[-1, P]], channel_multiplier=1).then_inc(idt, 1)
            nc.gpsimd.memset(g.ones_bf[:, :], 1.0).then_inc(filled, 1)
            nc.gpsimd.memset(g.fill[:, :], 0.0).then_inc(filled, 1)
            pool.wait_ge(filled, 2)
            nc.gpsimd.iota(g.fill[:, E:E + 1].bitcast(I32), [[0, 1]], base=N, channel_multiplier=1).then_inc(filled, 1)
            pool.wait_ge(filled, 3)
            pool.wait_ge(wg_ok, 1)
            for c in range(NE * CAP // P):
                pool.dma_start(g.slots_dram[c * P:(c + 1) * P, :], g.fill[:, :]).then_inc(fill_out, 16)
            pool.dma_start(g.out[N:NROWS, :], g.fill[:, 0:E]).then_inc(fill_out, 16)
            pool.wait_ge(fill_out, 16 * (NE * CAP // P + 1))

        @block.vector
        def _(dve):
            chain = [0]

            def link(ins):
                chain[0] += 1
                ins.then_inc(dch, 1)
                dve.wait_ge(dch, chain[0])

            v = nc.vector
            dve.wait_ge(w_c, 64)
            link(v.tensor_tensor(T0[:, 0:2], col(C_BLEND, 2), col(C_BLEND + 2, 2), ALU.max))
            for d in range(D):
                last = v.tensor_tensor(T0[:, 2 + 2 * d:4 + 2 * d], col(C_BLEND + 2 * d, 2), T0[:, 0:2], ALU.subtract)
            last.then_inc(small_ok, 1)
            link(v.tensor_scalar(NEGR, col(C_R), -1.0, None, ALU.mult))
            dve.wait_ge(idt, 3)
            link(v.memset(head_sel[:, :], 0.0))
            link(v.tensor_reduce(head_sel[:, 0:8], ident[:, :].rearrange("p (h d) -> p h d", d=HD), AX_X, ALU.add))
            v.tensor_scalar(head_sel[:, 0:8], head_sel[:, 0:8], NEGR, None, ALU.mult).then_inc(sel_ok, 1)
            for d in range(D):
                last = v.tensor_copy(wn2_rep[:, d, :], wn2_sb[:, d:d + 1].to_broadcast([2 * HID, P]))
            last.then_inc(rep_ok, 1)
            link(v.tensor_scalar(R2, col(C_R), 2.0, None, ALU.mult))
            v.tensor_scalar(BQ2, col(C_BQ, 2), R2, None, ALU.mult).then_inc(coef_ok, 1)
            dve.wait_ge(etau_ok, 2)
            link(v.tensor_scalar(T0[:, 6:9], small[:, 12:15], 1.0, None, ALU.add))
            link(v.reciprocal(ALPHA, T0[:, 6:9]))
            link(v.tensor_tensor(T0[:, 10:12], T0[:, 12:14], T0[:, 14:16], ALU.add))
            link(v.reciprocal(T0[:, 10:12], T0[:, 10:12]))
            for d in range(D):
                last = v.tensor_tensor(BW[:, 2 * d:2 * d + 2], T0[:, 12 + 2 * d:14 + 2 * d], T0[:, 10:12], ALU.mult)
            link(last)
            def context(b):
                dve.wait_ge(w_x[b], 32)
                for i in range(CT):
                    last = v.tensor_tensor_scan(ctxT[:, i, bs(b)], small[:, 0:1].to_broadcast([P, T]),
                                                xT_sb[:, i, bs(b)], 0.0, ALU.mult, ALU.add)
                last.then_inc(ctx_ok, 1)
            def gated(b):
                dve.wait_ge(gate_ok, CT * (b + 1))
                dve.wait_ge(soma_ok, CT * (b + 1))
                v.tensor_tensor(somaT[:, :, bs(b)], somaT[:, :, bs(b)], wgT[:, :, bs(b)], ALU.mult).then_inc(sg_ok, 1)
            def blended(b):
                dve.wait_ge(wg_ok, CT * (b + 1))
                link(v.tensor_tensor(wgT[:, :, bs(b)], wgT[:, :, bs(b)], xT_sb[:, :, bs(b)], ALU.mult))
                dve.wait_ge(mod_ok, D * (b + 1))
                for d in range(D):
                    for i in range(CT):
                        last = v.scalar_tensor_tensor(traces[:, d, i, bs(b)], modT[:, d, bs(b)], 0.5, wgT[:, i, bs(b)],
                                                      ALU.add, ALU.mult)
                link(last)
                for d in range(D):
                    if (b, d) == (1, 0):
                        gated(0)
                    for i in range(CT):
                        last = v.tensor_tensor_scan(traces[:, d, i, bs(b)], small[:, 1 + d:2 + d].to_broadcast([P, T]),
                                                    traces[:, d, i, bs(b)], 0.0, ALU.mult, ALU.add)
                link(last)
                for i in range(CT):
                    last = v.tensor_scalar(traces[:, 0, i, bs(b)], traces[:, 0, i, bs(b)], BW[:, i:i + 1], None, ALU.mult)
                link(last)
                for i in range(CT):
                    last = v.scalar_tensor_tensor(traces[:, 0, i, bs(b)], traces[:, 1, i, bs(b)], BW[:, 2 + i:3 + i],
                                                  traces[:, 0, i, bs(b)], ALU.mult, ALU.add)
                last.then_inc(temp_ok, 1)
            def normed(b):
                tiles = range(b * BT, (b + 1) * BT)
                dve.wait_ge(cond_ok, 2 * (b + 1))
                for t in tiles:
                    last = v.bn_stats(stats[:, t, :], cond[:, t, :])
                link(last)
                for t in tiles:
                    last = v.bn_aggr(mv[:, t, :], stats[:, t, :])
                link(last)
                bt = slice(b * BT, (b + 1) * BT)
                inverse_root(v, link, rstd[:, 1, bt], mv[:, bt, 1], variance[:, bt], rstd[:, 0, bt], root_seed[:, bt])
                for t in tiles:
                    last = v.tensor_scalar(cond[:, t, :], cond[:, t, :], mv[:, t, 0:1], rstd[:, 1, t:t + 1],
                                           ALU.subtract, ALU.mult)
                last.then_inc(ln_ok, 1)

            context(0)
            context(1)
            blended(0)
            blended(1)
            normed(0)
            gated(1)
            normed(1)
            def split(u):
                dve.wait_ge(part1_ok, u + 1)
                link(v.tensor_tensor(rest, scaled[:, u % 2], part_of(u, 0), ALU.subtract))
                if u >= 4:
                    dve.wait_ge(stored[u % 4], 16 * (u // 4))
                link(v.tensor_copy(part_of(u, 1), rest))
                v.tensor_tensor(part_of(u, 2), rest, part_of(u, 1), ALU.subtract).then_inc(split_ok, 1)
                dve.wait_ge(split_ok, u + 1)

            def split_norms(b):
                dve.wait_ge(nrm_ok, 2 * (b + 1))
                if b:
                    dve.wait_ge(nstored, 16 * 4 * b)
                link(v.tensor_tensor(rest, norms, nparts[:, 0, :], ALU.subtract))
                link(v.tensor_copy(nparts[:, 1, :], rest))
                v.tensor_tensor(nparts[:, 2, :], rest, nparts[:, 1, :], ALU.subtract).then_inc(nsplit_ok, 1)
                dve.wait_ge(nsplit_ok, b + 1)

            def values(b, j):
                o = ("v", b, j)
                dve.wait_ge(full, step[o] + 1)
                for hg in range(4):
                    last = v.tensor_tensor(
                        vals[:, 4 * b + hg, 4 * j:4 * j + 4, 0:HG * HD],
                        buf(o).rearrange("p (t e) -> p t e", e=E)[:, :, 64 * hg:64 * hg + 64],
                        g.rows_sb[:, 0:1, 64 * hg:64 * hg + 64].to_broadcast([P, 4, 64]), ALU.add)
                last.then_inc(val_ok, 1)

            for kind, b, i in order:
                if kind in "qk":
                    split((b * 2 + (kind == "k")) * CT + i)
                elif kind == "n":
                    split_norms(b)
                elif kind == "v":
                    values(b, i)

        @block.scalar
        def _(act):
            a = nc.scalar.activation
            act.wait_ge(w_c, 64)
            a(small[:, 12:15], col(C_TAU, 3), ACT.Exp).then_inc(etau_ok, 1)
            act.wait_ge(small_ok, 1)
            a(T0[:, 12:16], T0[:, 2:6], ACT.Exp).then_inc(etau_ok, 1)

            def evacuate(o, ok, dst, src, func, **kw):
                act.wait_ge(full, step[o] + 1)
                a(dst, src, func, **kw).then_inc(ok, 1)

            def queries_or_keys(kind, b, i):
                u = (b * 2 + (kind == "k")) * CT + i
                act.wait_ge(full, step[kind, b, i] + 1)
                if b:
                    act.wait_ge(full, step["n", b - 1, 0] + 1)
                bias = col((C_BQ if kind == "q" else C_BK) + i)
                src = buf((kind, b, i))
                a(squares[:, 2 * (kind == "k") + i], src, ACT.Square, bias=bias).then_inc(sq_ok, 1)
                if u >= 2:
                    act.wait_ge(split_ok, u - 1)
                if kind == "q":
                    a(scaled[:, u % 2], src, ACT.Identity, bias=BQ2[:, i:i + 1], scale=R2).then_inc(scaled_ok, 1)
                else:
                    a(scaled[:, u % 2], src, ACT.Identity, bias=bias).then_inc(scaled_ok, 1)
                act.wait_ge(scaled_ok, u + 1)
                if u >= 4:
                    act.wait_ge(stored[u % 4], 16 * (u // 4))
                a(part_of(u, 0), scaled[:, u % 2], ACT.Copy).then_inc(part1_ok, 1)

            for o in order:
                kind, b, i = o
                src = buf(o)
                if kind == "h1":
                    evacuate(o, h1_ok, h1T[:, b, :], src[:, 0:T // 2], ACT.Gelu, bias=col(C_BN1))
                elif kind == "wg":
                    evacuate(o, wg_ok, wgT[:, i, bs(b)], src, ACT.Sigmoid, bias=col(C_BG + i))
                elif kind == "mod":
                    evacuate(o, mod_ok, modT[:, i, bs(b)], src, ACT.Sigmoid, bias=col(C_BN2 + i))
                elif kind == "soma":
                    evacuate(o, soma_ok, somaT[:, i, bs(b)], src, ACT.Gelu, bias=col(C_BSOMA + i))
                elif kind == "gate":
                    act.wait_ge(temp_ok, b + 1)
                    evacuate(o, gate_ok, wgT[:, i, bs(b)], src, ACT.Sigmoid, bias=col(C_BTEMP + i))
                elif kind == "out":
                    evacuate(o, cond_ok, cond[:, b * BT + 4 * i:b * BT + 4 * i + 4, :].rearrange("p t e -> p (t e)"), src,
                             ACT.Identity)
                elif kind == "tr":
                    evacuate(o, hT_ok, hT[:, i, bs(b)], src, ACT.Identity, bias=col(C_BETA + i), scale=col(C_GAMMA + i))
                elif kind in "qk":
                    if o == ("q", 0, 0):
                        act.wait_ge(coef_ok, 1)
                    queries_or_keys(kind, b, i)
                elif kind == "n":
                    if b:
                        act.wait_ge(nsplit_ok, b)
                    evacuate(o, nrm_ok, norms, src, ACT.Identity)
                    if b:
                        act.wait_ge(nstored, 16 * 4 * b)
                    a(nparts[:, 0, :], src, ACT.Copy).then_inc(nrm_ok, 1)
            a(small[:, 15:16], small[:, 12:13], ACT.Exp)

        def read_of(o):
            kind, b, i = o
            return {"h1": (h1_ok, b + 1), "soma": (soma_ok, CT * b + i + 1), "wg": (wg_ok, CT * b + i + 1),
                    "mod": (mod_ok, D * b + i + 1), "gate": (gate_ok, CT * b + i + 1), "out": (cond_ok, 2 * b + i + 1),
                    "tr": (hT_ok, CT * b + i + 1), "q": (scaled_ok, 4 * b + i + 1), "k": (scaled_ok, 4 * b + 2 + i + 1),
                    "n": (nrm_ok, 2 * (b + 1)), "v": (val_ok, 2 * b + i + 1)}[kind]

        @block.tensor
        def _(pe):
            def start(o):
                if step[o] >= 4:
                    pe.wait_ge(*read_of(order[step[o] - 4]))

            def product(o, lhsT, rhs, ks):
                start(o)
                for half in range(2):
                    hs = slice(512 * half, 512 * half + 512)
                    for k in range(ks):
                        last = nc.tensor.matmul(buf(o)[:, hs], lhsT(k), rhs(k, half), start=(k == 0), stop=(k == ks - 1))
                last.then_inc(full, 1)

            def tok(b, half):
                return slice(b * T + 512 * half, b * T + 512 * half + 512)

            def rows_product(o, t0, lhsT, rhs):
                start(o)
                for j in range(4):
                    for k in range(CT):
                        last = nc.tensor.matmul(buf(o)[:, j * E:(j + 1) * E], lhsT(k, t0 + j), rhs(k), start=(k == 0),
                                                stop=(k == CT - 1))
                last.then_inc(full, 1)

            for o in order:
                kind, b, i = o
                if kind == "h1":
                    if b == 0:
                        pe.wait_ge(w_n, 16)
                    pe.wait_ge(w_x[b], 32)
                    start(o)
                    for k in range(CT):
                        for h in range(2):
                            last = nc.tensor.matmul(buf(o)[h * HID:(h + 1) * HID, 0:512], wn1_sb[:, k, :], xT_sb[:, k, tok(b, h)],
                                                    start=(k == 0), stop=(k == CT - 1), skip_group_check=True)
                    last.then_inc(full, 1)
                elif kind == "soma":
                    pe.wait_ge(w_s, 16)
                    product(o, lambda k: wsoma_sb[:, k, i * P:(i + 1) * P], lambda k, h: xT_sb[:, k, tok(b, h)], CT)
                elif kind == "wg":
                    pe.wait_ge(w_g, 16)
                    pe.wait_ge(ctx_ok, b + 1)
                    product(o, lambda k: wg_sb[:, k, i * P:(i + 1) * P],
                            lambda k, h: (xT_sb if k < CT else ctxT)[:, k % CT, tok(b, h)], 2 * CT)
                elif kind == "mod":
                    pe.wait_ge(rep_ok, 1)
                    pe.wait_ge(h1_ok, b + 1)
                    start(o)
                    for h in range(2):
                        rows = slice(h * HID, (h + 1) * HID)
                        last = nc.tensor.matmul(buf(o)[:, 512 * h:512 * h + 512], wn2_rep[rows, i, :], h1T[rows, b, :],
                                                start=True, stop=True)
                    last.then_inc(full, 1)
                elif kind == "gate":
                    pe.wait_ge(w_q, 64)
                    pe.wait_ge(temp_ok, b + 1)
                    product(o, lambda k: wtemp_sb[:, k, i * P:(i + 1) * P],
                            lambda k, h: traces[:, 0, k, tok(b, h)], CT)
                elif kind == "out":
                    pe.wait_ge(sg_ok, b + 1)
                    rows_product(o, b * BT + 4 * i, lambda k, t: somaT[:, k, t * P:(t + 1) * P], lambda k: wout_sb[:, k, :])
                elif kind == "tr":
                    pe.wait_ge(idt, 3)
                    pe.wait_ge(ln_ok, b + 1)
                    start(o)
                    for t in range(BT):
                        last = nc.tensor.transpose(buf(o)[:, t * P:(t + 1) * P], cond[:, b * BT + t, i * P:(i + 1) * P],
                                                   ident[:, :])
                    last.then_inc(full, 1)
                elif kind in "qk":
                    pe.wait_ge(hT_ok, CT * (b + 1))
                    c = "qk".index(kind)
                    product(o, lambda k: wqkv_sb[:, k, c * E + i * P:c * E + (i + 1) * P],
                            lambda k, h: hT[:, k, tok(b, h)], CT)
                elif kind == "n":
                    start(o)
                    pe.wait_ge(sel_ok, 1)
                    pe.wait_ge(sq_ok, 4 * (b + 1))
                    for half in range(2):
                        for w in range(4):
                            last = nc.tensor.matmul(buf(o)[32 * w:32 * w + 32, 512 * half:512 * half + 512], head_sel[:, :],
                                                    squares[:, w, 512 * half:512 * half + 512], start=True, stop=True)
                    last.then_inc(full, 1)
                else:
                    rows_product(o, b * BT + 4 * i, lambda k, t: hT[:, k, t * P:(t + 1) * P],
                                 lambda k: wqkv_sb[:, k, 2 * E:3 * E])


def place_ones(sp, g, i, qa, ka):
    for dst in (qa[96:99], ka[99:102]):
        sp.dma_start(dst, g.ones_bf[:, :].unsqueeze(1).to_broadcast([3, HG, T])).then_inc(g.ones_ok[i], 16)


def load_operands(sp, g, grp, qa, ka, loaded):
    rows = lambda d, j: d[j, bass.ds(grp * (HG * HD), HG * HD), :].rearrange("(h d) t -> d h t", d=HD)
    for r, j in enumerate((0, 1, 2, 0, 1, 0)):
        sp.dma_start(qa[r * HD:(r + 1) * HD, :, :], rows(g.q_dram, j)).then_inc(loaded, 16)
    for r, j in enumerate((0, 0, 0, 1, 1, 2)):
        sp.dma_start(ka[r * HD:(r + 1) * HD, :, :], rows(g.k_dram, j)).then_inc(loaded, 16)
    for kk, dst in ((0, qa[99:102]), (1, ka[96:99])):
        sp.dma_start(dst, g.n_dram[:, kk, bass.ds(grp * HG, HG), :]).then_inc(loaded, 16)


def load_values(sp, g, grp, vg, loaded):
    sp.dma_start(vg, g.vals[:, bass.ds(grp, 1), :, :].rearrange("p o t w -> p (o t) w")).then_inc(loaded, 16)


def store_group(sp, g, gg, i):
    sp.wait_ge(g.evac, gg * 4 + (EV0 + 2 + 2 * i))
    for h in range(HG):
        row = (i * HG + h) * HD
        sp.dma_start(g.oT[row:row + HD, bass.ds(gg, 1), :],
                     g.ost[i][32 * h:32 * h + HD, :].unsqueeze(1)).then_inc(g.ost_out[i], 16)


def block_b(nc, s, sem, sbuf, g):
    qa = [g.qa0, sbuf(s, "qa1", [KQ, HG, T], BF16)[:, :, :]]
    ka = [g.ka0, sbuf(s, "ka1", [KQ, HG, T], BF16)[:, :, :]]
    vg = [g.vg0, sbuf(s, "vg1", [P, BT, VW])]
    probs = sbuf(s, "probs", [P, 2, HG, T])
    ost = g.ost
    sc = [s.enter_context(nc.psum_tensor(f"scores{i}", [P, T], F32)) for i in range(3)]
    acc = s.enter_context(nc.psum_tensor("acc", [P, T], F32))
    STEPS = BT * HG
    LOADS = 16 * 15
    loaded, ones_ok = g.loaded, g.ones_ok
    scored, exped, pv, evac, ost_out = sem("scored"), sem("exped"), sem("pv_done"), g.evac, g.ost_out
    PIECES = 2 * BT
    PV0 = 4

    pid_sb = sbuf(s, "pid_sb", [1, B], I32)
    w_pid = sem("pid_loaded")

    def prefetch(sp):
        sp.dma_start(pid_sb[:, :], g.pid).then_inc(w_pid, 16)
        sp.wait_ge(w_pid, 16)
        for b in range(B):
            prof = sp.value_load(pid_sb[0:1, b:b + 1], min_val=0, max_val=NPROF - 1)
            one = bass.ds(prof, 1)
            sp.dma_start(g.wd[:, b, :, :], g.down_w[one, :, :].rearrange("o (k p) n -> p (o k) n", p=P)).then_inc(g.w_d, 16)
            sp.dma_start(g.bd[:, b:b + 1], g.down_b[one, :].rearrange("o n -> n o")).then_inc(g.w_d, 16)
            sp.dma_start(g.wu[:, b, :], g.up_w[one, :, :].rearrange("o k n -> (o k) n")).then_inc(g.w_d, 16)
            for j, src in enumerate((g.up_b, g.ln_g, g.ln_b)):
                sp.dma_start(g.rowp[:, b, j, :], src[one, :].broadcast_to([P, E])).then_inc(g.w_d, 16)
            for j, src in enumerate((g.ln_g, g.ln_b)):
                for k in range(CT):
                    sp.dma_start(g.colp[:, b, j, k:k + 1],
                                 src[one, k * P:(k + 1) * P].rearrange("o n -> n o")).then_inc(g.w_d, 16)
        sp.dma_start(g.wr[:, :, :], g.Wr.rearrange("(k p) n -> p k n", p=P)).then_inc(g.w_r, 16)
        sp.dma_start(g.xr[:, :, :], g.x.rearrange("(t p) e -> p t e", p=P)).then_inc(g.w_x, 16)
        for i in range(2):
            load_expert(sp, g, i, i)

    with nc.Block() as block:
        @block.gpsimd
        def _(pool):
            pool.wait_ge(g.w_x, 16)
            for c in range(CH):
                ts = slice(c * TC, (c + 1) * TC)
                nc.gpsimd.tensor_tensor(g.xr[:, ts, :], g.xr[:, ts, :], g.rows_sb[:, 1:2, :].to_broadcast([P, TC, E]),
                                        ALU.add).then_inc(g.xb_ok, 1)
            pool.wait_ge(g.w_d, 16 * 10 * B)
            for c in range(CH):
                ts = slice(c * TC, (c + 1) * TC)
                pool.wait_ge(g.xb_ok, c + 1)
                nc.gpsimd.tensor_tensor(g.xbu[:, ts, :], g.xr[:, ts, :],
                                        g.rowp[:, c * TC // BT, 0:1, :].to_broadcast([P, TC, E]), ALU.add).then_inc(g.xb_ok, 1)

        @block.sync
        def _(sp):
            def load(grp, i):
                load_operands(sp, g, grp, qa[i], ka[i], loaded[i])
                load_values(sp, g, grp, vg[i][:, :, :], loaded[i])

            place_ones(sp, g, 1, qa[1], ka[1])
            load(1, 1)
            prefetch(sp)
            sp.wait_ge(g.nstored, 16 * 4 * B)
            with sp.Fori(0, NG // 2 - 1) as gg:
                sp.wait_ge(pv, gg * (2 * PIECES) + (PV0 + PIECES))
                load(gg * 2 + 2, 0)
                store_group(sp, g, gg, 0)
                sp.wait_ge(pv, gg * (2 * PIECES) + (PV0 + 2 * PIECES))
                load(gg * 2 + 3, 1)
                store_group(sp, g, gg, 1)
            store_group(sp, g, NG // 2 - 1, 0)

        @block.vector
        def _(dve):
            v = nc.vector
            v.memset(ost[0][:, 0:1], 0.0).then_inc(ost_out[0], 64)
            v.memset(ost[1][:, 0:1], 0.0).then_inc(ost_out[1], 64)
            v.memset(ost[0][:, 1:2], 0.0).then_inc(pv, PV0)
            v.memset(ost[1][:, 1:2], 0.0).then_inc(evac, EV0)
            dve.wait_ge(evac, EV0)

            def evacuate(grp, gg, i):
                dve.wait_ge(ost_out[i], gg * 64 + 64)
                for half in range(2):
                    dve.wait_ge(pv, grp * PIECES + (PV0 + PIECES - 1 + half))
                    hs = slice(512 * half, 512 * half + 512)
                    v.tensor_copy(ost[i][:, hs], acc[:, hs]).then_inc(evac, 1)

            with dve.Fori(0, NG // 2) as gg:
                evacuate(gg * 2, gg, 0)
                evacuate(gg * 2 + 1, gg, 1)

        @block.scalar
        def _(act):
            with act.Fori(0, NG // 2) as gg:
                for i in range(2):
                    base, pieces = gg * (2 * STEPS) + i * STEPS, gg * (2 * PIECES) + i * PIECES
                    for n in range(STEPS):
                        t, h = n // HG, n % HG
                        act.wait_ge(scored, base + (n + 1))
                        if h == 0:
                            act.wait_ge(pv, pieces + (PV0 + 2 * t - 2))
                        nc.scalar.activation(probs[:, t % 2, h, :], sc[n % 3][:, :], ACT.Exp).then_inc(exped, 1)

        @block.tensor
        def _(pe):
            def scores(i, n):
                t, h = n // HG, n % HG
                for half in range(2):
                    last = nc.tensor.matmul(sc[n % 3][:, 512 * half:512 * half + 512], qa[i][:, h, t * P:(t + 1) * P],
                                            ka[i][:, h, 512 * half:512 * half + 512], start=True, stop=True)
                last.then_inc(scored, 1)

            def values(i, t, half):
                for h in range(HG):
                    last = nc.tensor.matmul(acc[32 * h:32 * h + 32, 512 * half:512 * half + 512],
                                            vg[i][:, t, HD * h:HD * h + 32], probs[:, t % 2, h, 512 * half:512 * half + 512],
                                            start=(t == 0), stop=(t == BT - 1), skip_group_check=True)
                last.then_inc(pv, 1)

            def group(grp, i, loads):
                for n in range(STEPS):
                    pe.wait_ge(exped, grp * STEPS + (n + 1))
                    if n + 3 < STEPS:
                        scores(i, n + 3)
                    elif loads is not None and n + 3 > STEPS:
                        if n + 2 == STEPS:
                            if grp is FIRST:
                                pe.wait_ge(ones_ok[1], 32)
                            pe.wait_ge(loaded[1 - i], loads * LOADS)
                        scores(1 - i, n + 2 - STEPS)
                        if n + 1 == STEPS:
                            scores(1 - i, 2)
                    if n in (HG - 1, HG + 1):
                        pe.wait_ge(evac, grp * 2 + (EV0 - 1 + (n - HG + 1) // 2))
                    if n % 2 and n >= HG - 1:
                        values(i, (n - (HG - 1)) // HG, (n - (HG - 1)) % HG // 2)
                    elif n == 1 and grp is not FIRST:
                        values(1 - i, BT - 1, 1)

            FIRST = 0
            pe.wait_ge(ones_ok[0], 32)
            pe.wait_ge(loaded[0], LOADS)
            for n in range(3):
                scores(0, n)
            group(FIRST, 0, 1)
            with pe.Fori(0, NG // 2 - 1) as gg:
                group(gg * 2 + 1, 1, gg + 2)
                group(gg * 2 + 2, 0, gg + 2)
            group(NG - 1, 1, None)
            values(1, BT - 1, 1)


def block_c(nc, s, sem, sbuf, g):
    ident = g.ident
    oT, xr, wd, bd, wu, rowp, wr = g.oT, g.xr, g.wd, g.bd, g.wu, g.rowp, g.wr
    colp, xbu = g.colp, g.xbu
    x1T = sbuf(s, "x1T", [P, 2, CT, TC * P])
    zT = sbuf(s, "zT", [P, 2, TC * P])
    y = sbuf(s, "y", [P, 2, TC, E])
    xfT = sbuf(s, "xfT", [P, 2, CT, TC * P])
    drow = sbuf(s, "drow", [P, NT, ROW])
    stats = sbuf(s, "stats_c", [P, NT, 6])
    mv = sbuf(s, "mv_c", [P, NT, 2])
    sd = sbuf(s, "sd_c", [P, 2, NT])
    variance = sbuf(s, "variance_c", [P, NT])
    root_seed = sbuf(s, "root_seed_c", [P, NT], I32)
    lg = sbuf(s, "lg", [P, NT, NE])
    mx = sbuf(s, "mx", [P, NT, 8])
    ix = sbuf(s, "ix", [P, NT, 8], U32)
    dl = sbuf(s, "dl", [P, NT, NE + 1])
    ex = sbuf(s, "ex", [P, NT, NE + 1])
    zz = sbuf(s, "zz", [P, NT, 2])
    ixf = sbuf(s, "ixf", [P, 2, NT])
    oh = sbuf(s, "oh", [P, 2, NT, NE])
    chosen = sbuf(s, "chosen", [P, NT, NE])
    off = sbuf(s, "off", [P, NT, NE])
    base = sbuf(s, "base", [P, NT + 1, NE])
    tmp = sbuf(s, "tmp", [P, 2, NT, NE])
    offk = sbuf(s, "offk", [P, 2, NT])
    over = sbuf(s, "over", [P, 2, NT])
    slotf = sbuf(s, "slotf", [P, 2, NT])
    sloti = sbuf(s, "sloti", [P, 2, NT], U32)
    iota_e = sbuf(s, "iota_e", [P, NE])
    iota_i = sbuf(s, "iota_i", [P, NE], I32)
    before = sbuf(s, "before", [P, P])
    ones = sbuf(s, "ones", [P, P])
    ps = s.enter_context(nc.psum_tensor("ps_c", [P, 4, T], F32))

    w_d, w_r = g.w_d, g.w_r
    nm_ok, yn_ok = sem("neg_mean_ok"), sem("y_normed")
    cst, dch = sem("c_constants"), sem("dve_c_chain")
    full = sem("ps_c_full")
    x1_ok, xbu_ok, t1_ok, z_ok, y_ok, rows_ok, biased, t2_ok, lg_ok, dl_ok, ex_ok, ch_ok, slot_ok, disp, outd, off_ok = (
        sem("x1_ok"), sem("x1_up_ok"), sem("x1T_ok"), sem("z_ok"), sem("y_ok"), sem("rows_gained"), sem("rows_biased"),
        sem("xfT_ok"), sem("logits_ok"), sem("shifted_ok"), sem("expd_ok"), sem("chosen_ok"), sem("slots_ok"),
        sem("dispatched"), sem("out_started"), sem("offsets_ok"))

    LAG = {"t1": 1, "y": 2, "lg": 3, "proj": 0, "z": 1, "t2": 2, "pre": 3}
    order = [(st, w - lag) for w in range(CH + 3) for st, lag in LAG.items() if 0 <= w - lag < CH]
    step = {o: i for i, o in enumerate(order)}
    buf = lambda o: ps[:, step[o] % 4]
    tl = lambda c: slice(c * TC, (c + 1) * TC)

    with nc.Block() as block:
        @block.sync
        def _(sp):
            store_group(sp, g, NG // 2 - 1, 1)
            for c in range(CH):
                sp.wait_ge(x1_ok, c + 1)
                sp.dma_start(g.out[c * TC * P:(c + 1) * TC * P, :].rearrange("(t p) e -> p t e", p=P),
                             xr[:, tl(c), :]).then_inc(outd, 16)
            sp.wait_ge(disp, 16 * 2 * NT)
            load_rows(sp, g, 0, g.xin0, g.xl[0])
            sp.wait_ge(outd, 16 * CH)

        @block.gpsimd
        def _(pool):
            p = nc.gpsimd
            p.memset(before[:, :], 1.0).then_inc(cst, 1)
            p.memset(ones[:, :], 1.0)
            p.memset(base[:, 0, :], 0.0).then_inc(cst, 1)
            p.iota(iota_i[:, :], [[1, NE]], base=0, channel_multiplier=0).then_inc(cst, 1)
            for t in range(NT):
                last = p.iota(drow[:, t, E:E + 1].bitcast(I32), [[0, 1]], base=t * P, channel_multiplier=1)
            last.then_inc(cst, 1)
            pool.wait_ge(cst, 4)
            p.tensor_copy(iota_e[:, :], iota_i[:, :]).then_inc(cst, 1)
            p.affine_select(out=before[:, :], in_=before[:, :], compare_op=ALU.is_gt, fill=0.0, base=0,
                            pattern=[[1, P]], channel_multiplier=-1).then_inc(cst, 1)
            pool.wait_ge(w_d, 16 * 10 * B)

            def rows(c):
                gain, bias = [rowp[:, c * TC // BT, j:j + 1, :].to_broadcast([P, TC, E]) for j in (1, 2)]
                pool.wait_ge(yn_ok, TC * (c + 1))
                p.tensor_tensor(drow[:, tl(c), 0:E], y[:, c % 2, :, :], gain, ALU.mult).then_inc(rows_ok, 1)
                pool.wait_ge(rows_ok, c + 1)
                p.tensor_tensor(drow[:, tl(c), 0:E], drow[:, tl(c), 0:E], bias, ALU.add).then_inc(biased, 1)

            for w in range(CH + 1):
                if w < CH:
                    rows(w)
                if w == 0:
                    continue
                c = w - 1
                pool.wait_ge(biased, c + 1)
                pool.wait_ge(slot_ok, c + 1)
                for t in range(c * TC, (c + 1) * TC):
                    for k in range(2):
                        pool.indirect_dma_start(
                            g.slots_dram, bass.IndirectOffsetOnAxis(ap=sloti[:, k, t:t + 1], axis=0),
                            drow[:, t, :], None, bounds_check=NE * CAP - 1, oob_is_err=False).then_inc(disp, 16)
            pool.wait_ge(disp, 16 * 2 * NT)

        @block.vector
        def _(dve):
            chain = [0]

            def link(ins):
                chain[0] += 1
                ins.then_inc(dch, 1)
                dve.wait_ge(dch, chain[0])

            v = nc.vector

            def x1(c):
                dve.wait_ge(full, step["proj", c] + 1)
                dve.wait_ge(g.xb_ok, 2 * CH)
                attn = buf(("proj", c)).rearrange("p (t e) -> p t e", e=E)
                v.tensor_tensor(xr[:, tl(c), :], attn, xr[:, tl(c), :], ALU.add).then_inc(x1_ok, 1)
                v.tensor_tensor(xbu[:, tl(c), :], attn, xbu[:, tl(c), :], ALU.add).then_inc(xbu_ok, 1)

            def norm(c):
                dve.wait_ge(full, step["y", c] + 1)
                dve.wait_ge(xbu_ok, c + 1)
                if c >= 2:
                    dve.wait_ge(rows_ok, c - 1)
                    dve.wait_ge(full, step["t2", c - 2] + 1)
                v.tensor_tensor(y[:, c % 2, :, :], buf(("y", c)).rearrange("p (t e) -> p t e", e=E), xbu[:, tl(c), :],
                                ALU.add).then_inc(y_ok, 1)
                dve.wait_ge(y_ok, c + 1)
                for j in range(TC):
                    last = v.bn_stats(stats[:, c * TC + j, :], y[:, c % 2, j, :])
                link(last)
                for j in range(TC):
                    last = v.bn_aggr(mv[:, c * TC + j, :], stats[:, c * TC + j, :])
                link(last)
                inverse_root(v, link, sd[:, 1, tl(c)], mv[:, tl(c), 1], variance[:, tl(c)], sd[:, 0, tl(c)], root_seed[:, tl(c)])
                v.scalar_tensor_tensor(sd[:, 0, tl(c)], mv[:, tl(c), 0], -1.0, sd[:, 1, tl(c)], ALU.mult,
                                       ALU.mult).then_inc(nm_ok, 1)
                for j in range(ACT_TILES, TC):
                    t = c * TC + j
                    v.tensor_scalar(y[:, c % 2, j, :], y[:, c % 2, j, :], mv[:, t, 0:1], sd[:, 1, t:t + 1],
                                    ALU.subtract, ALU.mult).then_inc(yn_ok, 1)

            def choose(c):
                ts = tl(c)
                dve.wait_ge(full, step["lg", c] + 1)
                v.tensor_copy(lg[:, ts, :], buf(("lg", c))[:, 0:TC * NE].rearrange("p (t e) -> p t e", e=NE)).then_inc(lg_ok, 1)
                dve.wait_ge(lg_ok, c + 1)
                for t in range(c * TC, (c + 1) * TC):
                    last = v.max(mx[:, t, :], lg[:, t, :])
                link(last)
                v.tensor_tensor(dl[:, ts, 0:NE], lg[:, ts, :], mx[:, ts, 0:1].to_broadcast([P, TC, NE]), ALU.subtract)
                v.tensor_tensor(dl[:, ts, NE:NE + 1], mx[:, ts, 1:2], mx[:, ts, 0:1], ALU.subtract).then_inc(dl_ok, 1)
                for t in range(c * TC, (c + 1) * TC):
                    last = v.max_index(ix[:, t, :], mx[:, t, :], lg[:, t, :])
                link(last)
                dve.wait_ge(cst, 6)
                link(v.tensor_copy(ixf[:, :, ts], ix[:, ts, 0:2].rearrange("p t k -> p k t")))
                for k in range(2):
                    last = v.tensor_tensor(oh[:, k, ts, :], ixf[:, k, ts].unsqueeze(2).to_broadcast([P, TC, NE]),
                                           iota_e[:, :].unsqueeze(1).to_broadcast([P, TC, NE]), ALU.is_equal)
                link(last)
                v.tensor_tensor(chosen[:, ts, :], oh[:, 0, ts, :], oh[:, 1, ts, :], ALU.add).then_inc(ch_ok, 1)
                v.tensor_copy(drow[:, ts, E + 3], ixf[:, 0, ts])
                dve.wait_ge(ex_ok, c + 1)
                link(v.tensor_reduce(zz[:, ts, 0], ex[:, ts, 0:NE], AX_X, ALU.add))
                link(v.reciprocal(zz[:, ts, 1], zz[:, ts, 0]))
                v.tensor_copy(drow[:, ts, E + 1], zz[:, ts, 1])
                link(v.tensor_tensor(drow[:, ts, E + 2], ex[:, ts, NE], zz[:, ts, 1], ALU.mult))

            def slots(c):
                ts = tl(c)
                dve.wait_ge(full, step["pre", c] + 1)
                pre = buf(("pre", c))
                for j in range(TC):
                    t = c * TC + j
                    link(v.tensor_tensor(base[:, t + 1, :], pre[:, 512 + NE * j:512 + NE * (j + 1)], base[:, t, :], ALU.add))
                v.tensor_tensor(off[:, ts, :], pre[:, 0:TC * NE].rearrange("p (t e) -> p t e", e=NE),
                                base[:, ts, :], ALU.add).then_inc(off_ok, 1)
                dve.wait_ge(off_ok, c + 1)
                for k in range(2):
                    last = v.tensor_tensor(tmp[:, k, ts, :], off[:, ts, :], oh[:, k, ts, :], ALU.mult)
                link(last)
                link(v.tensor_reduce(offk[:, :, ts], tmp[:, :, ts, :], AX_X, ALU.add))
                v.tensor_scalar(over[:, :, ts], offk[:, :, ts], float(CAP), float(OOB), ALU.is_ge, ALU.mult)
                link(v.scalar_tensor_tensor(slotf[:, :, ts], ixf[:, :, ts], float(CAP), offk[:, :, ts], ALU.mult, ALU.add))
                v.tensor_tensor(sloti[:, :, ts], slotf[:, :, ts], over[:, :, ts], ALU.add).then_inc(slot_ok, 1)

            stages = {"proj": x1, "y": norm, "lg": choose, "pre": slots}
            for st, c in order:
                if st in stages:
                    stages[st](c)
            dve.wait_ge(g.whi, 1)
            low_weights(v, g, 0, g.w1p0, g.w2p0)

        @block.scalar
        def _(act):
            a = nc.scalar.activation

            def t1(c):
                act.wait_ge(full, step["t1", c] + 1)
                if c >= 2:
                    act.wait_ge(full, step["z", c - 2] + 1)
                a(x1T[:, c % 2, :, :].rearrange("p k t -> p (k t)"), buf(("t1", c)), ACT.Copy).then_inc(t1_ok, 1)

            def z(c):
                b = c * TC // BT
                act.wait_ge(full, step["z", c] + 1)
                if c >= 2:
                    act.wait_ge(full, step["y", c - 2] + 1)
                act.wait_ge(w_d, 16 * 10 * B)
                a(zT[:, c % 2, :], buf(("z", c))[:, 0:TC * P], ACT.Relu, bias=bd[:, b:b + 1]).then_inc(z_ok, 1)

            def normed(c):
                act.wait_ge(nm_ok, c + 1)
                for j in range(ACT_TILES):
                    t = c * TC + j
                    a(y[:, c % 2, j, :], y[:, c % 2, j, :], ACT.Identity, bias=sd[:, 0, t:t + 1],
                      scale=sd[:, 1, t:t + 1]).then_inc(yn_ok, 1)

            def t2(c):
                act.wait_ge(full, step["t2", c] + 1)
                if c >= 2:
                    act.wait_ge(full, step["lg", c - 2] + 1)
                b, half = c * TC // BT, TC * P
                for k in range(CT):
                    a(xfT[:, c % 2, k, :], buf(("t2", c))[:, k * half:(k + 1) * half], ACT.Identity,
                      bias=colp[:, b, 1, k:k + 1], scale=colp[:, b, 0, k:k + 1]).then_inc(t2_ok, 1)

            def soft(c):
                act.wait_ge(dl_ok, c + 1)
                a(ex[:, tl(c), :], dl[:, tl(c), :], ACT.Exp).then_inc(ex_ok, 1)

            act.wait_ge(g.wl[0], 32)
            a(g.w1p0[:, 0, :, :], g.raw1[0][:, :, :], ACT.Copy)
            a(g.w2p0[:, 0, :, :], g.raw2[0][:, :, :], ACT.Copy).then_inc(g.whi, 1)
            stages = {"t1": t1, "z": z, "y": normed, "t2": t2, "lg": soft}
            for st, c in order:
                if st in stages:
                    stages[st](c)

        read_of = {"proj": xbu_ok, "t1": t1_ok, "z": z_ok, "y": y_ok, "t2": t2_ok, "lg": lg_ok, "pre": off_ok}
        reads = {"t2": CT}

        @block.tensor
        def _(pe):
            def start(o):
                if step[o] >= 4:
                    st, c = order[step[o] - 4]
                    pe.wait_ge(read_of[st], (c + 1) * reads.get(st, 1))

            def transposed(c, src):
                for k in range(CT):
                    for j in range(TC):
                        last = nc.tensor.transpose(buf_of[:, (k * TC + j) * P:(k * TC + j + 1) * P], src(j, k), ident[:, :])
                last.then_inc(full, 1)

            pe.wait_ge(w_d, 16 * 10 * B)
            pe.wait_ge(w_r, 16)
            for o in order:
                st, c = o
                start(o)
                buf_of = buf(o)
                b = c * TC // BT
                if st == "proj":
                    if c in (0, CH // 2):
                        for i in range(2):
                            pe.wait_ge(g.ost_out[i], 64 + 64 * CT * (b + 1))
                    for j in range(TC):
                        t = c * TC + j
                        for k in range(CT):
                            last = nc.tensor.matmul(buf_of[:, j * E:(j + 1) * E], oT[:, b * CT + k, t % BT * P:(t % BT + 1) * P],
                                                    g.wproj_sb[:, k, :], start=(k == 0), stop=(k == CT - 1))
                    last.then_inc(full, 1)
                elif st == "t1":
                    pe.wait_ge(x1_ok, c + 1)
                    transposed(c, lambda j, k: xr[:, c * TC + j, k * P:(k + 1) * P])
                elif st == "z":
                    pe.wait_ge(t1_ok, c + 1)
                    for k in range(CT):
                        last = nc.tensor.matmul(buf_of[:, 0:TC * P], wd[:, b, k, :], x1T[:, c % 2, k, :], start=(k == 0),
                                                stop=(k == CT - 1))
                    last.then_inc(full, 1)
                elif st == "y":
                    pe.wait_ge(z_ok, c + 1)
                    for j in range(TC):
                        last = nc.tensor.matmul(buf_of[:, j * E:(j + 1) * E], zT[:, c % 2, j * P:(j + 1) * P], wu[:, b, :],
                                                start=True, stop=True)
                    last.then_inc(full, 1)
                elif st == "t2":
                    pe.wait_ge(yn_ok, TC * (c + 1))
                    transposed(c, lambda j, k: y[:, c % 2, j, k * P:(k + 1) * P])
                elif st == "lg":
                    pe.wait_ge(t2_ok, CT * (c + 1))
                    for j in range(TC):
                        for k in range(CT):
                            last = nc.tensor.matmul(buf_of[:, j * NE:(j + 1) * NE], xfT[:, c % 2, k, j * P:(j + 1) * P],
                                                    wr[:, k, :], start=(k == 0), stop=(k == CT - 1))
                    last.then_inc(full, 1)
                else:
                    pe.wait_ge(cst, 6)
                    pe.wait_ge(ch_ok, c + 1)
                    ch = chosen[:, tl(c), :].rearrange("p t e -> p (t e)")
                    nc.tensor.matmul(buf_of[:, 0:TC * NE], before[:, :], ch, start=True, stop=True)
                    nc.tensor.matmul(buf_of[:, 512:512 + TC * NE], ones[:, :], ch, start=True, stop=True).then_inc(full, 1)


def load_expert(sp, g, e, i):
    one = bass.ds(e, 1)
    sp.dma_start(g.raw1[i][:, :, :], g.w1[one, :, :].rearrange("o (k p) f -> p (o k) f", p=P)).then_inc(g.wl[i], 16)
    sp.dma_start(g.raw2[i][:, :, :], g.w2[one, :, :].rearrange("o (k p) n -> p (o k) n", p=P)).then_inc(g.wl[i], 16)


def low_weights(v, g, i, w1p, w2p):
    v.tensor_tensor(w1p[:, 1, :, :], g.raw1[i][:, :, :], w1p[:, 0, :, :].bitcast(F32), ALU.subtract)
    v.tensor_tensor(w2p[:, 1, :, :], g.raw2[i][:, :, :], w2p[:, 0, :, :].bitcast(F32), ALU.subtract).then_inc(g.wlo, 1)


def load_rows(sp, g, e, xin, loaded):
    sp.dma_start(xin[:, :, :], g.slots_dram[bass.ds(e * CAP, CAP), :].rearrange("(t p) r -> p t r", p=P)).then_inc(loaded, 16)


def block_d(nc, s, sem, sbuf, g):
    raw1, raw2 = g.raw1, g.raw2
    w1p = [g.w1p0[:, :, :, :], sbuf(s, "w1p1", [P, 2, CT, FF], F32R)[:, :, :, :]]
    w2p = [g.w2p0[:, :, :, :], sbuf(s, "w2p1", [P, 2, FT, E], F32R)[:, :, :, :]]
    xin = [g.xin0, sbuf(s, "xin1", [P, ST, ROW])]
    xp = [sbuf(s, f"xp{i}", [P, 2, CT * CAP], F32R) for i in range(2)]
    stage = sbuf(s, "stage", [P, 4, CAP])
    hp = sbuf(s, "hp", [P, 2, FT, CAP], F32R)
    ye = [sbuf(s, f"ye{i}", [P, ST, E]) for i in range(2)]
    wsel = [sbuf(s, f"wsel{i}", [P, 4, ST]) for i in range(2)]
    tok = [sbuf(s, f"tok{i}", [P, ST], U32) for i in range(2)]
    expert = sbuf(s, "expert", [P, 2])
    start_sb = sbuf(s, "start_sb", [P, 4 + NE])
    ps_t = s.enter_context(nc.psum_tensor("ps_t", [P, CT * CAP], F32))
    ps_h = s.enter_context(nc.psum_tensor("ps_h", [P, 4, CAP], F32))
    ps_y = s.enter_context(nc.psum_tensor("ps_y", [P, ST * E], F32))
    xl, wl = g.xl, g.wl
    tr, hid, yp, yc, sel = sem("x_transposed"), sem("hidden_ready"), sem("y_ready"), sem("y_weighted"), sem("weights_selected")
    biased, added, sums, dch = sem("bias_added"), sem("rows_added"), sem("expert_summed"), sem("dve_d_chain")
    gel, hhi, hlo = sem("gelu_done"), sem("hidden_high"), sem("hidden_low")
    whi, wlo, xhi, xlo = g.whi, g.wlo, sem("x_high"), sem("x_low")
    YP0, YC0, HL0, SUM0 = 4, 2, 4, 2
    K = 5

    def experts(engine, body):
        with engine.Fori(0, NE // 2 - 1) as pair:
            for i in range(2):
                body(pair * 2 + i, i, pair, True)
        for i in range(2):
            body(NE - 2 + i, i, NE // 2 - 1, i == 0)

    with nc.Block() as block:
        @block.sync
        def _(sp):
            load_rows(sp, g, 1, xin[1], xl[1])
            with sp.Fori(0, NE // 2 - 1) as pair:
                for i in range(2):
                    e = pair * 2 + i
                    sp.wait_ge(xlo, e + 1)
                    sp.wait_ge(sel, e + 1)
                    load_rows(sp, g, e + 2, xin[i], xl[i])
                    sp.wait_ge(wlo, e + 1)
                    load_expert(sp, g, e + 2, i)

        @block.gpsimd
        def _(pool):
            nc.gpsimd.memset(start_sb[:, 0:1], 0.0).then_inc(yp, YP0)
            nc.gpsimd.memset(start_sb[:, 1:2], 0.0).then_inc(hlo, HL0)
            nc.gpsimd.memset(start_sb[:, 2:3], 0.0).then_inc(sums, SUM0)
            pool.wait_ge(sums, SUM0)
            pool.dma_start(g.out[0:N, :].rearrange("(t p) e -> p t e", p=P), g.rows_sb[:, 2:3, :].to_broadcast([P, NT, E]),
                           accum_op=ALU.add).then_inc(biased, 16)
            pool.wait_ge(biased, 16)
            nc.gpsimd.memset(start_sb[:, 3:4], 0.0).then_inc(yc, YC0)

            for e in range(NE):
                i = e % 2
                for t in range(ST):
                    pool.wait_ge(yc, 2 * e + (t if e == NE - 1 else t // 2) + YC0 + 1)
                    pool.indirect_dma_start(g.out, bass.IndirectOffsetOnAxis(ap=tok[i][:, t:t + 1], axis=0),
                                            ye[i][:, t, :], None, bounds_check=NROWS - 1, oob_is_err=True,
                                            compute_op=ALU.add).then_inc(added, 16)
                    pool.wait_ge(added, 16 * (ST * e + t + 1))
                nc.gpsimd.memset(start_sb[:, 4 + e:5 + e], 0.0).then_inc(sums, 1)


        @block.vector
        def _(dve):
            v = nc.vector

            def low(e, i, xturn, wturn):
                links = [0]

                def link(ins):
                    links[0] += 1
                    ins.then_inc(dch, 1)
                    dve.wait_ge(dch, e * K + (1 + links[0]))

                if wturn is not None:
                    dve.wait_ge(whi, e + 1)
                    low_weights(v, g, i, w1p[i], w2p[i])
                dve.wait_ge(xhi, e + 1)
                v.tensor_tensor(xp[i][:, 1, :], ps_t[:, :], xp[i][:, 0, :].bitcast(F32), ALU.subtract).then_inc(xlo, 1)
                dve.wait_ge(xl[i], xturn)
                dve.wait_ge(sums, e + (SUM0 - 1))
                v.tensor_copy(tok[i][:, :], xin[i][:, :, E].bitcast(U32))
                link(v.tensor_scalar(wsel[i][:, 0, :], xin[i][:, :, E + 3], expert[:, 0:1], None, ALU.is_equal))
                v.tensor_scalar(expert[:, 0:1], expert[:, 0:1], 1.0, None, ALU.add)
                link(v.tensor_tensor(wsel[i][:, 1, :], wsel[i][:, 0, :], xin[i][:, :, E + 1], ALU.mult))
                link(v.tensor_scalar(wsel[i][:, 2, :], wsel[i][:, 0, :], -1.0, 1.0, ALU.mult, ALU.add))
                link(v.tensor_tensor(wsel[i][:, 2, :], wsel[i][:, 2, :], xin[i][:, :, E + 2], ALU.mult))
                link(v.tensor_tensor(wsel[i][:, 3, :], wsel[i][:, 1, :], wsel[i][:, 2, :], ALU.add))
                assert links[0] == K
                v.tensor_copy(wsel[i][:, 0, :], wsel[i][:, 3, :]).then_inc(sel, 1)

            def one(e, i, pair, more):
                for f in range(FT):
                    dve.wait_ge(hhi, e * FT + (f + 1))
                    v.tensor_tensor(hp[:, 1, f, :], stage[:, f % 4, :], hp[:, 0, f, :].bitcast(F32),
                                    ALU.subtract).then_inc(hlo, 1)
                if more:
                    n = (pair + (1 if i else 0)) * 16 + 16
                    low(e + 1, 1 - i, n, n)
                dve.wait_ge(sel, e + 1)
                if not more:
                    for t in range(ST):
                        dve.wait_ge(yp, e * 2 + (YP0 + 1 + t))
                        v.tensor_scalar(ye[i][:, t, :], ps_h[:, t, 0:E], wsel[i][:, 0, t:t + 1], None, ALU.mult).then_inc(yc, 1)
                    return
                for h in range(2):
                    dve.wait_ge(yp, e * 2 + (YP0 + 1 + h))
                    for t in (2 * h, 2 * h + 1):
                        last = v.tensor_scalar(ye[i][:, t, :], ps_y[:, t * E:(t + 1) * E], wsel[i][:, 0, t:t + 1], None, ALU.mult)
                    last.then_inc(yc, 1)

            v.memset(expert[:, 0:1], 0.0).then_inc(dch, 1)
            dve.wait_ge(dch, 1)
            low(0, 0, 16, None)
            experts(dve, one)

        @block.scalar
        def _(act):
            a = nc.scalar.activation

            def high(e, i, wturn):
                if wturn is not None:
                    act.wait_ge(yp, e * 2 + (YP0 - 2))
                    act.wait_ge(wl[i], wturn)
                    a(w1p[i][:, 0, :, :], raw1[i][:, :, :], ACT.Copy)
                    a(w2p[i][:, 0, :, :], raw2[i][:, :, :], ACT.Copy).then_inc(whi, 1)
                act.wait_ge(tr, e + 1)
                a(xp[i][:, 0, :], ps_t[:, :], ACT.Copy).then_inc(xhi, 1)

            def one(e, i, pair, more):
                for f in range(FT):
                    act.wait_ge(hid, e * FT + (f + 1))
                    act.wait_ge(hlo, e * FT + (f + 1 + HL0 - 4))
                    a(stage[:, f % 4, :], ps_h[:, f % 4, :], ACT.Gelu_apprx_tanh).then_inc(gel, 1)
                    act.wait_ge(gel, e * FT + (f + 1))
                    a(hp[:, 0, f, :], stage[:, f % 4, :], ACT.Copy).then_inc(hhi, 1)
                if more:
                    high(e + 1, 1 - i, (pair + (1 if i else 0)) * 32 + 32)

            high(0, 0, None)
            experts(act, one)

        @block.tensor
        def _(pe):
            terms = ((0, 0), (0, 1), (1, 0))

            def turn(e, i, xturn):
                pe.wait_ge(xl[i], xturn)
                for k in range(CT):
                    for t in range(ST):
                        last = nc.tensor.transpose(ps_t[:, k * CAP + t * P:k * CAP + (t + 1) * P],
                                                   xin[i][:, t, k * P:(k + 1) * P], g.ident[:, :])
                last.then_inc(tr, 1)

            def one(e, i, pair, more):
                pe.wait_ge(xlo, e + 1)
                pe.wait_ge(wlo, e + 1)
                for f in range(FT):
                    if f < 4:
                        pe.wait_ge(hlo, e * FT + (f + 1 + HL0 - 4))
                    else:
                        pe.wait_ge(gel, e * FT + (f - 3))
                    n = 0
                    for k in range(CT):
                        for u, w in terms:
                            last = nc.tensor.matmul(ps_h[:, f % 4, :], w1p[i][:, u, k, f * P:(f + 1) * P],
                                                    xp[i][:, w, k * CAP:(k + 1) * CAP], start=(n == 0), stop=(n == 3 * CT - 1))
                            n += 1
                    last.then_inc(hid, 1)
                if more:
                    turn(e + 1, 1 - i, (pair + (1 if i else 0)) * 16 + 16)
                for t in range(ST):
                    if not more:
                        dst = ps_h[:, t, 0:E]
                        pe.wait_ge(gel, e * FT + (FT - 3 + t))
                    else:
                        dst = ps_y[:, t * E:(t + 1) * E]
                        if t % 2 == 0:
                            pe.wait_ge(yc, e * 2 + (YC0 - 1 + t // 2))
                    n = 0
                    for f in range(FT):
                        if t == 0:
                            pe.wait_ge(hlo, e * FT + (f + 1 + HL0))
                        for u, w in terms:
                            last = nc.tensor.matmul(dst, hp[:, u, f, t * P:(t + 1) * P],
                                                    w2p[i][:, w, f, :], start=(n == 0), stop=(n == 3 * FT - 1))
                            n += 1
                    if t % 2 or not more:
                        last.then_inc(yp, 1)

            turn(0, 0, 16)
            experts(pe, one)


def kernel(**inputs):
    import numpy as np
    import concourse.bacc as bacc
    from concourse.bass_utils import run_bass_kernel_spmd

    a = {k: np.asarray(v) for k, v in inputs.items()}
    f = lambda n: a["L0_" + n]
    tile = lambda v: v.reshape(-1, P).T
    every = lambda v: np.broadcast_to(v.reshape(1, -1), (P, v.size))
    bqkv = f("attn_bqkv")
    cols = np.concatenate([
        tile(f("cond_bg")), tile(f("cond_bsoma")), tile(f("cond_btemp")), tile(f("cond_gamma")), tile(f("cond_beta")),
        tile(bqkv[0:E]), tile(bqkv[E:2 * E]), tile(a["cond_1024"].reshape(-1)),
        np.tile(f("cond_bn1"), P // HID).reshape(P, 1), every(f("cond_tau_ctx")), every(a["condB_tauraws"]),
        every(a["condB_bn2"]), every(f("attn_r_sigma"))], axis=1)
    rows = np.stack([bqkv[2 * E:], f("attn_bproj"), f("ffn_bias").reshape(-1)])
    x = a["x"].reshape(N, E)
    arrays = {
        "x": x, "xT": x.T, "cols": cols, "rows": rows, "pid": a["itok_B_0_6"].reshape(1, B),
        "WgT": f("cond_Wg").T, "Wn1T": f("cond_Wn1").T, "Wn2T": a["cond_256"].T, "WsomaT": f("cond_Wsoma").T,
        "WtempT": f("cond_Wtemp").T, "WoutT": f("cond_Wout").T, "Wqkv": f("attn_Wqkv"), "Wproj": f("attn_Wproj"),
        "down_w": f("cond2_down_w"), "down_b": f("cond2_down_b"), "up_w": f("cond2_up_w"), "up_b": f("cond2_up_b"),
        "ln_g": f("cond2_ln_g"), "ln_b": f("cond2_ln_b"), "Wr": f("ffn_w_router"), "w1": f("ffn_w1"), "w2": f("ffn_w2")}
    arrays = {k: np.ascontiguousarray(v) for k, v in arrays.items()}
    nc = bacc.Bacc("TRN2", target_bir_lowering=False, num_devices=1)
    aps = {k: nc.dram_tensor(f"in_{k}", v.shape, mybir.dt.from_np(v.dtype), kind="ExternalInput").ap() for k, v in arrays.items()}
    out = nc.dram_tensor("out_rows", (NROWS, E), F32, kind="ExternalOutput").ap()
    aps["out"] = out
    build(nc, aps)
    r = run_bass_kernel_spmd(nc, [{f"in_{k}": v for k, v in arrays.items()}], core_ids=[0])
    return r.results[0]["out_rows"][:N].reshape(B, T, E)
```
